# Optimizing a Trainium2 kernel written in Bass

```python
import numpy as np
import jax
import jax.numpy as jnp

def _softmax(x, axis=-1):
    return jax.nn.softmax(x, axis=axis)

def _gelu(x):
    return jax.nn.gelu(x, approximate=True)

def _silu(x):
    return jax.nn.silu(x)

def _sigmoid(x):
    return jax.nn.sigmoid(x)

def _layernorm(x, axis=-1, eps=1e-05):
    m = jnp.mean(x, axis=axis, keepdims=True)
    v = jnp.var(x, axis=axis, keepdims=True)
    return (x - m) / jnp.sqrt(v + eps)

def _scatter_add(tgt, idx, src, axis=0):
    return tgt.at[idx].add(src)

def _segment_sum(src, seg, n):
    return jax.ops.segment_sum(src, seg, n)
kernel_name = 'mk_xattn_seq_d4_seqx_r8_f8d659'

def setup_inputs(seed: int=0):
    np.random.seed(seed)
    _w = jnp.asarray

    def _rec_inputs():
        import jax
        import jax.numpy as jnp
        _rk = jax.random.key(seed)
        x = 7.22e-05 + 1 * jax.random.normal(jax.random.fold_in(_rk, 1), (64, 64, 256), jnp.float32)
        _lenS = 64 - jax.random.randint(jax.random.fold_in(_rk, 7), (64,), 0, max(1, 64 // 4) + 1, jnp.int32)
        _lenS2 = 64 - jax.random.randint(jax.random.fold_in(_rk, 8), (64,), 0, max(1, 64 // 4) + 1, jnp.int32)
        _ctx_2048P = jax.random.normal(jax.random.fold_in(_rk, 11), (64, 16, 256), jnp.float32)
        _ctx_2048c = jax.random.dirichlet(jax.random.fold_in(_rk, 511), 0.3 * jnp.ones((16,), jnp.float32), (64, 64))
        _ctx_2048t = jnp.einsum('bsk,bkd->bsd', _ctx_2048c, _ctx_2048P)
        _ctx_2048t = _ctx_2048t * jax.lax.rsqrt(jnp.mean(jnp.square(_ctx_2048t)) + 1e-12) * 0.953939
        ctx_2048 = 2.81802e-05 + 1.00001 * (_ctx_2048t + 0.3 * jax.random.normal(jax.random.fold_in(_rk, 611), (64, 64, 256), jnp.float32))
        _validS = jnp.arange(64)[None, :] < _lenS[:, None]
        _validS2 = jnp.arange(64)[None, :] < _lenS2[:, None]
        _causal = jnp.tril(jnp.ones((64, 64), dtype=bool))
        mask_BxS2_bf1 = jnp.ones((64, 64), dtype=bool)
        mask_Bx1xSxS2_ff0 = jnp.where(jnp.ones((64, 1, 64, 64), dtype=bool), 0.0, -1000000000.0).astype(jnp.float32)
        return (x, ctx_2048, mask_BxS2_bf1, mask_Bx1xSxS2_ff0)
    x, ctx_2048, mask_BxS2_bf1, mask_Bx1xSxS2_ff0 = _rec_inputs()

    def _L0_xattn_setup():
        import jax, jax.numpy as jnp
        import numpy as np
        D = 256
        H = 16
        HD = D // H
        INNER = 4 * D
        EPS = 1e-05

        def layer_norm(x, w, b):
            mu = jnp.mean(x, axis=-1, keepdims=True)
            var = jnp.mean(jnp.square(x - mu), axis=-1, keepdims=True)
            return (x - mu) * jax.lax.rsqrt(var + EPS) * w + b
        key = jax.random.key(seed)
        ks = jax.random.split(key, 12)
        B, LQ, LK = (4, 128, 256)
        std = 0.02
        inp = {'hidden_states': jax.random.normal(ks[0], (B, LQ, D), jnp.float32), 'encoder_hidden_states': jax.random.normal(ks[1], (B, LK, D), jnp.float32), 'encoder_attention_mask': jnp.ones((B, LK), dtype=bool), 'ln1_w': jnp.ones((D,), jnp.float32), 'ln1_b': jnp.zeros((D,), jnp.float32), 'q_w': jax.random.normal(ks[2], (D, D), jnp.float32) * std, 'q_b': jnp.zeros((D,), jnp.float32), 'k_w': jax.random.normal(ks[3], (D, D), jnp.float32) * std, 'k_b': jnp.zeros((D,), jnp.float32), 'v_w': jax.random.normal(ks[4], (D, D), jnp.float32) * std, 'v_b': jnp.zeros((D,), jnp.float32), 'cproj_w': jax.random.normal(ks[5], (D, D), jnp.float32) * std, 'cproj_b': jnp.zeros((D,), jnp.float32), 'ln2_w': jnp.ones((D,), jnp.float32), 'ln2_b': jnp.zeros((D,), jnp.float32), 'fc_w': jax.random.normal(ks[6], (D, INNER), jnp.float32) * std, 'fc_b': jnp.zeros((INNER,), jnp.float32), 'proj_w': jax.random.normal(ks[7], (INNER, D), jnp.float32) * std, 'proj_b': jnp.zeros((D,), jnp.float32)}
        return inp
    _L0_xattn_all = _L0_xattn_setup()
    _L0_xattn_in = {k: v for k, v in _L0_xattn_all.items() if k in ('ln1_w', 'ln1_b', 'q_w', 'q_b', 'k_w', 'k_b', 'v_w', 'v_b', 'cproj_w', 'cproj_b', 'ln2_w', 'ln2_b', 'fc_w', 'fc_b', 'proj_w', 'proj_b')}
    del _L0_xattn_all

    def _L1_xattn_setup():
        import jax, jax.numpy as jnp
        import numpy as np
        E, H, L, B = (256, 32, 128, 4)
        S = E // H
        DM, DD = (32, 64)

        def _ln(x, w, b, eps=1e-05):
            m = x.mean(-1, keepdims=True)
            v = ((x - m) ** 2).mean(-1, keepdims=True)
            return (x - m) / jnp.sqrt(v + eps) * w + b

        def _block(x, state, ln1_w, ln1_b, ln2_w, ln2_b, maa_x, maa_w1, maa_w2, maa_stack, time_decay, td_w1, td_w2, u, Wr, Wk, Wv, Wg, Wo, gn_w, gn_b, ffn_maa_k, ffn_maa_r, Wfk, Wfr, Wfv):
            b, l, e = x.shape
            h = u.shape[0]
            s_ = e // h
            xa = _ln(x, ln1_w, ln1_b)
            sx = jnp.concatenate([state[:, 1:2] - xa[:, :1], xa[:, :-1] - xa[:, 1:]], axis=1)
            xxx = jnp.tanh((xa + sx * maa_x) @ maa_w1).reshape(b, l, 5, DM)
            xxx = jnp.einsum('blfd,fde->blfe', xxx, maa_w2)
            xm = xa[:, :, None] + sx[:, :, None] * (maa_stack + xxx)
            xk, xw, xv, xr, xg = (xm[:, :, j] for j in range(5))
            w = jnp.exp(-jnp.exp(time_decay + jnp.tanh(xw @ td_w1) @ td_w2)).reshape(b, l, h, s_)
            r = (xr @ Wr.T).reshape(b, l, h, s_)
            k = (xk @ Wk.T).reshape(b, l, h, s_)
            v = (xv @ Wv.T).reshape(b, l, h, s_)
            g = jax.nn.silu(xg @ Wg.T)
            s0 = state[:, 2:2 + s_].reshape(b, h, s_, s_)

            def step(s, rkvw):
                r_t, k_t, v_t, w_t = rkvw
                a = k_t[..., :, None] * v_t[..., None, :]
                out = jnp.einsum('bhi,bhij->bhj', r_t, u * a + s)
                s = a + w_t[..., :, None] * s
                return (s, out)
            rkvw = tuple((jnp.moveaxis(t, 1, 0) for t in (r, k, v, w)))
            _, out = jax.lax.scan(step, s0, rkvw)
            out = jnp.moveaxis(out, 0, 1).reshape(b, l, e)
            og = out.reshape(b, l, h, s_)
            m = og.mean(-1, keepdims=True)
            va = ((og - m) ** 2).mean(-1, keepdims=True)
            og = ((og - m) / jnp.sqrt(va + 1e-05)).reshape(b, l, e) * gn_w + gn_b
            x1 = x + og * g @ Wo.T
            xc = _ln(x1, ln2_w, ln2_b)
            sx2 = jnp.concatenate([state[:, 0:1] - xc[:, :1], xc[:, :-1] - xc[:, 1:]], axis=1)
            xk2 = xc + sx2 * ffn_maa_k
            xr2 = xc + sx2 * ffn_maa_r
            rr = jax.nn.sigmoid(xr2 @ Wfr.T)
            kk = jnp.square(jax.nn.relu(xk2 @ Wfk.T))
            return x1 + rr * (kk @ Wfv.T)
        key = jax.random.key(seed)
        ks = jax.random.split(key, 24)
        sc = 0.02
        d = {'x': jax.random.normal(ks[0], (B, L, E), jnp.float32), 'state': jax.random.normal(ks[1], (B, 2 + S, E), jnp.float32) * 0.1, 'ln1_w': jnp.ones((E,), jnp.float32), 'ln1_b': jnp.zeros((E,), jnp.float32), 'ln2_w': jnp.ones((E,), jnp.float32), 'ln2_b': jnp.zeros((E,), jnp.float32), 'maa_x': jax.random.normal(ks[2], (E,), jnp.float32) * 0.1, 'maa_w1': jax.random.normal(ks[3], (E, 5 * DM), jnp.float32) * sc, 'maa_w2': jax.random.normal(ks[4], (5, DM, E), jnp.float32) * sc, 'maa_stack': jax.random.normal(ks[5], (1, 5, E), jnp.float32) * 0.1, 'time_decay': jax.random.normal(ks[6], (E,), jnp.float32) * 0.5, 'td_w1': jax.random.normal(ks[7], (E, DD), jnp.float32) * sc, 'td_w2': jax.random.normal(ks[8], (DD, E), jnp.float32) * sc, 'u': jax.random.normal(ks[9], (H, S, 1), jnp.float32) * 0.1, 'Wr': jax.random.normal(ks[10], (E, E), jnp.float32) * sc, 'Wk': jax.random.normal(ks[11], (E, E), jnp.float32) * sc, 'Wv': jax.random.normal(ks[12], (E, E), jnp.float32) * sc, 'Wg': jax.random.normal(ks[13], (E, E), jnp.float32) * sc, 'Wo': jax.random.normal(ks[14], (E, E), jnp.float32) * sc, 'gn_w': jnp.ones((E,), jnp.float32), 'gn_b': jnp.zeros((E,), jnp.float32), 'ffn_maa_k': jax.random.normal(ks[15], (E,), jnp.float32) * 0.1, 'ffn_maa_r': jax.random.normal(ks[16], (E,), jnp.float32) * 0.1, 'Wfk': jax.random.normal(ks[17], (E, E), jnp.float32) * sc, 'Wfr': jax.random.normal(ks[18], (E, E), jnp.float32) * sc, 'Wfv': jax.random.normal(ks[19], (E, E), jnp.float32) * sc}
        return d
    _L1_xattn_all = _L1_xattn_setup()
    _L1_xattn_in = {k: v for k, v in _L1_xattn_all.items() if k in ('ln1_w', 'ln1_b', 'ln2_w', 'ln2_b', 'maa_x', 'maa_w1', 'maa_w2', 'maa_stack', 'time_decay', 'td_w1', 'td_w2', 'u', 'Wr', 'Wk', 'Wv', 'Wg', 'Wo', 'gn_w', 'gn_b', 'ffn_maa_k', 'ffn_maa_r', 'Wfk', 'Wfr', 'Wfv')}
    del _L1_xattn_all

    def _L2_xattn_setup():
        import jax, jax.numpy as jnp
        import numpy as np
        B, Q, S1, S2 = (4, 32, 256, 256)
        D, H, K, F = (256, 16, 128, 1024)
        LN_EPS = 1e-05

        def _layer_norm(x, scale, offset):
            mu = jnp.mean(x, axis=-1, keepdims=True)
            var = jnp.var(x, axis=-1, keepdims=True)
            return (x - mu) * jax.lax.rsqrt(var + LN_EPS) * scale + offset

        def _cross_attention(q_in, kv_in, wq, bq, wk, bk, wv, bv, wo, bo, bias_k, bias_v):
            b, q_len, _ = q_in.shape
            t = kv_in.shape[1]
            qh = (q_in @ wq + bq).reshape(b, q_len, H, K)
            kh = (kv_in @ wk + bk).reshape(b, t, H, K)
            vh = (kv_in @ wv + bv).reshape(b, t, H, K)
            kh = jnp.concatenate([kh, jnp.broadcast_to(bias_k, (b, 1, H, K))], axis=1)
            vh = jnp.concatenate([vh, jnp.broadcast_to(bias_v, (b, 1, H, K))], axis=1)
            scale = jnp.sqrt(jnp.asarray(K, q_in.dtype))
            logits = jnp.einsum('bqhk,bthk->bhqt', qh, kh) / scale
            weights = jax.nn.softmax(logits, axis=-1)
            ctx = jnp.einsum('bhqt,bthk->bqhk', weights, vh).reshape(b, q_len, H * K)
            return ctx @ wo + bo

        def _forward(x, xf_1, xf_2, ln1_scale, ln1_offset, wq1, bq1, wk1, bk1, wv1, bv1, wo1, bo1, bias_k1, bias_v1, ln2_scale, ln2_offset, wq2, bq2, wk2, bk2, wv2, bv2, wo2, bo2, bias_k2, bias_v2, ln_mlp_scale, ln_mlp_offset, w_fc1, b_fc1, w_fc2, b_fc2):
            res = x
            h = _layer_norm(x, ln1_scale, ln1_offset)
            x = res + _cross_attention(h, xf_1, wq1, bq1, wk1, bk1, wv1, bv1, wo1, bo1, bias_k1, bias_v1)
            res = x
            h = _layer_norm(x, ln2_scale, ln2_offset)
            x = res + _cross_attention(h, xf_2, wq2, bq2, wk2, bk2, wv2, bv2, wo2, bo2, bias_k2, bias_v2)
            h = _layer_norm(x, ln_mlp_scale, ln_mlp_offset)
            h = jax.nn.gelu(h @ w_fc1 + b_fc1, approximate=False) @ w_fc2 + b_fc2
            return x + h
        key = jax.random.key(seed)
        ks = iter(jax.random.split(key, 64))

        def rn(shape, s=0.02):
            return jax.random.normal(next(ks), shape, jnp.float32) * s
        inp = {'x': rn((B, Q, D), 1.0), 'xf_1': rn((B, S1, D), 1.0), 'xf_2': rn((B, S2, D), 1.0)}
        for i in (1, 2):
            inp[f'ln{i}_scale'] = jnp.ones((D,), jnp.float32)
            inp[f'ln{i}_offset'] = jnp.zeros((D,), jnp.float32)
            inp[f'wq{i}'] = rn((D, H * K))
            inp[f'bq{i}'] = jnp.zeros((H * K,), jnp.float32)
            inp[f'wk{i}'] = rn((D, H * K))
            inp[f'bk{i}'] = jnp.zeros((H * K,), jnp.float32)
            inp[f'wv{i}'] = rn((D, H * K))
            inp[f'bv{i}'] = jnp.zeros((H * K,), jnp.float32)
            inp[f'wo{i}'] = rn((H * K, D))
            inp[f'bo{i}'] = jnp.zeros((D,), jnp.float32)
            inp[f'bias_k{i}'] = rn((1, 1, H, K))
            inp[f'bias_v{i}'] = rn((1, 1, H, K))
        inp['ln_mlp_scale'] = jnp.ones((D,), jnp.float32)
        inp['ln_mlp_offset'] = jnp.zeros((D,), jnp.float32)
        inp['w_fc1'] = rn((D, F))
        inp['b_fc1'] = jnp.zeros((F,), jnp.float32)
        inp['w_fc2'] = rn((F, D))
        inp['b_fc2'] = jnp.zeros((D,), jnp.float32)
        return inp
    _L2_xattn_all = _L2_xattn_setup()
    _L2_xattn_in = {k: v for k, v in _L2_xattn_all.items() if k in ('ln1_scale', 'ln1_offset', 'wq1', 'bq1', 'wk1', 'bk1', 'wv1', 'bv1', 'wo1', 'bo1', 'bias_k1', 'bias_v1', 'ln2_scale', 'ln2_offset', 'wq2', 'bq2', 'wk2', 'bk2', 'wv2', 'bv2', 'wo2', 'bo2', 'bias_k2', 'bias_v2', 'ln_mlp_scale', 'ln_mlp_offset', 'w_fc1', 'b_fc1', 'w_fc2', 'b_fc2')}
    del _L2_xattn_all

    def _L3_xattn_setup():
        import jax, jax.numpy as jnp
        import numpy as np
        H = 256
        NH = 32
        KVH = 8
        HD = H // NH
        GROUPS = NH // KVH
        EPS = 1e-06
        B, L, S = (4, 128, 128)

        def _gqa_forward(hidden_state, encoder_hidden_state, encoder_attention_mask, Wq, bq, Wk, bk, Wv, bv, Wo, bo, gamma, beta):
            b, l, _ = hidden_state.shape
            s = encoder_hidden_state.shape[1]
            q = hidden_state @ Wq + bq
            k = encoder_hidden_state @ Wk + bk
            v = encoder_hidden_state @ Wv + bv
            q = q.reshape(b, l, KVH, GROUPS, HD).transpose(0, 2, 3, 1, 4)
            k = k.reshape(b, s, KVH, HD).transpose(0, 2, 1, 3)
            v = v.reshape(b, s, KVH, HD).transpose(0, 2, 1, 3)
            scale = 1.0 / jnp.sqrt(jnp.asarray(HD, q.dtype))
            scores = jnp.einsum('bkgld,bksd->bkgls', q, k) * scale
            scores = scores + encoder_attention_mask[:, :, None, :, :]
            attn = jax.nn.softmax(scores, axis=-1)
            out = jnp.einsum('bkgls,bksd->bkgld', attn, v)
            out = out.transpose(0, 3, 1, 2, 4).reshape(b, l, H)
            out = out @ Wo + bo
            x = out + hidden_state
            mu = jnp.mean(x, axis=-1, keepdims=True)
            var = jnp.var(x, axis=-1, keepdims=True)
            return (x - mu) * jax.lax.rsqrt(var + EPS) * gamma + beta
        key = jax.random.key(seed)
        ks = jax.random.split(key, 12)
        sd = 0.02
        return {'hidden_state': jax.random.normal(ks[0], (B, L, H), jnp.float32), 'encoder_hidden_state': jax.random.normal(ks[1], (B, S, H), jnp.float32), 'encoder_attention_mask': jnp.zeros((B, 1, L, S), jnp.float32), 'Wq': jax.random.normal(ks[2], (H, H), jnp.float32) * sd, 'bq': jnp.zeros((H,), jnp.float32), 'Wk': jax.random.normal(ks[3], (H, KVH * HD), jnp.float32) * sd, 'bk': jnp.zeros((KVH * HD,), jnp.float32), 'Wv': jax.random.normal(ks[4], (H, KVH * HD), jnp.float32) * sd, 'bv': jnp.zeros((KVH * HD,), jnp.float32), 'Wo': jax.random.normal(ks[5], (H, H), jnp.float32) * sd, 'bo': jnp.zeros((H,), jnp.float32), 'gamma': jnp.ones((H,), jnp.float32), 'beta': jnp.zeros((H,), jnp.float32)}
    _L3_xattn_all = _L3_xattn_setup()
    _L3_xattn_in = {k: v for k, v in _L3_xattn_all.items() if k in ('Wq', 'bq', 'Wk', 'bk', 'Wv', 'bv', 'Wo', 'bo', 'gamma', 'beta')}
    del _L3_xattn_all
    return {'x': x, 'ctx_2048': ctx_2048, 'mask_BxS2_bf1': mask_BxS2_bf1, 'mask_Bx1xSxS2_ff0': mask_Bx1xSxS2_ff0, 'L0_xattn_ln1_w': _L0_xattn_in['ln1_w'], 'L0_xattn_ln1_b': _L0_xattn_in['ln1_b'], 'L0_xattn_q_w': _L0_xattn_in['q_w'], 'L0_xattn_q_b': _L0_xattn_in['q_b'], 'L0_xattn_k_w': _L0_xattn_in['k_w'], 'L0_xattn_k_b': _L0_xattn_in['k_b'], 'L0_xattn_v_w': _L0_xattn_in['v_w'], 'L0_xattn_v_b': _L0_xattn_in['v_b'], 'L0_xattn_cproj_w': _L0_xattn_in['cproj_w'], 'L0_xattn_cproj_b': _L0_xattn_in['cproj_b'], 'L0_xattn_ln2_w': _L0_xattn_in['ln2_w'], 'L0_xattn_ln2_b': _L0_xattn_in['ln2_b'], 'L0_xattn_fc_w': _L0_xattn_in['fc_w'], 'L0_xattn_fc_b': _L0_xattn_in['fc_b'], 'L0_xattn_proj_w': _L0_xattn_in['proj_w'], 'L0_xattn_proj_b': _L0_xattn_in['proj_b'], 'L1_xattn_ln1_w': _L1_xattn_in['ln1_w'], 'L1_xattn_ln1_b': _L1_xattn_in['ln1_b'], 'L1_xattn_ln2_w': _L1_xattn_in['ln2_w'], 'L1_xattn_ln2_b': _L1_xattn_in['ln2_b'], 'L1_xattn_maa_x': _L1_xattn_in['maa_x'], 'L1_xattn_maa_w1': _L1_xattn_in['maa_w1'], 'L1_xattn_maa_w2': _L1_xattn_in['maa_w2'], 'L1_xattn_maa_stack': _L1_xattn_in['maa_stack'], 'L1_xattn_time_decay': _L1_xattn_in['time_decay'], 'L1_xattn_td_w1': _L1_xattn_in['td_w1'], 'L1_xattn_td_w2': _L1_xattn_in['td_w2'], 'L1_xattn_u': _L1_xattn_in['u'], 'L1_xattn_Wr': _L1_xattn_in['Wr'], 'L1_xattn_Wk': _L1_xattn_in['Wk'], 'L1_xattn_Wv': _L1_xattn_in['Wv'], 'L1_xattn_Wg': _L1_xattn_in['Wg'], 'L1_xattn_Wo': _L1_xattn_in['Wo'], 'L1_xattn_gn_w': _L1_xattn_in['gn_w'], 'L1_xattn_gn_b': _L1_xattn_in['gn_b'], 'L1_xattn_ffn_maa_k': _L1_xattn_in['ffn_maa_k'], 'L1_xattn_ffn_maa_r': _L1_xattn_in['ffn_maa_r'], 'L1_xattn_Wfk': _L1_xattn_in['Wfk'], 'L1_xattn_Wfr': _L1_xattn_in['Wfr'], 'L1_xattn_Wfv': _L1_xattn_in['Wfv'], 'L2_xattn_ln1_scale': _L2_xattn_in['ln1_scale'], 'L2_xattn_ln1_offset': _L2_xattn_in['ln1_offset'], 'L2_xattn_wq1': _L2_xattn_in['wq1'], 'L2_xattn_bq1': _L2_xattn_in['bq1'], 'L2_xattn_wk1': _L2_xattn_in['wk1'], 'L2_xattn_bk1': _L2_xattn_in['bk1'], 'L2_xattn_wv1': _L2_xattn_in['wv1'], 'L2_xattn_bv1': _L2_xattn_in['bv1'], 'L2_xattn_wo1': _L2_xattn_in['wo1'], 'L2_xattn_bo1': _L2_xattn_in['bo1'], 'L2_xattn_bias_k1': _L2_xattn_in['bias_k1'], 'L2_xattn_bias_v1': _L2_xattn_in['bias_v1'], 'L2_xattn_ln2_scale': _L2_xattn_in['ln2_scale'], 'L2_xattn_ln2_offset': _L2_xattn_in['ln2_offset'], 'L2_xattn_wq2': _L2_xattn_in['wq2'], 'L2_xattn_bq2': _L2_xattn_in['bq2'], 'L2_xattn_wk2': _L2_xattn_in['wk2'], 'L2_xattn_bk2': _L2_xattn_in['bk2'], 'L2_xattn_wv2': _L2_xattn_in['wv2'], 'L2_xattn_bv2': _L2_xattn_in['bv2'], 'L2_xattn_wo2': _L2_xattn_in['wo2'], 'L2_xattn_bo2': _L2_xattn_in['bo2'], 'L2_xattn_bias_k2': _L2_xattn_in['bias_k2'], 'L2_xattn_bias_v2': _L2_xattn_in['bias_v2'], 'L2_xattn_ln_mlp_scale': _L2_xattn_in['ln_mlp_scale'], 'L2_xattn_ln_mlp_offset': _L2_xattn_in['ln_mlp_offset'], 'L2_xattn_w_fc1': _L2_xattn_in['w_fc1'], 'L2_xattn_b_fc1': _L2_xattn_in['b_fc1'], 'L2_xattn_w_fc2': _L2_xattn_in['w_fc2'], 'L2_xattn_b_fc2': _L2_xattn_in['b_fc2'], 'L3_xattn_Wq': _L3_xattn_in['Wq'], 'L3_xattn_bq': _L3_xattn_in['bq'], 'L3_xattn_Wk': _L3_xattn_in['Wk'], 'L3_xattn_bk': _L3_xattn_in['bk'], 'L3_xattn_Wv': _L3_xattn_in['Wv'], 'L3_xattn_bv': _L3_xattn_in['bv'], 'L3_xattn_Wo': _L3_xattn_in['Wo'], 'L3_xattn_bo': _L3_xattn_in['bo'], 'L3_xattn_gamma': _L3_xattn_in['gamma'], 'L3_xattn_beta': _L3_xattn_in['beta']}

def reference(x, ctx_2048, mask_BxS2_bf1, mask_Bx1xSxS2_ff0, L0_xattn_ln1_w, L0_xattn_ln1_b, L0_xattn_q_w, L0_xattn_q_b, L0_xattn_k_w, L0_xattn_k_b, L0_xattn_v_w, L0_xattn_v_b, L0_xattn_cproj_w, L0_xattn_cproj_b, L0_xattn_ln2_w, L0_xattn_ln2_b, L0_xattn_fc_w, L0_xattn_fc_b, L0_xattn_proj_w, L0_xattn_proj_b, L1_xattn_ln1_w, L1_xattn_ln1_b, L1_xattn_ln2_w, L1_xattn_ln2_b, L1_xattn_maa_x, L1_xattn_maa_w1, L1_xattn_maa_w2, L1_xattn_maa_stack, L1_xattn_time_decay, L1_xattn_td_w1, L1_xattn_td_w2, L1_xattn_u, L1_xattn_Wr, L1_xattn_Wk, L1_xattn_Wv, L1_xattn_Wg, L1_xattn_Wo, L1_xattn_gn_w, L1_xattn_gn_b, L1_xattn_ffn_maa_k, L1_xattn_ffn_maa_r, L1_xattn_Wfk, L1_xattn_Wfr, L1_xattn_Wfv, L2_xattn_ln1_scale, L2_xattn_ln1_offset, L2_xattn_wq1, L2_xattn_bq1, L2_xattn_wk1, L2_xattn_bk1, L2_xattn_wv1, L2_xattn_bv1, L2_xattn_wo1, L2_xattn_bo1, L2_xattn_bias_k1, L2_xattn_bias_v1, L2_xattn_ln2_scale, L2_xattn_ln2_offset, L2_xattn_wq2, L2_xattn_bq2, L2_xattn_wk2, L2_xattn_bk2, L2_xattn_wv2, L2_xattn_bv2, L2_xattn_wo2, L2_xattn_bo2, L2_xattn_bias_k2, L2_xattn_bias_v2, L2_xattn_ln_mlp_scale, L2_xattn_ln_mlp_offset, L2_xattn_w_fc1, L2_xattn_b_fc1, L2_xattn_w_fc2, L2_xattn_b_fc2, L3_xattn_Wq, L3_xattn_bq, L3_xattn_Wk, L3_xattn_bk, L3_xattn_Wv, L3_xattn_bv, L3_xattn_Wo, L3_xattn_bo, L3_xattn_gamma, L3_xattn_beta):
    import jax
    import jax.numpy as jnp

    def _L0_xattn_ref(hidden_states, encoder_hidden_states, encoder_attention_mask, ln1_w, ln1_b, q_w, q_b, k_w, k_b, v_w, v_b, cproj_w, cproj_b, ln2_w, ln2_b, fc_w, fc_b, proj_w, proj_b):
        import jax, jax.numpy as jnp
        import numpy as np
        D = 256
        H = 16
        HD = D // H
        INNER = 4 * D
        EPS = 1e-05

        def layer_norm(x, w, b):
            mu = jnp.mean(x, axis=-1, keepdims=True)
            var = jnp.mean(jnp.square(x - mu), axis=-1, keepdims=True)
            return (x - mu) * jax.lax.rsqrt(var + EPS) * w + b
        B, LQ, _ = hidden_states.shape
        LK = encoder_hidden_states.shape[1]
        residual = hidden_states
        x = layer_norm(hidden_states, ln1_w, ln1_b)
        q = (x @ q_w + q_b).reshape(B, LQ, H, HD).transpose(0, 2, 1, 3)
        k = (encoder_hidden_states @ k_w + k_b).reshape(B, LK, H, HD).transpose(0, 2, 1, 3)
        v = (encoder_hidden_states @ v_w + v_b).reshape(B, LK, H, HD).transpose(0, 2, 1, 3)
        scale = 1.0 / np.sqrt(HD).astype(np.float32)
        scores = jnp.einsum('bhqd,bhkd->bhqk', q, k) * scale
        mask = encoder_attention_mask[:, None, None, :]
        mask_value = jnp.finfo(scores.dtype).min
        scores = jnp.where(mask, scores, mask_value)
        attn = jax.nn.softmax(scores, axis=-1)
        out = jnp.einsum('bhqk,bhkd->bhqd', attn, v)
        out = out.transpose(0, 2, 1, 3).reshape(B, LQ, D)
        out = out @ cproj_w + cproj_b
        hidden = out + residual
        residual = hidden
        y = layer_norm(hidden, ln2_w, ln2_b)
        y = jax.nn.gelu(y @ fc_w + fc_b, approximate=True)
        y = y @ proj_w + proj_b
        return residual + y

    def _L1_xattn_ref(x, state, ln1_w, ln1_b, ln2_w, ln2_b, maa_x, maa_w1, maa_w2, maa_stack, time_decay, td_w1, td_w2, u, Wr, Wk, Wv, Wg, Wo, gn_w, gn_b, ffn_maa_k, ffn_maa_r, Wfk, Wfr, Wfv):
        import jax, jax.numpy as jnp
        import numpy as np
        E, H, L, B = (256, 32, 128, 4)
        S = E // H
        DM, DD = (32, 64)

        def _ln(x, w, b, eps=1e-05):
            m = x.mean(-1, keepdims=True)
            v = ((x - m) ** 2).mean(-1, keepdims=True)
            return (x - m) / jnp.sqrt(v + eps) * w + b

        def _block(x, state, ln1_w, ln1_b, ln2_w, ln2_b, maa_x, maa_w1, maa_w2, maa_stack, time_decay, td_w1, td_w2, u, Wr, Wk, Wv, Wg, Wo, gn_w, gn_b, ffn_maa_k, ffn_maa_r, Wfk, Wfr, Wfv):
            b, l, e = x.shape
            h = u.shape[0]
            s_ = e // h
            xa = _ln(x, ln1_w, ln1_b)
            sx = jnp.concatenate([state[:, 1:2] - xa[:, :1], xa[:, :-1] - xa[:, 1:]], axis=1)
            xxx = jnp.tanh((xa + sx * maa_x) @ maa_w1).reshape(b, l, 5, DM)
            xxx = jnp.einsum('blfd,fde->blfe', xxx, maa_w2)
            xm = xa[:, :, None] + sx[:, :, None] * (maa_stack + xxx)
            xk, xw, xv, xr, xg = (xm[:, :, j] for j in range(5))
            w = jnp.exp(-jnp.exp(time_decay + jnp.tanh(xw @ td_w1) @ td_w2)).reshape(b, l, h, s_)
            r = (xr @ Wr.T).reshape(b, l, h, s_)
            k = (xk @ Wk.T).reshape(b, l, h, s_)
            v = (xv @ Wv.T).reshape(b, l, h, s_)
            g = jax.nn.silu(xg @ Wg.T)
            s0 = state[:, 2:2 + s_].reshape(b, h, s_, s_)

            def step(s, rkvw):
                r_t, k_t, v_t, w_t = rkvw
                a = k_t[..., :, None] * v_t[..., None, :]
                out = jnp.einsum('bhi,bhij->bhj', r_t, u * a + s)
                s = a + w_t[..., :, None] * s
                return (s, out)
            rkvw = tuple((jnp.moveaxis(t, 1, 0) for t in (r, k, v, w)))
            _, out = jax.lax.scan(step, s0, rkvw)
            out = jnp.moveaxis(out, 0, 1).reshape(b, l, e)
            og = out.reshape(b, l, h, s_)
            m = og.mean(-1, keepdims=True)
            va = ((og - m) ** 2).mean(-1, keepdims=True)
            og = ((og - m) / jnp.sqrt(va + 1e-05)).reshape(b, l, e) * gn_w + gn_b
            x1 = x + og * g @ Wo.T
            xc = _ln(x1, ln2_w, ln2_b)
            sx2 = jnp.concatenate([state[:, 0:1] - xc[:, :1], xc[:, :-1] - xc[:, 1:]], axis=1)
            xk2 = xc + sx2 * ffn_maa_k
            xr2 = xc + sx2 * ffn_maa_r
            rr = jax.nn.sigmoid(xr2 @ Wfr.T)
            kk = jnp.square(jax.nn.relu(xk2 @ Wfk.T))
            return x1 + rr * (kk @ Wfv.T)
        return _block(x, state, ln1_w, ln1_b, ln2_w, ln2_b, maa_x, maa_w1, maa_w2, maa_stack, time_decay, td_w1, td_w2, u, Wr, Wk, Wv, Wg, Wo, gn_w, gn_b, ffn_maa_k, ffn_maa_r, Wfk, Wfr, Wfv)

    def _L2_xattn_ref(x, xf_1, xf_2, ln1_scale, ln1_offset, wq1, bq1, wk1, bk1, wv1, bv1, wo1, bo1, bias_k1, bias_v1, ln2_scale, ln2_offset, wq2, bq2, wk2, bk2, wv2, bv2, wo2, bo2, bias_k2, bias_v2, ln_mlp_scale, ln_mlp_offset, w_fc1, b_fc1, w_fc2, b_fc2):
        import jax, jax.numpy as jnp
        import numpy as np
        B, Q, S1, S2 = (4, 32, 256, 256)
        D, H, K, F = (256, 16, 128, 1024)
        LN_EPS = 1e-05

        def _layer_norm(x, scale, offset):
            mu = jnp.mean(x, axis=-1, keepdims=True)
            var = jnp.var(x, axis=-1, keepdims=True)
            return (x - mu) * jax.lax.rsqrt(var + LN_EPS) * scale + offset

        def _cross_attention(q_in, kv_in, wq, bq, wk, bk, wv, bv, wo, bo, bias_k, bias_v):
            b, q_len, _ = q_in.shape
            t = kv_in.shape[1]
            qh = (q_in @ wq + bq).reshape(b, q_len, H, K)
            kh = (kv_in @ wk + bk).reshape(b, t, H, K)
            vh = (kv_in @ wv + bv).reshape(b, t, H, K)
            kh = jnp.concatenate([kh, jnp.broadcast_to(bias_k, (b, 1, H, K))], axis=1)
            vh = jnp.concatenate([vh, jnp.broadcast_to(bias_v, (b, 1, H, K))], axis=1)
            scale = jnp.sqrt(jnp.asarray(K, q_in.dtype))
            logits = jnp.einsum('bqhk,bthk->bhqt', qh, kh) / scale
            weights = jax.nn.softmax(logits, axis=-1)
            ctx = jnp.einsum('bhqt,bthk->bqhk', weights, vh).reshape(b, q_len, H * K)
            return ctx @ wo + bo

        def _forward(x, xf_1, xf_2, ln1_scale, ln1_offset, wq1, bq1, wk1, bk1, wv1, bv1, wo1, bo1, bias_k1, bias_v1, ln2_scale, ln2_offset, wq2, bq2, wk2, bk2, wv2, bv2, wo2, bo2, bias_k2, bias_v2, ln_mlp_scale, ln_mlp_offset, w_fc1, b_fc1, w_fc2, b_fc2):
            res = x
            h = _layer_norm(x, ln1_scale, ln1_offset)
            x = res + _cross_attention(h, xf_1, wq1, bq1, wk1, bk1, wv1, bv1, wo1, bo1, bias_k1, bias_v1)
            res = x
            h = _layer_norm(x, ln2_scale, ln2_offset)
            x = res + _cross_attention(h, xf_2, wq2, bq2, wk2, bk2, wv2, bv2, wo2, bo2, bias_k2, bias_v2)
            h = _layer_norm(x, ln_mlp_scale, ln_mlp_offset)
            h = jax.nn.gelu(h @ w_fc1 + b_fc1, approximate=False) @ w_fc2 + b_fc2
            return x + h
        return _forward(x, xf_1, xf_2, ln1_scale, ln1_offset, wq1, bq1, wk1, bk1, wv1, bv1, wo1, bo1, bias_k1, bias_v1, ln2_scale, ln2_offset, wq2, bq2, wk2, bk2, wv2, bv2, wo2, bo2, bias_k2, bias_v2, ln_mlp_scale, ln_mlp_offset, w_fc1, b_fc1, w_fc2, b_fc2)

    def _L3_xattn_ref(hidden_state, encoder_hidden_state, encoder_attention_mask, Wq, bq, Wk, bk, Wv, bv, Wo, bo, gamma, beta):
        import jax, jax.numpy as jnp
        import numpy as np
        H = 256
        NH = 32
        KVH = 8
        HD = H // NH
        GROUPS = NH // KVH
        EPS = 1e-06
        B, L, S = (4, 128, 128)

        def _gqa_forward(hidden_state, encoder_hidden_state, encoder_attention_mask, Wq, bq, Wk, bk, Wv, bv, Wo, bo, gamma, beta):
            b, l, _ = hidden_state.shape
            s = encoder_hidden_state.shape[1]
            q = hidden_state @ Wq + bq
            k = encoder_hidden_state @ Wk + bk
            v = encoder_hidden_state @ Wv + bv
            q = q.reshape(b, l, KVH, GROUPS, HD).transpose(0, 2, 3, 1, 4)
            k = k.reshape(b, s, KVH, HD).transpose(0, 2, 1, 3)
            v = v.reshape(b, s, KVH, HD).transpose(0, 2, 1, 3)
            scale = 1.0 / jnp.sqrt(jnp.asarray(HD, q.dtype))
            scores = jnp.einsum('bkgld,bksd->bkgls', q, k) * scale
            scores = scores + encoder_attention_mask[:, :, None, :, :]
            attn = jax.nn.softmax(scores, axis=-1)
            out = jnp.einsum('bkgls,bksd->bkgld', attn, v)
            out = out.transpose(0, 3, 1, 2, 4).reshape(b, l, H)
            out = out @ Wo + bo
            x = out + hidden_state
            mu = jnp.mean(x, axis=-1, keepdims=True)
            var = jnp.var(x, axis=-1, keepdims=True)
            return (x - mu) * jax.lax.rsqrt(var + EPS) * gamma + beta
        return _gqa_forward(hidden_state, encoder_hidden_state, encoder_attention_mask, Wq, bq, Wk, bk, Wv, bv, Wo, bo, gamma, beta)
    x = _L0_xattn_ref(x, ctx_2048, mask_BxS2_bf1, L0_xattn_ln1_w, L0_xattn_ln1_b, L0_xattn_q_w, L0_xattn_q_b, L0_xattn_k_w, L0_xattn_k_b, L0_xattn_v_w, L0_xattn_v_b, L0_xattn_cproj_w, L0_xattn_cproj_b, L0_xattn_ln2_w, L0_xattn_ln2_b, L0_xattn_fc_w, L0_xattn_fc_b, L0_xattn_proj_w, L0_xattn_proj_b)
    x = _L1_xattn_ref(x, ctx_2048, L1_xattn_ln1_w, L1_xattn_ln1_b, L1_xattn_ln2_w, L1_xattn_ln2_b, L1_xattn_maa_x, L1_xattn_maa_w1, L1_xattn_maa_w2, L1_xattn_maa_stack, L1_xattn_time_decay, L1_xattn_td_w1, L1_xattn_td_w2, L1_xattn_u, L1_xattn_Wr, L1_xattn_Wk, L1_xattn_Wv, L1_xattn_Wg, L1_xattn_Wo, L1_xattn_gn_w, L1_xattn_gn_b, L1_xattn_ffn_maa_k, L1_xattn_ffn_maa_r, L1_xattn_Wfk, L1_xattn_Wfr, L1_xattn_Wfv)
    x = _L2_xattn_ref(x, ctx_2048, ctx_2048, L2_xattn_ln1_scale, L2_xattn_ln1_offset, L2_xattn_wq1, L2_xattn_bq1, L2_xattn_wk1, L2_xattn_bk1, L2_xattn_wv1, L2_xattn_bv1, L2_xattn_wo1, L2_xattn_bo1, L2_xattn_bias_k1, L2_xattn_bias_v1, L2_xattn_ln2_scale, L2_xattn_ln2_offset, L2_xattn_wq2, L2_xattn_bq2, L2_xattn_wk2, L2_xattn_bk2, L2_xattn_wv2, L2_xattn_bv2, L2_xattn_wo2, L2_xattn_bo2, L2_xattn_bias_k2, L2_xattn_bias_v2, L2_xattn_ln_mlp_scale, L2_xattn_ln_mlp_offset, L2_xattn_w_fc1, L2_xattn_b_fc1, L2_xattn_w_fc2, L2_xattn_b_fc2)
    x = _L3_xattn_ref(x, ctx_2048, mask_Bx1xSxS2_ff0, L3_xattn_Wq, L3_xattn_bq, L3_xattn_Wk, L3_xattn_bk, L3_xattn_Wv, L3_xattn_bv, L3_xattn_Wo, L3_xattn_bo, L3_xattn_gamma, L3_xattn_beta)
    return x

_drawn_inputs = setup_inputs


def setup_inputs(seed=0):
    import zlib

    import numpy as np

    out = dict(_drawn_inputs(seed))
    spreads = {'L0_xattn_ln1_w': (1.0, 0.6),
     'L0_xattn_ln1_b': (0.0, 0.8),
     'L0_xattn_q_b': (0.0, 0.8),
     'L0_xattn_k_b': (0.0, 2.0),
     'L0_xattn_v_b': (0.0, 0.277),
     'L0_xattn_cproj_b': (0.0, 0.1),
     'L0_xattn_ln2_w': (1.0, 0.6),
     'L0_xattn_ln2_b': (0.0, 0.764),
     'L0_xattn_fc_b': (0.0, 0.1),
     'L0_xattn_proj_b': (0.0, 0.1),
     'L1_xattn_ln1_w': (1.0, 0.6),
     'L1_xattn_ln1_b': (0.0, 0.6),
     'L1_xattn_ln2_w': (1.0, 0.6),
     'L1_xattn_ln2_b': (0.0, 0.8),
     'L1_xattn_gn_w': (1.0, 0.6),
     'L1_xattn_gn_b': (0.0, 0.8),
     'L2_xattn_ln1_scale': (1.0, 0.6),
     'L2_xattn_ln1_offset': (0.0, 0.8),
     'L2_xattn_bq1': (0.0, 0.8),
     'L2_xattn_bk1': (0.0, 2.0),
     'L2_xattn_bv1': (0.0, 0.1),
     'L2_xattn_bo1': (0.0, 0.1),
     'L2_xattn_ln2_scale': (1.0, 0.6),
     'L2_xattn_ln2_offset': (0.0, 0.8),
     'L2_xattn_bq2': (0.0, 0.8),
     'L2_xattn_bk2': (0.0, 2.0),
     'L2_xattn_bv2': (0.0, 0.285),
     'L2_xattn_bo2': (0.0, 0.1),
     'L2_xattn_ln_mlp_scale': (1.0, 0.6),
     'L2_xattn_ln_mlp_offset': (0.0, 2.0),
     'L2_xattn_b_fc1': (0.0, 0.65),
     'L2_xattn_b_fc2': (0.0, 0.1),
     'L3_xattn_bq': (0.0, 2.0),
     'L3_xattn_bk': (0.0, 2.0),
     'L3_xattn_bv': (0.0, 0.836),
     'L3_xattn_bo': (0.0, 0.1),
     'L3_xattn_gamma': (1.0, 0.2),
     'L3_xattn_beta': (0.0, 0.1)}
    factors = {'L0_xattn_q_w': 8.0,
     'L0_xattn_k_w': 8.0,
     'L1_xattn_maa_x': 8.0,
     'L1_xattn_maa_w1': 8.0,
     'L1_xattn_maa_w2': 8.0,
     'L1_xattn_maa_stack': 3.042,
     'L1_xattn_time_decay': 2.955,
     'L1_xattn_td_w1': 8.0,
     'L1_xattn_td_w2': 8.0,
     'L1_xattn_u': 6.284,
     'L1_xattn_ffn_maa_k': 8.0,
     'L1_xattn_ffn_maa_r': 8.0,
     'L1_xattn_Wfk': 3.006,
     'L1_xattn_Wfr': 8.0,
     'L1_xattn_Wfv': 2.824,
     'L2_xattn_wq1': 8.0,
     'L2_xattn_wk1': 8.0,
     'L2_xattn_bias_k1': 64.0,
     'L2_xattn_bias_v1': 64.0,
     'L2_xattn_wq2': 8.0,
     'L2_xattn_wk2': 8.0,
     'L2_xattn_bias_k2': 64.0,
     'L2_xattn_bias_v2': 64.0,
     'L3_xattn_Wq': 8.0,
     'L3_xattn_Wk': 8.0}
    for name, (base, spread) in spreads.items():
        noise = np.random.default_rng([zlib.crc32(name.encode()), seed]).standard_normal(out[name].shape)
        drawn = base * np.exp(spread * noise) if base else spread * noise
        out[name] = jnp.asarray(drawn.astype(out[name].dtype))
    for name, factor in factors.items():
        out[name] = (out[name] * factor).astype(out[name].dtype)
    return out
```

```python
import math
from contextlib import ExitStack

import concourse.bass as bass
from concourse import mybir

F32 = mybir.dt.float32
U8 = mybir.dt.uint8
ALU = mybir.AluOpType
ACT = mybir.ActivationFunctionType
AX = mybir.AxisListType

P = 128
B = 64
S = 64
D = 256
DC = D // P
T = 256
NB = T // S
NP = T // P
TRIPS = B * S // T
INNER = 4 * D
MC = INNER // P

COLS = ["L0_xattn_ln1_w", "L0_xattn_ln1_b", "L0_xattn_q_b", "L0_xattn_k_b", "L0_xattn_ln2_w",
        "L0_xattn_ln2_b", "L0_xattn_fc_b",
        "L1_xattn_ln1_w", "L1_xattn_ln1_b", "L1_xattn_ln2_w", "L1_xattn_ln2_b", "L1_xattn_maa_x",
        "L1_xattn_maa_stack", "L1_xattn_time_decay", "L1_xattn_u", "L1_xattn_gn_w",
        "L1_xattn_gn_b", "L1_xattn_ffn_maa_k", "L1_xattn_ffn_maa_r",
        "L2_xattn_ln1_scale", "L2_xattn_ln1_offset", "L2_xattn_bq1", "L2_xattn_bk1",
        "L2_xattn_bias_k1", "L2_xattn_bias_v1", "L2_xattn_ln2_scale", "L2_xattn_ln2_offset",
        "L2_xattn_bq2", "L2_xattn_bk2", "L2_xattn_bias_k2", "L2_xattn_bias_v2",
        "L2_xattn_ln_mlp_scale", "L2_xattn_ln_mlp_offset", "L2_xattn_b_fc1",
        "L3_xattn_bq", "L3_xattn_bk_rep"]
COL_WIDTH = {"L0_xattn_fc_b": 8, "L1_xattn_maa_stack": 10, "L2_xattn_bq1": 16, "L2_xattn_bk1": 16,
             "L2_xattn_bias_k1": 16, "L2_xattn_bias_v1": 16, "L2_xattn_bq2": 16, "L2_xattn_bk2": 16,
             "L2_xattn_bias_k2": 16, "L2_xattn_bias_v2": 16, "L2_xattn_b_fc1": 8}
ROWS = ["L0_xattn_v_b", "L0_xattn_cproj_b", "L0_xattn_proj_b", "L2_xattn_bo1", "L2_xattn_bo2",
        "L2_xattn_b_fc2", "L3_xattn_bo", "L3_xattn_gamma", "L3_xattn_beta", "L3_xattn_bv"]



class Norm:
    pass


class NormSignals:
    pass


class Program:

    def __init__(self, nc, dram):
        self.nc = nc
        self.dram = dram
        self.at = {}
        self.col0 = {}
        n = 0
        for name in COLS:
            self.col0[name] = n
            n += COL_WIDTH.get(name, 2)
        self.ncols = n

    def col(self, name, c=0):
        n = self.col0[name] + c
        return self.cols[:, n:n + 1]

    def cols_of(self, name):
        n = self.col0[name]
        return self.cols[:, n:n + COL_WIDTH.get(name, 2)]

    def ln_tiles(self, sb, tag=""):
        ln = Norm()
        ln.stats = sb(f"ln{tag}_stats", [P, NP, 6])
        ln.mv = sb(f"ln{tag}_mv", [P, NP, 2])
        ln.ve = sb(f"ln{tag}_ve", [P, NP])
        ln.rstd = sb(f"ln{tag}_rstd", [P, NP])
        return ln

    def ln_sems(self, sem, tag=""):
        s = NormSignals()
        s.stats, s.mv, s.xn_ready = (sem(f"ln{tag}_{n}", NP) for n in ("stats", "mv", "xn_ready"))
        s.ve, s.rstd = sem(f"ln{tag}_ve", 1), sem(f"ln{tag}_rstd", 1)
        return s

    def ln_rstd(self, pool, ln, s, n):
        pool.wait_ge(s.ve, n + 1)
        self.nc.gpsimd.tensor_tensor(ln.rstd[:], ln.ve[:], self.neg_half[:, 0:NP], ALU.pow
                                     ).then_inc(s.rstd, 1)

    def ln_normalise(self, dve, ln, s, src, dst, n, eps=1e-5):
        v = self.nc.vector
        for t in range(NP):
            v.bn_stats(ln.stats[:, t, :], src[:, t, :]).then_inc(s.stats, 1)
        dve.wait_ge(s.stats, NP * n + NP)
        v.nop(nofuse=True)
        for t in range(NP):
            v.bn_aggr(ln.mv[:, t, :], ln.stats[:, t, :]).then_inc(s.mv, 1)
        dve.wait_ge(s.mv, NP * n + NP)
        v.tensor_scalar(ln.ve[:], ln.mv[:, :, 1], eps, None, ALU.add).then_inc(s.ve, 1)
        dve.wait_ge(s.rstd, n + 1)
        for t in range(NP):
            v.tensor_scalar(dst[:, t, :], src[:, t, :], ln.mv[:, t, 0:1], ln.rstd[:, t:t + 1],
                            ALU.subtract, ALU.mult).then_inc(s.xn_ready, 1)

    def transpose_tiles(self, src, n):
        for c in range(DC):
            for t in range(NP):
                mm = self.nc.tensor.transpose(bank(self.psum, n, [DC, NP, P])[:, c, t, :],
                                              src[:, t, c * P:(c + 1) * P], self.ident)
        return mm

    def project_T(self, w, xT, n, outs):
        for m in range(outs):
            for c in range(DC):
                x = xT[:, c]
                mm = self.nc.tensor.matmul(bank(self.psum, n, [2, T])[:, m, :],
                                           w[:, c, m * P:(m + 1) * P], x,
                                           start=(c == 0), stop=(c == DC - 1))
        return mm

    def project_rows(self, xT, w, n, chunks):
        for t in range(NP):
            for c in range(chunks):
                mm = self.nc.tensor.matmul(bank(self.psum, n, [NP, D])[:, t, :],
                                           xT[:, c, t * P:(t + 1) * P], w[:, c, :],
                                           start=(c == 0), stop=(c == chunks - 1))
        return mm

    def rowv(self, name):
        n = D * ROWS.index(name)
        return self.rows[:, n:n + (S if name == "L3_xattn_bv" else D)]

    def row(self, name, times):
        return self.rowv(name).unsqueeze(1).to_broadcast([P, times, D])


def weight(ap):
    return ap.rearrange("(c p) n -> p c n", p=P)


def bank(ps, n, shape=None):
    v = ps[:, n, :]
    if shape is not None:
        names = "abcd"[:len(shape)]
        v = v.rearrange(f"p ({' '.join(names)}) -> p {' '.join(names)}", **dict(zip(names, shape)))
    return v


def tokens(ap):
    return ap.rearrange("(g t p) e -> g p t e", t=NP, p=P)


def start_counts(nc, sems):
    with nc.Block() as block:
        @block.gpsimd
        def _(pool):
            for s, _ in sems:
                nc.gpsimd.sem_clear(s)
            for s, per in sems:
                if per:
                    nc.gpsimd.sem_inc(s, per)



def stage_l0(pr, x_src, x_dst):
    nc, dram, PS = pr.nc, pr.dram, pr.psum
    H, HD = 16, 16
    SCALE = 1.0 / math.sqrt(HD)
    MASKED = 3.4028234663852886e38
    RG = 4
    with ExitStack() as ctx:
        def sb(name, shape, dt=F32):
            return ctx.enter_context(nc.sbuf_tensor("l0_" + name, shape, dt))

        sems = []

        def sem(name, per):
            s = ctx.enter_context(nc.semaphore("l0_" + name))
            sems.append((s, per))
            return s

        wq, wk, wv, wo = (sb(n, [P, DC, D]) for n in ("wq", "wk", "wv", "wo"))
        wfc = sb("wfc", [P, DC, INNER])
        wproj = sb("wproj", [P, MC, D])
        qb_scaled = sb("qb_scaled", [P, DC])
        key_mask = sb("key_mask", [P, B // 2, S], U8)
        mask_add = sb("mask_add", [P, B // 2, S])
        x_in = sb("x_in", [P, NP, D])
        x_res = sb("x_res", [P, NP, D])
        ctxT = sb("ctxT", [P, DC, NB, 2, S])
        ln = pr.ln_tiles(sb)
        xn = sb("xn", [P, NP, D])
        hT = sb("hT", [P, DC, T])
        qT = sb("qT", [P, DC, T])
        k_blk = sb("k_blk", [P, DC, NB, 2, S])
        v_blk = sb("v_blk", [P, NB, H // 2, 2, HD])
        sc = [sb(f"sc{t}", [P, H, S]) for t in range(NP)]
        mx = sb("mx", [P, NP, H])
        sm = sb("sm", [P, NP, H])
        rs = sb("rs", [P, NP, H])
        pT = sb("pT", [P, NP, H // 2, P])
        oT = sb("oT", [P, DC, T])
        xb = sb("xb", [P, NP, D])
        hid = sb("hid", [P, NP, D])
        hb = sb("hb", [P, NP, D])
        h2T = sb("h2T", [P, DC, T])
        act = sb("act", [P, MC, T])
        outt = sb("outt", [P, NP, D])

        weights_in, mask_in, setup = sem("weights_in", 0), sem("mask_in", 0), sem("setup", 0)
        x_loaded, ctx_loaded, res_loaded = (sem("x_loaded", 16), sem("ctx_loaded", 64),
                                            sem("res_loaded", 16))
        stored = sem("stored", 16)
        ln_s = pr.ln_sems(sem)
        xnT_ps, hT_ready = sem("xnT_ps", 1), sem("hT_ready", 2)
        q_ps, qT_ready = sem("q_ps", 1), sem("qT_ready", 2)
        k_ps, k_ready = sem("k_ps", 1), sem("k_ready", 4)
        v_ps, v_ready = sem("v_ps", 2), sem("v_ready", 8)
        s_ps, s_masked, s_max, s_sub, s_exp = (sem(n, NP) for n in
                                               ("s_ps", "s_masked", "s_max", "s_sub", "s_exp"))
        s_sum, s_rec, p_ready = (sem(n, NP) for n in ("s_sum", "s_rec", "p_ready"))
        pT_ps, pT_ready = sem("pT_ps", NP), sem("pT_ready", NP)
        o_ps, oT_ready = sem("o_ps", 1), sem("oT_ready", 1)
        c_ps, xb_ready, hid_ready = sem("c_ps", 1), sem("xb_ready", 1), sem("hid_ready", 1)
        ln2_s = pr.ln_sems(sem, "2")
        hnT_ps, h2T_ready = sem("hnT_ps", 1), sem("h2T_ready", 2)
        fc_ps, act_ready, m_ps = sem("fc_ps", 4), sem("act_ready", MC), sem("m_ps", 1)
        hb_ready, out_ready = sem("hb_ready", 1), sem("out_ready", 1)
        start_counts(nc, sems)
        xv, ov = tokens(x_src), tokens(x_dst)
        cv = dram["ctxT"].rearrange("(c p) (g b s) -> g c p b s", p=P, b=NB, s=S)

        block = ctx.enter_context(nc.Block())

        @block.sync
        def _(sp):
            for b2 in range(2):
                src = dram["key_mask"].rearrange("(n t) k -> t n k", t=2)[b2]
                sp.dma_start(key_mask[64 * b2:64 * b2 + 64, :, :],
                             src.partition_broadcast(64)).then_inc(mask_in, 16)

            def load(i):
                sp.dma_start(x_in[:], xv[i - 1]).then_inc(x_loaded, 16)
                load_ctx(i)
                sp.dma_start(x_res[:], xv[i - 1]).then_inc(res_loaded, 16)

            def load_ctx(i):
                for c in range(DC):
                    for u in range(2):
                        sp.dma_start(ctxT[:, c, :, u, :], cv[i - 1, c]).then_inc(ctx_loaded, 16)

            def store(i):
                sp.wait_ge(out_ready, i + 1)
                sp.dma_start(ov[i - 1], outt[:]).then_inc(stored, 16)

            load(1)
            for dst, name in ((wq, "L0_xattn_q_w"), (wk, "L0_xattn_k_w"), (wv, "L0_xattn_v_w"),
                              (wo, "L0_xattn_cproj_w"), (wfc, "L0_xattn_fc_w"),
                              (wproj, "L0_xattn_proj_w")):
                sp.dma_start(dst[:], weight(dram[name])).then_inc(weights_in, 16)
            with sp.Fori(1, TRIPS) as i:
                sp.wait_ge(ln_s.xn_ready, 2 * i + 2)
                sp.dma_start(x_in[:], xv[i]).then_inc(x_loaded, 16)
                sp.wait_ge(v_ps, 2 * i + 2)
                load_ctx(i + 1)
                sp.wait_ge(xb_ready, i + 1)
                sp.dma_start(x_res[:], xv[i]).then_inc(res_loaded, 16)
                store(i)
            store(TRIPS)
            sp.wait_ge(stored, 16 * TRIPS + 16)

        @block.gpsimd
        def _(pool):
            nc.gpsimd.memset(v_blk[:], 0.0).then_inc(setup, 1)
            with pool.Fori(1, TRIPS + 1) as i:
                pr.ln_rstd(pool, ln, ln_s, i)
                pool.wait_ge(res_loaded, 16 * (i + 1))
                pool.wait_ge(hid_ready, i)
                nc.gpsimd.tensor_tensor(xb[:], x_res[:], pr.row("L0_xattn_cproj_b", NP), ALU.add
                                        ).then_inc(xb_ready, 1)
                for t in range(NP):
                    s3 = sc[t][:]
                    pool.wait_ge(s_rec, 2 * i + t + 1)
                    nc.gpsimd.tensor_tensor(s3, s3, rs[:, t, :].unsqueeze(2).to_broadcast([P, H, S]),
                                            ALU.mult).then_inc(p_ready, 1)
                pr.ln_rstd(pool, ln, ln2_s, i)
                pool.wait_ge(hid_ready, i + 1)
                pool.wait_ge(out_ready, i)
                nc.gpsimd.tensor_tensor(hb[:], hid[:], pr.row("L0_xattn_proj_b", NP), ALU.add
                                        ).then_inc(hb_ready, 1)

        @block.scalar
        def _(act_e):
            act_e.wait_ge(setup, 3)
            with act_e.Fori(1, TRIPS + 1) as i:
                act_e.wait_ge(q_ps, i + 1)
                for c in range(DC):
                    nc.scalar.activation(qT[:, c, :], bank(PS, 5, [2, T])[:, c, :], ACT.Identity,
                                         bias=qb_scaled[:, c:c + 1], scale=SCALE
                                         ).then_inc(qT_ready, 1)
                for t in range(NP):
                    act_e.wait_ge(s_sub, 2 * i + t + 1)
                    nc.scalar.activation(sc[t][:], sc[t][:], ACT.Exp).then_inc(s_exp, 1)
                for t in range(NP):
                    act_e.wait_ge(pT_ps, 2 * i + t + 1)
                    nc.scalar.copy(pT[:, t, :, :], PS[:, 2 * t:2 * t + 2, :].rearrange(
                        "p a (b q) -> p (a b) q", q=P)).then_inc(pT_ready, 1)
                act_e.wait_ge(o_ps, i + 1)
                nc.scalar.copy(oT[:], bank(PS, 6, [DC, T])).then_inc(oT_ready, 1)
                for m in range(MC):
                    act_e.wait_ge(fc_ps, 4 * i + m // 2 + 1)
                    nc.scalar.activation(act[:, m, :], bank(PS, m // 2, [2, T])[:, m % 2, :],
                                         ACT.Gelu_apprx_tanh, bias=pr.col("L0_xattn_fc_b", m)
                                         ).then_inc(act_ready, 1)

        @block.vector
        def _(dve):
            dve.wait_ge(mask_in, 32)
            nc.vector.tensor_scalar(mask_add[:], key_mask[:], MASKED, -MASKED, ALU.mult, ALU.add
                                    ).then_inc(setup, 1)
            nc.vector.tensor_scalar(qb_scaled[:], pr.cols_of("L0_xattn_q_b"), SCALE, None, ALU.mult
                                    ).then_inc(setup, 1)
            dve.wait_ge(setup, 3)
            with dve.Fori(1, TRIPS + 1) as i:
                dve.wait_ge(x_loaded, 16 * (i + 1))
                dve.wait_ge(xnT_ps, i)
                pr.ln_normalise(dve, ln, ln_s, x_in, xn, i)
                dve.wait_ge(xnT_ps, i + 1)
                for c in range(DC):
                    nc.vector.tensor_scalar(hT[:, c, :], bank(PS, 4, [DC, T])[:, c, :],
                                            pr.col("L0_xattn_ln1_w", c), pr.col("L0_xattn_ln1_b", c),
                                            ALU.mult, ALU.add).then_inc(hT_ready, 1)
                dve.wait_ge(k_ps, i + 1)
                for c in range(DC):
                    for hh in range(2):
                        nc.vector.tensor_scalar(
                            k_blk[:, c, :, hh, :],
                            bank(PS, 6, [DC, NB, S])[:, c, :, :],
                            pr.col("L0_xattn_k_b", c), pr.head2[:, hh:hh + 1], ALU.add, ALU.mult
                        ).then_inc(k_ready, 1)
                for t in range(NP):
                    dve.wait_ge(v_ps, 2 * i + t + 1)
                    for hh in range(2):
                        half = slice(64 * hh, 64 * hh + 64)
                        for u in range(2):
                            vp = bank(PS, 7 if t == 0 else 5, [2, H // 2, 2, HD])
                            bias = pr.rowv("L0_xattn_v_b")[half, :].rearrange(
                                "p (a h e) -> p a h e", h=2, e=HD)[:, :, hh, :]
                            nc.vector.tensor_tensor(v_blk[half, 2 * t + u, :, hh, :],
                                                    vp[half, u, :, hh, :], bias,
                                                    ALU.add).then_inc(v_ready, 1)
                for t in range(NP):
                    dve.wait_ge(s_ps, 2 * i + t + 1)
                    m = mask_add[:, NP * (i - 1) + t, :]
                    nc.vector.tensor_tensor(
                        sc[t][:].rearrange("p (r h) k -> p r h k", r=RG),
                        PS[:, 0:RG, 0:256].rearrange("p r (h k) -> p r h k", k=S),
                        m.unsqueeze(1).unsqueeze(1).to_broadcast([P, RG, H // RG, S]), ALU.add
                    ).then_inc(s_masked, 1)
                    dve.wait_ge(s_masked, 2 * i + t + 1)
                    nc.vector.tensor_reduce(mx[:, t, :], sc[t][:], AX.X, ALU.max
                                            ).then_inc(s_max, 1)
                    dve.wait_ge(s_max, 2 * i + t + 1)
                    nc.vector.tensor_tensor(sc[t][:], sc[t][:],
                                            mx[:, t, :].unsqueeze(2).to_broadcast([P, H, S]),
                                            ALU.subtract).then_inc(s_sub, 1)
                for t in range(NP):
                    dve.wait_ge(s_exp, 2 * i + t + 1)
                    nc.vector.tensor_reduce(sm[:, t, :], sc[t][:], AX.X, ALU.add
                                            ).then_inc(s_sum, 1)
                    dve.wait_ge(s_sum, 2 * i + t + 1)
                    nc.vector.reciprocal(rs[:, t, :], sm[:, t, :]).then_inc(s_rec, 1)
                dve.wait_ge(c_ps, i + 1)
                dve.wait_ge(xb_ready, i + 1)
                dve.wait_ge(hb_ready, i)
                nc.vector.tensor_tensor(hid[:], bank(PS, 7, [NP, D]), xb[:], ALU.add
                                        ).then_inc(hid_ready, 1)
                dve.wait_ge(hid_ready, i + 1)
                pr.ln_normalise(dve, ln, ln2_s, hid, xn, i)
                dve.wait_ge(hnT_ps, i + 1)
                for c in range(DC):
                    nc.vector.tensor_scalar(h2T[:, c, :], bank(PS, 4, [DC, T])[:, c, :],
                                            pr.col("L0_xattn_ln2_w", c), pr.col("L0_xattn_ln2_b", c),
                                            ALU.mult, ALU.add).then_inc(h2T_ready, 1)
                dve.wait_ge(m_ps, i + 1)
                dve.wait_ge(hb_ready, i + 1)
                dve.wait_ge(stored, 16 * i)
                nc.vector.tensor_tensor(outt[:], bank(PS, 5, [NP, D]), hb[:], ALU.add
                                        ).then_inc(out_ready, 1)

        @block.tensor
        def _(pe):
            pe.wait_ge(weights_in, 16 * 6)
            pe.wait_ge(setup, 3)
            with pe.Fori(1, TRIPS + 1) as i:
                pe.wait_ge(h2T_ready, 2 * i)
                pe.wait_ge(ln_s.xn_ready, 2 * i + 2)
                pr.transpose_tiles(xn, 4).then_inc(xnT_ps, 1)
                pe.wait_ge(hid_ready, i)
                pe.wait_ge(out_ready, i)
                pe.wait_ge(ctx_loaded, 64 * (i + 1))
                pr.project_T(wk, ctxT[:, :, :, 0, :], 6, DC).then_inc(k_ps, 1)
                pe.wait_ge(hT_ready, 2 * i + 2)
                pr.project_T(wq, hT, 5, DC).then_inc(q_ps, 1)

                def values(t):
                    for u in range(2):
                        b = 2 * t + u
                        for c in range(DC):
                            two = ctxT[:, c, b, :, :].rearrange("p u s -> p (u s)")
                            mm = nc.tensor.matmul(bank(PS, 7 if t == 0 else 5, [2, D])[:, u, :],
                                                  two, wv[:, c, :], start=(c == 0), stop=(c == 1))
                    mm.then_inc(v_ps, 1)

                def scores(t):
                    for r in range(RG):
                        rows = slice(32 * r, 32 * r + 32)
                        for c in range(DC):
                            for b2 in range(2):
                                b = 2 * t + b2
                                mm = nc.tensor.matmul(
                                    bank(PS, r, [4, P])[64 * b2:64 * b2 + 64, c, :],
                                    qT[rows, c, b * S:(b + 1) * S],
                                    k_blk[rows, c, b, :, :], start=True, stop=True)
                    mm.then_inc(s_ps, 1)

                values(0)
                pe.wait_ge(qT_ready, 2 * i + 2)
                pe.wait_ge(k_ready, 4 * i + 4)
                pe.wait_ge(act_ready, 8 * i)
                scores(0)
                values(1)
                pe.wait_ge(s_masked, 2 * i + 1)
                scores(1)
                pe.wait_ge(s_masked, 2 * i + 2)
                for t in range(NP):
                    pe.wait_ge(p_ready, 2 * i + t + 1)
                    for n in range(H // 2):
                        mm = nc.tensor.transpose(
                            bank(PS, 2 * t + n // 4, [4, P])[:, n % 4, :],
                            sc[t][:, 2 * n:2 * n + 2, :].rearrange("p h k -> p (h k)"), pr.ident)
                    mm.then_inc(pT_ps, 1)
                pe.wait_ge(v_ready, 8 * i + 8)
                for t in range(NP):
                    pe.wait_ge(pT_ready, 2 * i + t + 1)
                    for c in range(DC):
                        for r in range(RG):
                            for b2 in range(2):
                                b = 2 * t + b2
                                mm = nc.tensor.matmul(
                                    bank(PS, 6, [DC, T])[32 * r:32 * r + 32, c, b * S:(b + 1) * S],
                                    v_blk[:, b, c * RG + r, :, :].rearrange("p h e -> p (h e)"),
                                    pT[:, t, 2 * r + c, b2 * S:(b2 + 1) * S],
                                    start=True, stop=True)
                mm.then_inc(o_ps, 1)
                pe.wait_ge(oT_ready, i + 1)
                pr.project_rows(oT, wo, 7, DC).then_inc(c_ps, 1)
                pe.wait_ge(ln2_s.xn_ready, 2 * i + 2)
                pr.transpose_tiles(xn, 4).then_inc(hnT_ps, 1)
                pe.wait_ge(h2T_ready, 2 * i + 2)
                for n in range(MC // 2):
                    for m in range(2 * n, 2 * n + 2):
                        for c in range(DC):
                            mm = nc.tensor.matmul(bank(PS, n, [2, T])[:, m % 2, :],
                                                  wfc[:, c, m * P:(m + 1) * P], h2T[:, c, :],
                                                  start=(c == 0), stop=(c == 1))
                    mm.then_inc(fc_ps, 1)
                pe.wait_ge(act_ready, 8 * i + 8)
                pr.project_rows(act, wproj, 5, MC).then_inc(m_ps, 1)



def stage_l1(pr, x_src, x_dst):
    nc, dram, PS = pr.nc, pr.dram, pr.psum
    HS = 8
    DM, DD, F = 32, 64, 5
    S1 = S + 1
    L = "L1_xattn_"
    with ExitStack() as ctx:
        def sb(name, shape, dt=F32):
            return ctx.enter_context(nc.sbuf_tensor("l1_" + name, shape, dt))

        sems = []

        def sem(name, per):
            s = ctx.enter_context(nc.semaphore("l1_" + name))
            sems.append((s, per))
            return s

        maa_w1 = sb("maa_w1", [P, DC, F * DM])
        maa_w2a = sb("maa_w2a", [P, D])
        maa_w2b = sb("maa_w2b", [DM, D])
        td_w1 = sb("td_w1", [P, DC, DD])
        td_w2 = sb("td_w2", [DD, D])
        wr, wk, wv, wg, wo, wfk, wfr, wfv = (sb(n, [P, DC, D]) for n in (
            "wr", "wk", "wv", "wg", "wo", "wfk", "wfr", "wfv"))
        eps = sb("eps", [P, 1])
        edge = sb("edge", [P, DC, 2, B])
        state0 = sb("state0", [P, DC, HS, B])
        x_in = sb("x_in", [P, NP, D])
        x_res = sb("x_res", [P, NP, D])
        ln = pr.ln_tiles(sb)
        xn = sb("xn", [P, NP, D])
        xa = sb("xa", [P, DC, NB, S1])
        sx = sb("sx", [P, DC, NB, S])
        xx = sb("xx", [P, DC, T])
        th = sb("th", [P, T])
        th4 = sb("th4", [DM, T])
        tf = [sb(f"tf{f}", [P, DC, T]) for f in range(F)]
        xm = [sb(f"xm{f}", [P, DC, T]) for f in range(F)]
        td_t = sb("td_t", [DD, T])
        ew = sb("ew", [P, DC, T])
        w = sb("w", [P, DC, NB, S1])
        kT, rT, vT, gT, sg = (sb(n, [P, DC, T]) for n in ("kT", "rT", "vT", "gT", "sg"))
        ge = sb("ge", [P, DC, T])
        ruk = sb("ruk", [P, DC, T])
        bonus = sb("bonus", [P, DC, T])
        a = sb("a", [P, HS, DC, NB, S1])
        st = sb("st", [P, HS, DC, NB, S1])
        m = sb("m", [P, HS, DC, T])
        og, cen, sq, sd, rstd, yT = (sb(n, [P, DC, T]) for n in (
            "og", "cen", "sq", "sd", "rstd", "yT"))
        x1 = sb("x1", [P, NP, D])
        ln2 = pr.ln_tiles(sb, "2")
        x1n = sb("x1n", [P, NP, D])
        xc = sb("xc", [P, DC, NB, S1])
        sx2 = sb("sx2", [P, DC, NB, S])
        xk2, xr2, rk, kk = (sb(n, [P, DC, T]) for n in ("xk2", "xr2", "rk", "kk"))
        rr = sb("rr", [P, NP, D])
        outt = sb("outt", [P, NP, D])

        weights_in, setup = sem("weights_in", 0), sem("setup", 0)
        x_loaded, res_loaded, stored = (sem(n, 16) for n in ("x_loaded", "res_loaded", "stored"))
        ln_s = pr.ln_sems(sem)
        xnT_ps, xa_ready, edge_ready, sx_ready, xx_ready = (sem(n, per) for n, per in (
            ("xnT_ps", 1), ("xa_ready", 2), ("edge_ready", 1), ("sx_ready", 1), ("xx_ready", 2)))
        w1_ps, th_ready, w2_ps, tf_ready, xm_ready = (sem(n, per) for n, per in (
            ("w1_ps", 1), ("th_ready", 2), ("w2_ps", F), ("tf_ready", 2 * F), ("xm_ready", F)))
        td1_ps, td1_ready, td2_ps, ew_ready, w_ready = (sem(n, 1) for n in (
            "td1_ps", "td1_ready", "td2_ps", "ew_ready", "w_ready"))
        k_ps, k_ready, r_ps, r_ready, v_ps, v_ready, g_ps, g_copied, g_exp, g_den, g_rec, sg_ready = (
            sem(n, 1) for n in ("k_ps", "k_ready", "r_ps", "r_ready", "v_ps", "v_ready", "g_ps",
                                "g_copied", "g_exp", "g_den", "g_rec", "sg_ready"))
        ruk_ready, ruk_ps, bonus_ready = sem("ruk_ready", 2), sem("ruk_ps", 1), sem("bonus_ready", 1)
        st0_ready = sem("st0_ready", 1)
        vrep_ps, a_ready, scan_done, m_ready = (sem(n, HS) for n in (
            "vrep_ps", "a_ready", "scan_done", "m_ready"))
        gat_ps, og_ready, mean_ps, cen_ready, sq_ready, var_ps, sd_ready, rstd_ready, cn_ready = (
            sem(n, 1) for n in ("gat_ps", "og_ready", "mean_ps", "cen_ready", "sq_ready",
                                "var_ps", "sd_ready", "rstd_ready", "cn_ready"))
        gn_ready, y_ready, wo_ps, x1_ready = (sem(n, per) for n, per in (
            ("gn_ready", 2), ("y_ready", 1), ("wo_ps", 1), ("x1_ready", 1)))
        ln2_s = pr.ln_sems(sem, "2")
        xcT_ps, xc_ready, edge2_ready, sx2_ready, xk2_ready, xr2_ready = (sem(n, per) for n, per in (
            ("xcT_ps", 1), ("xc_ready", 2), ("edge2_ready", 1), ("sx2_ready", 1),
            ("xk2_ready", 2), ("xr2_ready", 2)))
        fk_ps, rk_ready, kk_ready, fr_ps, fe_ready, fd_ready, rr_ready, fv_ps, mo_ready, out_ready = (
            sem(n, 1) for n in ("fk_ps", "rk_ready", "kk_ready", "fr_ps", "fe_ready", "fd_ready",
                                "rr_ready", "fv_ps", "mo_ready", "out_ready"))
        start_counts(nc, sems)
        xv, ov = tokens(x_src), tokens(x_dst)

        def both(eng, steps):
            for front, back in steps:
                if front:
                    front(1)
            with eng.Fori(1, TRIPS) as i:
                for front, back in steps:
                    if back:
                        back(i)
                    if front:
                        front(i + 1)
            for front, back in steps:
                if back:
                    back(TRIPS)

        block = ctx.enter_context(nc.Block())

        @block.sync
        def _(sp):
            def load_x(i):
                sp.dma_start(x_in[:], xv[i - 1]).then_inc(x_loaded, 16)

            def load_res(i):
                sp.dma_start(x_res[:], xv[i - 1]).then_inc(res_loaded, 16)

            def store(i):
                sp.wait_ge(out_ready, i + 1)
                sp.dma_start(ov[i - 1], outt[:]).then_inc(stored, 16)

            load_x(1)
            load_res(1)
            for dst, src in (
                    (edge, dram["edgeT"].rearrange("c p (r b) -> p c r b", r=2)),
                    (maa_w1, weight(dram[f"{L}maa_w1"])), (maa_w2a, dram["maa_w2"][0:P, :]),
                    (maa_w2b, dram["maa_w2"][P:P + DM, :]), (td_w1, weight(dram[f"{L}td_w1"])),
                    (td_w2, dram[f"{L}td_w2"]),
                    (state0, dram["state0"].rearrange("p (c j b) -> p c j b", c=DC, j=HS)),
                    (wk, weight(dram[f"{L}Wk"])), (wr, weight(dram[f"{L}Wr"])),
                    (wv, weight(dram[f"{L}Wv"])), (wg, weight(dram[f"{L}Wg"])),
                    (wo, weight(dram[f"{L}Wo"])), (wfk, weight(dram[f"{L}Wfk"])),
                    (wfr, weight(dram[f"{L}Wfr"])), (wfv, weight(dram[f"{L}Wfv"]))):
                sp.dma_start(dst[:], src).then_inc(weights_in, 16)
            sp.wait_ge(ln_s.xn_ready, 4)
            load_x(2)
            with sp.Fori(1, TRIPS - 1) as i:
                sp.wait_ge(ln_s.xn_ready, 2 * i + 4)
                load_x(i + 2)
                sp.wait_ge(x1_ready, i + 1)
                load_res(i + 1)
                store(i)
            sp.wait_ge(x1_ready, TRIPS)
            load_res(TRIPS)
            store(TRIPS - 1)
            store(TRIPS)
            sp.wait_ge(stored, 16 * TRIPS + 16)

        @block.gpsimd
        def _(pool):
            nc.gpsimd.memset(w[:, :, :, 0], 0.0).then_inc(setup, 1)
            pool.wait_ge(weights_in, 16 * 15)
            pool.wait_ge(setup, 2)

            def front_norm(i):
                pr.ln_rstd(pool, ln, ln_s, i)
                pool.wait_ge(sx_ready, i)
                nc.gpsimd.nop(nofuse=True)
                nc.gpsimd.tensor_copy(xa[:, :, :, 0], edge[:, :, 1, bass.ds(NB * (i - 1), NB)]
                                      ).then_inc(edge_ready, 1)

            def mixed(i):
                for f in range(F):
                    pool.wait_ge(tf_ready, 2 * F * i + 2 * f + 2)
                    nc.gpsimd.tensor_tensor(
                        xm[f][:].rearrange("p c (b s) -> p c b s", s=S),
                        tf[f][:].rearrange("p c (b s) -> p c b s", s=S), xa[:, :, :, 1:S1],
                        ALU.add).then_inc(xm_ready, 1)

            def initial(i):
                pool.wait_ge(scan_done, HS * i)
                nc.gpsimd.nop(nofuse=True)
                nc.gpsimd.tensor_copy(
                    a[:, :, :, :, 0],
                    state0[:, :, :, bass.ds(NB * (i - 1), NB)].rearrange("p c j b -> p j c b")
                ).then_inc(st0_ready, 1)

            def read_out(j0):
                def step(i):
                    for j in range(j0, j0 + 4):
                        pool.wait_ge(scan_done, HS * i + j + 1)
                        pool.wait_ge(r_ready, i + 1)
                        nc.gpsimd.tensor_tensor(
                            m[:, j, :, :].rearrange("p c (b s) -> p c b s", s=S),
                            rT[:].rearrange("p c (b s) -> p c b s", s=S), st[:, j, :, :, 0:S],
                            ALU.mult).then_inc(m_ready, 1)
                return step

            def square(i):
                pool.wait_ge(cen_ready, i + 1)
                nc.gpsimd.tensor_tensor(sq[:], cen[:], cen[:], ALU.mult).then_inc(sq_ready, 1)

            def gate(i):
                pool.wait_ge(gn_ready, 2 * i + 2)
                pool.wait_ge(sg_ready, i + 1)
                nc.gpsimd.tensor_tensor(yT[:], og[:], sg[:], ALU.mult).then_inc(y_ready, 1)

            def back_norm(i):
                pr.ln_rstd(pool, ln2, ln2_s, i)
                pool.wait_ge(xr2_ready, 2 * i)
                pool.wait_ge(sx2_ready, i)
                nc.gpsimd.nop(nofuse=True)
                nc.gpsimd.tensor_copy(xc[:, :, :, 0], edge[:, :, 0, bass.ds(NB * (i - 1), NB)]
                                      ).then_inc(edge2_ready, 1)

            def back_shift(i):
                pool.wait_ge(xc_ready, 2 * i + 2)
                pool.wait_ge(edge2_ready, i + 1)
                nc.gpsimd.tensor_tensor(sx2[:], xc[:, :, :, 0:S], xc[:, :, :, 1:S1], ALU.subtract
                                        ).then_inc(sx2_ready, 1)

            def relu_squared(i):
                pool.wait_ge(rk_ready, i + 1)
                nc.gpsimd.tensor_tensor(kk[:], rk[:], rk[:], ALU.mult).then_inc(kk_ready, 1)

            def final(i):
                pool.wait_ge(mo_ready, i + 1)
                pool.wait_ge(stored, 16 * i)
                nc.gpsimd.tensor_tensor(outt[:], rr[:], x1[:], ALU.add).then_inc(out_ready, 1)

            both(pool, [(None, initial), (None, read_out(0)), (front_norm, read_out(4)),
                        (None, square), (mixed, gate), (None, back_norm), (None, back_shift),
                        (None, relu_squared), (None, final)])

        @block.scalar
        def _(act_e):
            act_e.wait_ge(setup, 2)

            def shift_tanh(i):
                act_e.wait_ge(w1_ps, i + 1)
                act_e.wait_ge(w2_ps, F * i)
                nc.scalar.activation(th[:], PS[:, 5, 0:T], ACT.Tanh).then_inc(th_ready, 1)
                nc.scalar.activation(th4[:], PS[0:DM, 5, T:2 * T], ACT.Tanh).then_inc(th_ready, 1)

            def projected1(i):
                act_e.wait_ge(td1_ps, i + 1)
                nc.scalar.activation(td_t[:], PS[0:DD, 4, 0:T], ACT.Tanh).then_inc(td1_ready, 1)
                act_e.wait_ge(k_ps, i + 1)
                act_e.wait_ge(a_ready, HS * i)
                nc.scalar.copy(kT[:], bank(PS, 5, [DC, T])).then_inc(k_ready, 1)

            def projected2(i):
                act_e.wait_ge(r_ps, i + 1)
                act_e.wait_ge(m_ready, HS * i)
                nc.scalar.copy(rT[:], bank(PS, 7, [DC, T])).then_inc(r_ready, 1)
                act_e.wait_ge(td2_ps, i + 1)
                for c in range(DC):
                    ins = nc.scalar.activation(ew[:, c, :], bank(PS, 6, [DC, T])[:, c, :], ACT.Exp,
                                               bias=pr.col(f"{L}time_decay", c))
                ins.then_inc(ew_ready, 1)
                act_e.wait_ge(ew_ready, i + 1)
                act_e.wait_ge(scan_done, HS * i)
                nc.scalar.activation(w[:, :, :, 1:S1], ew[:].rearrange("p c (b s) -> p c b s", s=S),
                                     ACT.Exp, scale=-1.0).then_inc(w_ready, 1)
                act_e.wait_ge(v_ps, i + 1)
                act_e.wait_ge(vrep_ps, HS * i)
                nc.scalar.copy(vT[:], bank(PS, 4, [DC, T])).then_inc(v_ready, 1)

            def gate(i):
                act_e.wait_ge(g_ps, i + 1)
                act_e.wait_ge(sg_ready, i)
                nc.scalar.copy(gT[:], bank(PS, 5, [DC, T])).then_inc(g_copied, 1)
                nc.scalar.activation(ge[:], bank(PS, 5, [DC, T]), ACT.Exp, scale=-1.0
                                     ).then_inc(g_exp, 1)

            def deviation(i):
                act_e.wait_ge(var_ps, i + 1)
                nc.scalar.activation(sd[:], bank(PS, 1, [DC, T]), ACT.Sqrt, scale=1.0 / HS,
                                     bias=eps[:, 0:1]).then_inc(sd_ready, 1)

            def ffn_in(i):
                act_e.wait_ge(fk_ps, i + 1)
                nc.scalar.activation(rk[:], bank(PS, 0, [DC, T]), ACT.Relu).then_inc(rk_ready, 1)
                act_e.wait_ge(fr_ps, i + 1)
                act_e.wait_ge(out_ready, i)
                nc.scalar.activation(rr[:], bank(PS, 1, [NP, D]), ACT.Exp, scale=-1.0
                                     ).then_inc(fe_ready, 1)

            both(act_e, [(shift_tanh, None), (None, deviation), (projected1, None),
                         (projected2, None), (gate, None), (None, ffn_in)])

        @block.vector
        def _(dve):
            nc.vector.memset(eps[:], 1e-5).then_inc(setup, 1)

            def front_norm(i):
                dve.wait_ge(x_loaded, 16 * (i + 1))
                dve.wait_ge(xnT_ps, i)
                pr.ln_normalise(dve, ln, ln_s, x_in, xn, i)

            def shift(i):
                dve.wait_ge(xnT_ps, i + 1)
                dve.wait_ge(xm_ready, F * i)
                for c in range(DC):
                    nc.vector.tensor_scalar(xa[:, c, :, 1:S1], bank(PS, 4, [DC, NB, S])[:, c, :, :],
                                            pr.col(f"{L}ln1_w", c), pr.col(f"{L}ln1_b", c),
                                            ALU.mult, ALU.add).then_inc(xa_ready, 1)
                dve.wait_ge(xa_ready, 2 * i + 2)
                dve.wait_ge(edge_ready, i + 1)
                nc.vector.tensor_tensor(sx[:], xa[:, :, :, 0:S], xa[:, :, :, 1:S1], ALU.subtract
                                        ).then_inc(sx_ready, 1)
                dve.wait_ge(sx_ready, i + 1)
                for c in range(DC):
                    nc.vector.scalar_tensor_tensor(
                        out=xx[:, c, :].rearrange("p (b s) -> p b s", s=S), in0=sx[:, c, :, :],
                        scalar=pr.col(f"{L}maa_x", c), in1=xa[:, c, :, 1:S1],
                        op0=ALU.mult, op1=ALU.add).then_inc(xx_ready, 1)

            def mix(i):
                for f in range(F):
                    dve.wait_ge(w2_ps, F * i + f + 1)
                    for c in range(DC):
                        nc.vector.scalar_tensor_tensor(
                            out=tf[f][:, c, :],
                            in0=bank(PS, (6, 7, 4, 5, 6)[f], [DC, T])[:, c, :],
                            scalar=pr.col(f"{L}maa_stack", 2 * f + c),
                            in1=sx[:, c, :, :].rearrange("p b s -> p (b s)"),
                            op0=ALU.add, op1=ALU.mult).then_inc(tf_ready, 1)

            def gate(i):
                dve.wait_ge(k_ready, i + 1)
                dve.wait_ge(r_ready, i + 1)
                for c in range(DC):
                    nc.vector.scalar_tensor_tensor(
                        out=ruk[:, c, :], in0=rT[:, c, :], scalar=pr.col(f"{L}u", c),
                        in1=kT[:, c, :], op0=ALU.mult, op1=ALU.mult).then_inc(ruk_ready, 1)
                dve.wait_ge(g_exp, i + 1)
                nc.vector.tensor_scalar(ge[:], ge[:], 1.0, None, ALU.add).then_inc(g_den, 1)
                dve.wait_ge(g_den, i + 1)
                nc.vector.reciprocal(ge[:], ge[:]).then_inc(g_rec, 1)
                dve.wait_ge(g_rec, i + 1)
                dve.wait_ge(y_ready, i)
                nc.vector.tensor_tensor(sg[:], gT[:], ge[:], ALU.mult).then_inc(sg_ready, 1)
                dve.wait_ge(ruk_ps, i + 1)
                dve.wait_ge(v_ready, i + 1)
                nc.vector.tensor_tensor(bonus[:], bank(PS, 6, [DC, T]), vT[:], ALU.mult
                                        ).then_inc(bonus_ready, 1)

            def scan(j0):
                def step(i):
                    for j in range(j0, j0 + 4):
                        dve.wait_ge(vrep_ps, HS * i + j + 1)
                        nc.vector.tensor_tensor(
                            a[:, j, :, :, 1:S1], kT[:].rearrange("p c (b s) -> p c b s", s=S),
                            bank(PS, j % 2, [DC, NB, S]), ALU.mult).then_inc(a_ready, 1)
                        dve.wait_ge(a_ready, HS * i + j + 1)
                        dve.wait_ge(st0_ready, i + 1)
                        dve.wait_ge(w_ready, i + 1)
                        dve.wait_ge(m_ready, HS * i)
                        dve.nop(nofuse=True)
                        nc.vector.tensor_tensor_scan(
                            st[:, j, :, :, :].rearrange("p c b s -> p (c b s)"),
                            w[:].rearrange("p c b s -> p (c b s)"),
                            a[:, j, :, :, :].rearrange("p c b s -> p (c b s)"),
                            0.0, ALU.mult, ALU.add).then_inc(scan_done, 1)
                return step

            def mean(i):
                dve.wait_ge(gat_ps, i + 1)
                nc.vector.tensor_tensor(og[:], PS[:, 2:4, 0:T], bonus[:], ALU.add
                                        ).then_inc(og_ready, 1)

            def centre(i):
                dve.wait_ge(mean_ps, i + 1)
                nc.vector.scalar_tensor_tensor(
                    out=cen[:], in0=bank(PS, 0, [DC, T]), scalar=-1.0 / HS, in1=og[:],
                    op0=ALU.mult, op1=ALU.add).then_inc(cen_ready, 1)

            def group_norm(i):
                dve.wait_ge(sd_ready, i + 1)
                nc.vector.reciprocal(rstd[:], sd[:]).then_inc(rstd_ready, 1)
                dve.wait_ge(rstd_ready, i + 1)
                nc.vector.tensor_tensor(cen[:], cen[:], rstd[:], ALU.mult).then_inc(cn_ready, 1)
                dve.wait_ge(cn_ready, i + 1)
                for c in range(DC):
                    nc.vector.tensor_scalar(og[:, c, :], cen[:, c, :], pr.col(f"{L}gn_w", c),
                                            pr.col(f"{L}gn_b", c), ALU.mult, ALU.add
                                            ).then_inc(gn_ready, 1)

            def back_norm(i):
                dve.wait_ge(wo_ps, i + 1)
                dve.wait_ge(res_loaded, 16 * (i + 1))
                dve.wait_ge(out_ready, i)
                nc.vector.tensor_tensor(x1[:], bank(PS, 2, [NP, D]), x_res[:], ALU.add
                                        ).then_inc(x1_ready, 1)
                dve.wait_ge(x1_ready, i + 1)
                dve.wait_ge(xcT_ps, i)
                pr.ln_normalise(dve, ln2, ln2_s, x1, x1n, i)

            def back_shift(i):
                dve.wait_ge(xcT_ps, i + 1)
                for c in range(DC):
                    nc.vector.tensor_scalar(xc[:, c, :, 1:S1], bank(PS, 3, [DC, NB, S])[:, c, :, :],
                                            pr.col(f"{L}ln2_w", c), pr.col(f"{L}ln2_b", c),
                                            ALU.mult, ALU.add).then_inc(xc_ready, 1)
                dve.wait_ge(sx2_ready, i + 1)
                for dst, name, done in ((xk2, "ffn_maa_k", xk2_ready), (xr2, "ffn_maa_r", xr2_ready)):
                    for c in range(DC):
                        nc.vector.scalar_tensor_tensor(
                            out=dst[:, c, :].rearrange("p (b s) -> p b s", s=S),
                            in0=sx2[:, c, :, :], scalar=pr.col(f"{L}{name}", c),
                            in1=xc[:, c, :, 1:S1], op0=ALU.mult, op1=ALU.add).then_inc(done, 1)

            def receptance(i):
                dve.wait_ge(fe_ready, i + 1)
                nc.vector.tensor_scalar(rr[:], rr[:], 1.0, None, ALU.add).then_inc(fd_ready, 1)
                dve.wait_ge(fd_ready, i + 1)
                nc.vector.reciprocal(rr[:], rr[:]).then_inc(rr_ready, 1)
                dve.wait_ge(rr_ready, i + 1)
                dve.wait_ge(fv_ps, i + 1)
                nc.vector.tensor_tensor(rr[:], bank(PS, 2, [NP, D]), rr[:], ALU.mult
                                        ).then_inc(mo_ready, 1)

            both(dve, [(None, scan(0)), (front_norm, scan(4)), (shift, mean), (None, centre),
                       (mix, group_norm), (None, back_norm), (None, back_shift), (gate, None),
                       (None, receptance)])

        @block.tensor
        def _(pe):
            pe.wait_ge(weights_in, 16 * 15)
            pe.wait_ge(setup, 2)

            def front_turn(i):
                pe.wait_ge(v_ready, i)
                pe.wait_ge(ln_s.xn_ready, 2 * i + 2)
                pr.transpose_tiles(xn, 4).then_inc(xnT_ps, 1)

            def shift_in(i):
                pe.wait_ge(g_copied, i)
                pe.wait_ge(g_exp, i)
                pe.wait_ge(xx_ready, 2 * i + 2)
                for c in range(DC):
                    nc.tensor.matmul(PS[:, 5, 0:T], maa_w1[:, c, 0:P], xx[:, c, :],
                                     start=(c == 0), stop=(c == 1))
                for c in range(DC):
                    mm = nc.tensor.matmul(PS[0:DM, 5, T:2 * T], maa_w1[:, c, P:P + DM], xx[:, c, :],
                                          start=(c == 0), stop=(c == 1))
                mm.then_inc(w1_ps, 1)

            def mix(i):
                pe.wait_ge(th_ready, 2 * i + 2)
                pe.wait_ge(bonus_ready, i)
                pe.wait_ge(r_ready, i)
                for f in range(F):
                    rows = slice(DM * f, DM * f + DM) if f < 4 else slice(0, DM)
                    w2, src = (maa_w2a, th) if f < 4 else (maa_w2b, th4)
                    if f == 4:
                        pe.wait_ge(tf_ready, 10 * i + 2)
                    for c in range(DC):
                        mm = nc.tensor.matmul(bank(PS, (6, 7, 4, 5, 6)[f], [DC, T])[:, c, :],
                                              w2[rows, c * P:(c + 1) * P], src[rows, :],
                                              start=True, stop=True)
                    mm.then_inc(w2_ps, 1)

            def projections1(i):
                pe.wait_ge(tf_ready, 10 * i + 6)
                pe.wait_ge(xm_ready, F * i + 2)
                for c in range(DC):
                    mm = nc.tensor.matmul(PS[0:DD, 4, 0:T], td_w1[:, c, :], xm[1][:, c, :],
                                          start=(c == 0), stop=(c == 1))
                mm.then_inc(td1_ps, 1)
                pe.wait_ge(tf_ready, 10 * i + 10)
                pr.project_T(wk, xm[0], 5, DC).then_inc(k_ps, 1)

            def projections2(i):
                pe.wait_ge(xm_ready, F * i + 4)
                pr.project_T(wr, xm[3], 7, DC).then_inc(r_ps, 1)
                pe.wait_ge(td1_ready, i + 1)
                for c in range(DC):
                    mm = nc.tensor.matmul(bank(PS, 6, [DC, T])[:, c, :],
                                          td_w2[:, c * P:(c + 1) * P], td_t[:],
                                          start=True, stop=True)
                mm.then_inc(td2_ps, 1)
                pr.project_T(wv, xm[2], 4, DC).then_inc(v_ps, 1)

            def projections3(i):
                pe.wait_ge(xm_ready, F * i + 5)
                pe.wait_ge(k_ready, i + 1)
                pr.project_T(wg, xm[4], 5, DC).then_inc(g_ps, 1)
                pe.wait_ge(ew_ready, i + 1)
                pe.wait_ge(ruk_ready, 2 * i + 2)
                for c in range(DC):
                    mm = nc.tensor.matmul(bank(PS, 6, [DC, T])[:, c, :], pr.same_head,
                                          ruk[:, c, :], start=True, stop=True)
                mm.then_inc(ruk_ps, 1)

            def spread(i, j):
                for c in range(DC):
                    mm = nc.tensor.matmul(bank(PS, j % 2, [DC, T])[:, c, :], pr.spread[:, j, :],
                                          vT[:, c, :], start=True, stop=True)
                mm.then_inc(vrep_ps, 1)

            def gather(i, j):
                pe.wait_ge(m_ready, HS * i + j + 1)
                for c in range(DC):
                    mm = nc.tensor.matmul(PS[:, 2 + c, 0:T], pr.gather[:, j, :], m[:, j, c, :],
                                          start=(j == 0), stop=(j == HS - 1))
                if j == HS - 1:
                    mm.then_inc(gat_ps, 1)

            def states1(i):
                pe.wait_ge(v_ready, i + 1)
                pe.wait_ge(rk_ready, i)
                pe.wait_ge(fe_ready, i)
                pe.wait_ge(mo_ready, i)
                pe.wait_ge(xc_ready, 2 * i)
                for j in range(4):
                    if j >= 2:
                        pe.wait_ge(a_ready, HS * i + j - 1)
                    spread(i, j)
                gather(i, 0)

            def states2(i):
                for j in range(4, 8):
                    pe.wait_ge(a_ready, HS * i + j - 1)
                    spread(i, j)
                    gather(i, j - 3)

            def states3(i):
                for j in range(5, 8):
                    gather(i, j)

            def mean(i):
                pe.wait_ge(og_ready, i + 1)
                for c in range(DC):
                    mm = nc.tensor.matmul(bank(PS, 0, [DC, T])[:, c, :], pr.same_head,
                                          og[:, c, :], start=True, stop=True)
                mm.then_inc(mean_ps, 1)

            def variance(i):
                pe.wait_ge(sq_ready, i + 1)
                for c in range(DC):
                    mm = nc.tensor.matmul(bank(PS, 1, [DC, T])[:, c, :], pr.same_head,
                                          sq[:, c, :], start=True, stop=True)
                mm.then_inc(var_ps, 1)

            def out_projection(i):
                pe.wait_ge(y_ready, i + 1)
                pr.project_rows(yT, wo, 2, DC).then_inc(wo_ps, 1)

            def back_turn(i):
                pe.wait_ge(ln2_s.xn_ready, 2 * i + 2)
                pr.transpose_tiles(x1n, 3).then_inc(xcT_ps, 1)

            def ffn_in(i):
                pe.wait_ge(xk2_ready, 2 * i + 2)
                pr.project_T(wfk, xk2, 0, DC).then_inc(fk_ps, 1)
                pe.wait_ge(xr2_ready, 2 * i + 2)
                pr.project_rows(xr2, wfr, 1, DC).then_inc(fr_ps, 1)

            def ffn_out(i):
                pe.wait_ge(kk_ready, i + 1)
                pr.project_rows(kk, wfv, 2, DC).then_inc(fv_ps, 1)

            both(pe, [(None, states1), (front_turn, states2), (shift_in, states3), (None, mean),
                      (mix, variance), (projections1, out_projection), (projections2, back_turn),
                      (projections3, ffn_in), (None, ffn_out)])



def stage_cross(pr, x_src, x_dst, tag):
    nc, dram, PS = pr.nc, pr.dram, pr.psum
    H, HD = 16, 128
    SCALE = 1.0 / math.sqrt(HD)
    K1 = S + 1
    L = "L2_xattn_"
    with ExitStack() as ctx:
        def sb(name, shape, dt=F32):
            return ctx.enter_context(nc.sbuf_tensor(f"x{tag}_{name}", shape, dt))

        sems = []

        def sem(name, per):
            s = ctx.enter_context(nc.semaphore(f"x{tag}_{name}"))
            sems.append((s, per))
            return s

        wq, wk, wv = (sb(n, [P, DC, H * HD]) for n in ("wq", "wk", "wv"))
        wo = sb("wo", [P, H, D])
        bv_row = sb("bv_row", [P, H * HD])
        bq_scaled = sb("bq_scaled", [P, H])
        bias_v_diag = sb("bias_v_diag", [P, H, H])
        bias_vo = sb("bias_vo", [H, D])
        x_in = sb("x_in", [P, NP, D])
        x_res = sb("x_res", [P, NP, D])
        ctxT = sb("ctxT", [P, DC, T])
        ln = pr.ln_tiles(sb)
        xn = sb("xn", [P, NP, D])
        hT = sb("hT", [P, DC, T])
        qT = sb("qT", [P, H, T])
        kT = sb("kT", [P, H, NB, K1])
        v = sb("v", [P, NP, H * HD])
        sc = [sb(f"sc{t}", [P, H, K1]) for t in range(NP)]
        pn = [sb(f"pn{t}", [P, H, S]) for t in range(NP)]
        px = sb("px", [P, NP, H])
        mx = sb("mx", [P, NP, H])
        sm = sb("sm", [P, NP, H])
        rs = sb("rs", [P, NP, H])
        pT = [sb(f"pT{t}", [P, H, P]) for t in range(NP)]
        p_extra = sb("p_extra", [H, NP, P])
        oT = sb("oT", [P, H, T])
        xb = sb("xb", [P, NP, D])
        outt = sb("outt", [P, NP, D])

        weights_in, setup, bias_ps = sem("weights_in", 0), sem("setup", 0), sem("bias_ps", 0)
        x_loaded, ctx_loaded, res_loaded = (sem(n, 16) for n in
                                            ("x_loaded", "ctx_loaded", "res_loaded"))
        stored = sem("stored", 16)
        ln_s = pr.ln_sems(sem)
        xnT_ps, hT_ready = sem("xnT_ps", 1), sem("hT_ready", 2)
        k_ps, k_ready, q_ps, q_ready = (sem(n, per) for n, per in (
            ("k_ps", H // 2), ("k_ready", H), ("q_ps", H // 2), ("q_ready", H)))
        v_ps, v_ready = sem("v_ps", 8), sem("v_ready", 8)
        s_ps, s_max, s_sub, s_exp, s_sum, s_rec, p_ready = (sem(n, NP) for n in (
            "s_ps", "s_max", "s_sub", "s_exp", "s_sum", "s_rec", "p_ready"))
        pT_ps, pT_ready = sem("pT_ps", NP), sem("pT_ready", 4 * NP)
        px_ready = sem("px_ready", NP)
        pe_ps, p_extra_ready = sem("pe_ps", 1), sem("p_extra_ready", 1)
        o_ps, o_ready = sem("o_ps", 8), sem("o_ready", 8)
        y_ps, xb_ready, out_ready = sem("y_ps", 1), sem("xb_ready", 1), sem("out_ready", 1)
        start_counts(nc, sems)
        xv, ov = tokens(x_src), tokens(x_dst)
        cv = dram["ctxT"].rearrange("(c p) (g t) -> g p c t", p=P, t=T)

        block = ctx.enter_context(nc.Block())

        @block.sync
        def _(sp):
            def load_ctx(i):
                sp.dma_start(ctxT[:], cv[i - 1]).then_inc(ctx_loaded, 16)

            def store(i):
                sp.wait_ge(out_ready, i + 1)
                sp.dma_start(ov[i - 1], outt[:]).then_inc(stored, 16)

            load_ctx(1)
            sp.dma_start(wk[:], weight(dram[f"{L}wk{tag}"])).then_inc(weights_in, 16)
            sp.dma_start(x_in[:], xv[0]).then_inc(x_loaded, 16)
            sp.dma_start(wq[:], weight(dram[f"{L}wq{tag}"])).then_inc(weights_in, 16)
            sp.dma_start(wv[:], weight(dram[f"{L}wv{tag}"])).then_inc(weights_in, 16)
            sp.dma_start(bv_row[:], dram[f"{L}bv{tag}"][0, :].partition_broadcast(P)
                         ).then_inc(weights_in, 16)
            sp.dma_start(x_res[:], xv[0]).then_inc(res_loaded, 16)
            sp.dma_start(wo[:], weight(dram[f"{L}wo{tag}"])).then_inc(weights_in, 16)
            with sp.Fori(1, TRIPS) as i:
                sp.wait_ge(ln_s.xn_ready, 2 * i + 2)
                sp.dma_start(x_in[:], xv[i]).then_inc(x_loaded, 16)
                sp.wait_ge(v_ps, 8 * i + 8)
                load_ctx(i + 1)
                sp.wait_ge(xb_ready, i + 1)
                sp.dma_start(x_res[:], xv[i]).then_inc(res_loaded, 16)
                store(i)
            store(TRIPS)
            sp.wait_ge(stored, 16 * TRIPS + 16)

        @block.gpsimd
        def _(pool):
            nc.gpsimd.memset(pT[0][:], 0.0).then_inc(setup, 1)
            nc.gpsimd.memset(pT[1][:], 0.0).then_inc(setup, 1)
            with pool.Fori(1, TRIPS + 1) as i:
                pr.ln_rstd(pool, ln, ln_s, i)
                pool.wait_ge(res_loaded, 16 * (i + 1))
                pool.wait_ge(out_ready, i)
                nc.gpsimd.tensor_tensor(xb[:], x_res[:], pr.row(f"{L}bo{tag}", NP), ALU.add
                                        ).then_inc(xb_ready, 1)
                for t in range(NP):
                    pool.wait_ge(s_rec, 2 * i + t + 1)
                    pool.wait_ge(pT_ps, 2 * i + t)
                    nc.gpsimd.tensor_tensor(pn[t][:], sc[t][:, :, 0:S],
                                            rs[:, t, :].unsqueeze(2).to_broadcast([P, H, S]),
                                            ALU.mult).then_inc(p_ready, 1)
                    pool.wait_ge(pe_ps, i)
                    nc.gpsimd.tensor_tensor(px[:, t, :], sc[t][:, :, S], rs[:, t, :], ALU.mult
                                            ).then_inc(px_ready, 1)

        @block.scalar
        def _(act_e):
            act_e.wait_ge(setup, 6)
            with act_e.Fori(1, TRIPS + 1) as i:
                for h in range(H):
                    act_e.wait_ge(k_ps, 8 * i + h // 2 + 1)
                    nc.scalar.activation(kT[:, h, :, 0:S],
                                         bank(PS, 4 + h // 2 % 4, [2, NB, S])[:, h % 2, :, :],
                                         ACT.Identity, bias=pr.col(f"{L}bk{tag}", h)
                                         ).then_inc(k_ready, 1)
                for h in range(H):
                    act_e.wait_ge(q_ps, 8 * i + h // 2 + 1)
                    nc.scalar.activation(qT[:, h, :], bank(PS, 4 + h // 2 % 4, [2, T])[:, h % 2, :],
                                         ACT.Identity, bias=bq_scaled[:, h:h + 1], scale=SCALE
                                         ).then_inc(q_ready, 1)
                for t in range(NP):
                    act_e.wait_ge(s_sub, 2 * i + t + 1)
                    nc.scalar.activation(sc[t][:], sc[t][:], ACT.Exp).then_inc(s_exp, 1)
                for n in range(2 * 4):
                    act_e.wait_ge(o_ps, 8 * i + n + 1)
                    t, h = n // 4, n % 4 * 4
                    nc.scalar.copy(oT[:, h:h + 4, t * P:(t + 1) * P],
                                   bank(PS, 5 + n % 3, [4, P])).then_inc(o_ready, 1)

        @block.vector
        def _(dve):
            nc.vector.tensor_scalar(bq_scaled[:], pr.cols_of(f"{L}bq{tag}"), SCALE, None, ALU.mult
                                    ).then_inc(setup, 1)
            nc.vector.tensor_copy(kT[:, :, :, S], pr.cols_of(f"{L}bias_k{tag}").unsqueeze(2)
                                  .to_broadcast([P, H, NB])).then_inc(setup, 1)
            nc.vector.memset(bias_v_diag[:], 0.0).then_inc(setup, 1)
            dve.wait_ge(setup, 5)
            nc.vector.tensor_copy(bias_v_diag[:].rearrange("p a b -> p (a b)")[:, 0:H * H:H + 1],
                                  pr.cols_of(f"{L}bias_v{tag}")).then_inc(setup, 1)
            dve.wait_ge(bias_ps, 1)
            nc.vector.tensor_copy(bias_vo[:], PS[0:H, 0, 0:D]).then_inc(setup, 1)
            with dve.Fori(1, TRIPS + 1) as i:
                dve.wait_ge(x_loaded, 16 * (i + 1))
                dve.wait_ge(xnT_ps, i)
                pr.ln_normalise(dve, ln, ln_s, x_in, xn, i)
                dve.wait_ge(xnT_ps, i + 1)
                for c in range(DC):
                    nc.vector.tensor_scalar(hT[:, c, :], bank(PS, 0, [DC, T])[:, c, :],
                                            pr.col(f"{L}ln{tag}_scale", c),
                                            pr.col(f"{L}ln{tag}_offset", c),
                                            ALU.mult, ALU.add).then_inc(hT_ready, 1)

                def softmax_in(t):
                    dve.wait_ge(s_ps, 2 * i + t + 1)
                    ps = PS[:, 0:4, 0:4 * K1].rearrange("p r (h k) -> p r h k", k=K1)
                    nc.vector.tensor_reduce(mx[:, t, :].rearrange("p (r h) -> p r h", r=4), ps,
                                            AX.X, ALU.max).then_inc(s_max, 1)
                    dve.wait_ge(s_max, 2 * i + t + 1)
                    nc.vector.tensor_tensor(
                        sc[t][:].rearrange("p (r h) k -> p r h k", r=4), ps,
                        mx[:, t, :].rearrange("p (r h) -> p r h", r=4).unsqueeze(3)
                        .to_broadcast([P, 4, 4, K1]), ALU.subtract).then_inc(s_sub, 1)

                def softmax_sum(t):
                    dve.wait_ge(s_exp, 2 * i + t + 1)
                    nc.vector.tensor_reduce(sm[:, t, :], sc[t][:], AX.X, ALU.add
                                            ).then_inc(s_sum, 1)
                    dve.wait_ge(s_sum, 2 * i + t + 1)
                    nc.vector.reciprocal(rs[:, t, :], sm[:, t, :]).then_inc(s_rec, 1)

                def values(t):
                    for n in range(4):
                        dve.wait_ge(v_ps, 8 * i + 4 * t + n + 1)
                        cols = slice(512 * n, 512 * n + 512)
                        nc.vector.tensor_tensor(v[:, t, cols], PS[:, 4 + n, :], bv_row[:, cols],
                                                ALU.add).then_inc(v_ready, 1)

                softmax_in(0)
                values(0)
                softmax_sum(0)
                softmax_in(1)
                values(1)
                softmax_sum(1)
                for t in range(NP):
                    dve.wait_ge(pT_ps, 2 * i + t + 1)
                    for hh in range(2):
                        for b2 in range(2):
                            src = slice(64 * hh, 64 * hh + 64)
                            dst = slice(64 * b2, 64 * b2 + 64)
                            nc.vector.tensor_copy(
                                pT[t][dst, hh:H:2, dst].rearrange("p (a n) q -> p a n q", a=2),
                                PS[src, 2 * t:2 * t + 2, :].rearrange(
                                    "p a (n q) -> p a n q", q=P)[:, :, :, dst]
                            ).then_inc(pT_ready, 1)
                dve.wait_ge(pe_ps, i + 1)
                nc.vector.tensor_copy(p_extra[:], bank(PS, 4, [4, P])[0:H, 0:NP, :]
                                      ).then_inc(p_extra_ready, 1)
                dve.wait_ge(y_ps, i + 1)
                dve.wait_ge(xb_ready, i + 1)
                dve.wait_ge(stored, 16 * i)
                nc.vector.tensor_tensor(outt[:], bank(PS, 4, [NP, D]), xb[:], ALU.add
                                        ).then_inc(out_ready, 1)

        @block.tensor
        def _(pe):
            pe.wait_ge(weights_in, 16 * 5)
            pe.wait_ge(setup, 6)
            for h in range(H):
                mm = nc.tensor.matmul(PS[0:H, 0, 0:D], bias_v_diag[:, h, :], wo[:, h, :],
                                      start=(h == 0), stop=(h == H - 1))
            mm.then_inc(bias_ps, 1)
            pe.wait_ge(setup, 7)

            def project(w, xT, u):
                for h in range(2 * u, 2 * u + 2):
                    for c in range(DC):
                        mm = nc.tensor.matmul(bank(PS, 4 + u % 4, [2, T])[:, h % 2, :],
                                              w[:, c, h * HD:(h + 1) * HD], xT[:, c, :],
                                              start=(c == 0), stop=(c == 1))
                return mm

            with pe.Fori(1, TRIPS + 1) as i:
                pe.wait_ge(o_ready, 8 * i)
                pe.wait_ge(out_ready, i)
                pe.wait_ge(ctx_loaded, 16 * (i + 1))
                for u in range(8):
                    if u >= 4:
                        pe.wait_ge(k_ready, 16 * i + 2 * (u - 3))
                    if u == 6:
                        pe.wait_ge(pT_ready, 8 * i)
                        pe.wait_ge(ln_s.xn_ready, 2 * i + 2)
                        pr.transpose_tiles(xn, 0).then_inc(xnT_ps, 1)
                    project(wk, ctxT, u).then_inc(k_ps, 1)
                pe.wait_ge(hT_ready, 2 * i + 2)
                for u in range(8):
                    if u < 4:
                        pe.wait_ge(k_ready, 16 * i + 2 * (u + 5))
                    else:
                        pe.wait_ge(q_ready, 16 * i + 2 * (u - 3))
                    project(wq, hT, u).then_inc(q_ps, 1)

                def scores(t):
                    for h in range(H):
                        for b2 in range(2):
                            b = 2 * t + b2
                            mm = nc.tensor.matmul(
                                PS[64 * b2:64 * b2 + 64, h // 4, h % 4 * K1:(h % 4 + 1) * K1],
                                qT[:, h, b * S:(b + 1) * S], kT[:, h, b, :],
                                start=True, stop=True)
                    mm.then_inc(s_ps, 1)

                def values(t):
                    for n in range(4):
                        if t == 1:
                            pe.wait_ge(v_ready, 8 * i + n + 1)
                        for c in range(DC):
                            mm = nc.tensor.matmul(PS[:, 4 + n, :], ctxT[:, c, t * P:(t + 1) * P],
                                                  wv[:, c, 512 * n:512 * n + 512],
                                                  start=(c == 0), stop=(c == 1))
                        mm.then_inc(v_ps, 1)

                pe.wait_ge(q_ready, 16 * i + 16)
                scores(0)
                values(0)
                pe.wait_ge(s_sub, 2 * i + 1)
                scores(1)
                values(1)
                pe.wait_ge(s_sub, 2 * i + 2)
                for t in range(NP):
                    pe.wait_ge(p_ready, 2 * i + t + 1)
                    for n in range(H // 2):
                        mm = nc.tensor.transpose(bank(PS, 2 * t + n // 4, [4, P])[:, n % 4, :],
                                                 pn[t][:, 2 * n:2 * n + 2, :].rearrange(
                                                     "p h k -> p (h k)"), pr.ident)
                    mm.then_inc(pT_ps, 1)
                pe.wait_ge(v_ready, 8 * i + 8)
                pe.wait_ge(px_ready, 2 * i + 2)
                for t in range(NP):
                    mm = nc.tensor.transpose(bank(PS, 4, [4, P])[0:H, t, :], px[:, t, :],
                                             pr.ident)
                mm.then_inc(pe_ps, 1)
                for n in range(8):
                    t = n // 4
                    pe.wait_ge(pT_ready, 8 * i + 4 * t + 4)
                    if n >= 3:
                        pe.wait_ge(o_ready, 8 * i + n - 2)
                    for h in range(n % 4 * 4, n % 4 * 4 + 4):
                        mm = nc.tensor.matmul(bank(PS, 5 + n % 3, [4, P])[:, h % 4, :],
                                              v[:, t, h * HD:(h + 1) * HD], pT[t][:, h, :],
                                              start=True, stop=True)
                    mm.then_inc(o_ps, 1)
                pe.wait_ge(p_extra_ready, i + 1)
                pe.wait_ge(o_ready, 8 * i + 8)
                for t in range(NP):
                    y = bank(PS, 4, [NP, D])[:, t, :]
                    for h in range(H):
                        nc.tensor.matmul(y, oT[:, h, t * P:(t + 1) * P], wo[:, h, :],
                                         start=(h == 0), stop=False)
                    mm = nc.tensor.matmul(y, p_extra[:, t, :], bias_vo[:], start=False, stop=True)
                mm.then_inc(y_ps, 1)


def stage_cross1(pr, x_src, x_dst):
    stage_cross(pr, x_src, x_dst, 1)


def stage_cross2(pr, x_src, x_dst):
    stage_cross(pr, x_src, x_dst, 2)



def stage_l3(pr, x_src, x_dst):
    nc, dram, PS = pr.nc, pr.dram, pr.psum
    H, KVH, HD = 32, 8, 8
    G = H // KVH
    SCALE = 1.0 / math.sqrt(HD)
    RG = 4
    L, M = "L3_xattn_", "L2_xattn_"
    with ExitStack() as ctx:
        def sb(name, shape, dt=F32):
            return ctx.enter_context(nc.sbuf_tensor("l3_" + name, shape, dt))

        sems = []

        def sem(name, per):
            s = ctx.enter_context(nc.semaphore("l3_" + name))
            sems.append((s, per))
            return s

        wfc = sb("wfc", [P, DC, INNER])
        wproj = sb("wproj", [P, MC, D])
        wq, wk, wo = (sb(n, [P, DC, D]) for n in ("wq", "wk", "wo"))
        wv = sb("wv", [P, DC, KVH * HD])
        bq_scaled = sb("bq_scaled", [P, DC])
        x_in = sb("x_in", [P, NP, D])
        x_res = sb("x_res", [P, NP, D])
        ctxT = sb("ctxT", [P, DC, NB, 2, S])
        mask = sb("mask", [P, NP, S])
        ln = pr.ln_tiles(sb)
        xn = sb("xn", [P, NP, D])
        hT = sb("hT", [P, DC, T])
        act = sb("act", [P, MC, T])
        xb = sb("xb", [P, NP, D])
        x3 = sb("x3", [P, NP, D])
        x3b = sb("x3b", [P, NP, D])
        x3T = sb("x3T", [P, DC, T])
        qT = sb("qT", [P, DC, T])
        k_blk = sb("k_blk", [P, DC, NB, G, S])
        v_blk = sb("v_blk", [P, NB, KVH, 2, G, HD])
        sc = [sb(f"sc{t}", [P, H, S]) for t in range(NP)]
        mx, sm, rs = (sb(n, [P, NP, H]) for n in ("mx", "sm", "rs"))
        pT = [sb(f"pT{t}", [P, H // 2, P]) for t in range(NP)]
        oT = sb("oT", [P, DC, T])
        y = sb("y", [P, NP, D])
        lnf = pr.ln_tiles(sb, "f")
        yn = sb("yn", [P, NP, D])
        outt = sb("outt", [P, NP, D])

        weights_in, setup = sem("weights_in", 0), sem("setup", 0)
        x_loaded, res_loaded, ctx_loaded, mask_loaded = (
            sem("x_loaded", 16), sem("res_loaded", 16), sem("ctx_loaded", 64),
            sem("mask_loaded", 16))
        stored = sem("stored", 16)
        ln_s = pr.ln_sems(sem)
        xnT_ps, hT_ready = sem("xnT_ps", 1), sem("hT_ready", 2)
        fc_ps, act_ready, m_ps = sem("fc_ps", 4), sem("act_ready", MC), sem("m_ps", 1)
        xb_ready, x3_ready = sem("xb_ready", 1), sem("x3_ready", 1)
        x3T_ps, x3T_ready, x3b_ready = sem("x3T_ps", 1), sem("x3T_ready", 1), sem("x3b_ready", 1)
        q_ps, qT_ready = sem("q_ps", 1), sem("qT_ready", 2)
        k_ps, k_ready, v_ps, v_ready = (sem("k_ps", 1), sem("k_ready", 8), sem("v_ps", 1),
                                        sem("v_ready", 4))
        s_ps, s_masked, s_max, s_sub, s_exp, s_sum, s_rec, p_ready = (sem(n, NP) for n in (
            "s_ps", "s_masked", "s_max", "s_sub", "s_exp", "s_sum", "s_rec", "p_ready"))
        pT_ps, pT_ready = sem("pT_ps", NP), sem("pT_ready", NP)
        o_ps, oT_ready, y_ps, y_ready = (sem(n, 1) for n in ("o_ps", "oT_ready", "y_ps", "y_ready"))
        lnf_s = pr.ln_sems(sem, "f")
        gamma_done, out_ready = sem("gamma_done", 1), sem("out_ready", 1)
        start_counts(nc, sems)
        xv, ov = tokens(x_src), tokens(x_dst)
        cv = dram["ctxT"].rearrange("(c p) (g b s) -> g c p b s", p=P, b=NB, s=S)
        mv = dram["mask"].rearrange("(g t p) s -> g p t s", t=NP, p=P)

        def both(eng, steps):
            for mlp, _ in steps:
                if mlp:
                    mlp(1)
            with eng.Fori(1, TRIPS) as i:
                for mlp, att in steps:
                    if att:
                        att(i)
                    if mlp:
                        mlp(i + 1)
            for _, att in steps:
                if att:
                    att(TRIPS)

        block = ctx.enter_context(nc.Block())

        @block.sync
        def _(sp):
            def load_x(i):
                sp.dma_start(x_in[:], xv[i - 1]).then_inc(x_loaded, 16)

            def load_res(i):
                sp.dma_start(x_res[:], xv[i - 1]).then_inc(res_loaded, 16)

            def load_ctx(i):
                for c in range(DC):
                    for u in range(2):
                        sp.dma_start(ctxT[:, c, :, u, :], cv[i - 1, c]).then_inc(ctx_loaded, 16)

            def load_mask(i):
                sp.dma_start(mask[:], mv[i - 1]).then_inc(mask_loaded, 16)

            def store(i):
                sp.wait_ge(out_ready, i + 1)
                sp.dma_start(ov[i - 1], outt[:]).then_inc(stored, 16)

            load_x(1)
            load_res(1)
            for dst, name in ((wfc, f"{M}w_fc1"), (wproj, f"{M}w_fc2"), (wk, f"{L}Wk_rep"),
                              (wq, f"{L}Wq"), (wv, f"{L}Wv"), (wo, f"{L}Wo")):
                sp.dma_start(dst[:], weight(dram[name])).then_inc(weights_in, 16)
            load_ctx(1)
            load_mask(1)
            sp.wait_ge(ln_s.xn_ready, 4)
            load_x(2)
            sp.wait_ge(xb_ready, 2)
            load_res(2)
            with sp.Fori(1, TRIPS - 1) as i:
                sp.wait_ge(v_ps, i + 1)
                load_ctx(i + 1)
                sp.wait_ge(ln_s.xn_ready, 2 * i + 4)
                load_x(i + 2)
                sp.wait_ge(s_masked, 2 * i + 2)
                load_mask(i + 1)
                sp.wait_ge(xb_ready, i + 2)
                load_res(i + 2)
                store(i)
            sp.wait_ge(v_ps, TRIPS)
            load_ctx(TRIPS)
            sp.wait_ge(s_masked, 2 * TRIPS)
            load_mask(TRIPS)
            store(TRIPS - 1)
            store(TRIPS)
            sp.wait_ge(stored, 16 * TRIPS + 16)

        @block.gpsimd
        def _(pool):
            nc.gpsimd.memset(v_blk[:], 0.0).then_inc(setup, 1)

            def mlp_rstd(i):
                pr.ln_rstd(pool, ln, ln_s, i)

            def mlp_residual(i):
                pool.wait_ge(res_loaded, 16 * (i + 1))
                pool.wait_ge(x3_ready, i)
                nc.gpsimd.tensor_tensor(xb[:], x_res[:], pr.row(f"{M}b_fc2", NP), ALU.add
                                        ).then_inc(xb_ready, 1)

            def residual(i):
                pool.wait_ge(x3_ready, i + 1)
                pool.wait_ge(y_ready, i)
                nc.gpsimd.tensor_tensor(x3b[:], x3[:], pr.row(f"{L}bo", NP), ALU.add
                                        ).then_inc(x3b_ready, 1)

            def normalise(t):
                def step(i):
                    pool.wait_ge(s_rec, 2 * i + t + 1)
                    nc.gpsimd.tensor_tensor(sc[t][:], sc[t][:],
                                            rs[:, t, :].unsqueeze(2).to_broadcast([P, H, S]),
                                            ALU.mult).then_inc(p_ready, 1)
                return step

            def final(i):
                pr.ln_rstd(pool, lnf, lnf_s, i)
                pool.wait_ge(lnf_s.xn_ready, 2 * i + 2)
                nc.gpsimd.tensor_tensor(yn[:], yn[:], pr.row(f"{L}gamma", NP), ALU.mult
                                        ).then_inc(gamma_done, 1)
                pool.wait_ge(stored, 16 * i)
                pool.wait_ge(gamma_done, i + 1)
                nc.gpsimd.tensor_tensor(outt[:], yn[:], pr.row(f"{L}beta", NP), ALU.add
                                        ).then_inc(out_ready, 1)

            both(pool, [(None, residual), (mlp_rstd, None), (None, normalise(0)),
                        (mlp_residual, normalise(1)), (None, final)])

        @block.scalar
        def _(act_e):
            act_e.wait_ge(setup, 2)

            def x_transposed(i):
                act_e.wait_ge(x3T_ps, i + 1)
                nc.scalar.copy(x3T[:], bank(PS, 4, [DC, T])).then_inc(x3T_ready, 1)

            def queries(i):
                act_e.wait_ge(q_ps, i + 1)
                for c in range(DC):
                    nc.scalar.activation(qT[:, c, :], bank(PS, 4, [2, T])[:, c, :], ACT.Identity,
                                         bias=bq_scaled[:, c:c + 1], scale=SCALE
                                         ).then_inc(qT_ready, 1)

            def exps(t):
                def step(i):
                    act_e.wait_ge(s_sub, 2 * i + t + 1)
                    nc.scalar.activation(sc[t][:], sc[t][:], ACT.Exp).then_inc(s_exp, 1)
                return step

            def turned(t):
                def step(i):
                    act_e.wait_ge(pT_ps, 2 * i + t + 1)
                    nc.scalar.copy(pT[t][:].rearrange("p (a b) q -> p a (b q)", a=4),
                                   PS[:, 0:4, :]).then_inc(pT_ready, 1)
                return step

            def attended(i):
                act_e.wait_ge(o_ps, i + 1)
                nc.scalar.copy(oT[:], bank(PS, 4, [DC, T])).then_inc(oT_ready, 1)

            def gelu(i):
                for m in range(MC):
                    act_e.wait_ge(fc_ps, 4 * i + m // 2 + 1)
                    nc.scalar.activation(act[:, m, :],
                                         bank(PS, 7 - m // 2 % 2, [2, T])[:, m % 2, :],
                                         ACT.Gelu, bias=pr.col(f"{M}b_fc1", m)
                                         ).then_inc(act_ready, 1)

            both(act_e, [(None, x_transposed), (None, queries), (None, exps(0)), (gelu, exps(1)),
                         (None, turned(0)), (None, turned(1)), (None, attended)])

        @block.vector
        def _(dve):
            nc.vector.tensor_scalar(bq_scaled[:], pr.cols_of(f"{L}bq"), SCALE, None, ALU.mult
                                    ).then_inc(setup, 1)
            dve.wait_ge(setup, 2)

            def mlp_norm(i):
                dve.wait_ge(x_loaded, 16 * (i + 1))
                dve.wait_ge(xnT_ps, i)
                pr.ln_normalise(dve, ln, ln_s, x_in, xn, i)

            def mlp_weighted(i):
                dve.wait_ge(xnT_ps, i + 1)
                for c in range(DC):
                    nc.vector.tensor_scalar(hT[:, c, :], bank(PS, 6, [DC, T])[:, c, :],
                                            pr.col(f"{M}ln_mlp_scale", c),
                                            pr.col(f"{M}ln_mlp_offset", c),
                                            ALU.mult, ALU.add).then_inc(hT_ready, 1)

            def mlp_out(i):
                dve.wait_ge(m_ps, i + 1)
                dve.wait_ge(xb_ready, i + 1)
                dve.wait_ge(x3T_ps, i)
                dve.wait_ge(x3b_ready, i)
                nc.vector.tensor_tensor(x3[:], bank(PS, 7, [NP, D]), xb[:], ALU.add
                                        ).then_inc(x3_ready, 1)

            def keys(i):
                dve.wait_ge(k_ps, i + 1)
                for c in range(DC):
                    for g in range(G):
                        nc.vector.tensor_scalar(
                            k_blk[:, c, :, g, :], bank(PS, 5, [DC, NB, S])[:, c, :, :],
                            pr.col("L3_xattn_bk_rep", c), pr.head4[:, g:g + 1], ALU.add, ALU.mult
                        ).then_inc(k_ready, 1)

            def values(i):
                dve.wait_ge(v_ps, i + 1)
                for gp in range(2):
                    for hh in range(2):
                        half = slice(64 * hh, 64 * hh + 64)
                        bias = pr.rowv("L3_xattn_bv")[half, :].unsqueeze(1).to_broadcast(
                            [64, NB, KVH * HD]).rearrange("p b (h e) -> p b h e", e=HD)
                        nc.vector.tensor_tensor(
                            v_blk[half, :, :, gp, 2 * gp + hh, :],
                            bank(PS, 5, [8, KVH, HD])[half, 0:NB, :, :], bias, ALU.add
                        ).then_inc(v_ready, 1)

            def softmax_in(t):
                def step(i):
                    dve.wait_ge(mask_loaded, 16 * (i + 1))
                    dve.wait_ge(s_ps, 2 * i + t + 1)
                    nc.vector.tensor_tensor(
                        sc[t][:].rearrange("p (r h) k -> p r h k", r=RG),
                        PS[:, 0:RG, :].rearrange("p r (h k) -> p r h k", k=S),
                        mask[:, t, :].unsqueeze(1).unsqueeze(1).to_broadcast([P, RG, H // RG, S]),
                        ALU.add).then_inc(s_masked, 1)
                    dve.wait_ge(s_masked, 2 * i + t + 1)
                    nc.vector.tensor_reduce(mx[:, t, :], sc[t][:], AX.X, ALU.max
                                            ).then_inc(s_max, 1)
                    dve.wait_ge(s_max, 2 * i + t + 1)
                    nc.vector.tensor_tensor(sc[t][:], sc[t][:],
                                            mx[:, t, :].unsqueeze(2).to_broadcast([P, H, S]),
                                            ALU.subtract).then_inc(s_sub, 1)
                return step

            def softmax_sum(t):
                def step(i):
                    dve.wait_ge(s_exp, 2 * i + t + 1)
                    nc.vector.tensor_reduce(sm[:, t, :], sc[t][:], AX.X, ALU.add
                                            ).then_inc(s_sum, 1)
                    dve.wait_ge(s_sum, 2 * i + t + 1)
                    nc.vector.reciprocal(rs[:, t, :], sm[:, t, :]).then_inc(s_rec, 1)
                return step

            def final(i):
                dve.wait_ge(y_ps, i + 1)
                dve.wait_ge(x3b_ready, i + 1)
                nc.vector.tensor_tensor(y[:], bank(PS, 5, [NP, D]), x3b[:], ALU.add
                                        ).then_inc(y_ready, 1)
                dve.wait_ge(y_ready, i + 1)
                dve.wait_ge(out_ready, i)
                pr.ln_normalise(dve, lnf, lnf_s, y, yn, i, eps=1e-6)

            both(dve, [(None, keys), (mlp_norm, values), (mlp_weighted, softmax_in(0)),
                       (None, softmax_in(1)), (None, softmax_sum(0)), (None, softmax_sum(1)),
                       (mlp_out, None), (None, final)])

        @block.tensor
        def _(pe):
            pe.wait_ge(weights_in, 16 * 6)
            pe.wait_ge(setup, 2)

            def mlp_turn(i):
                pe.wait_ge(act_ready, 8 * i)
                pe.wait_ge(ln_s.xn_ready, 2 * i + 2)
                pr.transpose_tiles(xn, 6).then_inc(xnT_ps, 1)

            def mlp_up(i):
                pe.wait_ge(x3_ready, i)
                pe.wait_ge(hT_ready, 2 * i + 2)
                for u in range(MC // 2):
                    if u >= 2:
                        pe.wait_ge(act_ready, 8 * i + 2 * (u - 1))
                    for m in range(2 * u, 2 * u + 2):
                        for c in range(DC):
                            mm = nc.tensor.matmul(bank(PS, 7 - u % 2, [2, T])[:, m % 2, :],
                                                  wfc[:, c, m * P:(m + 1) * P], hT[:, c, :],
                                                  start=(c == 0), stop=(c == 1))
                    mm.then_inc(fc_ps, 1)

            def mlp_down(i):
                pe.wait_ge(act_ready, 8 * i + 8)
                pr.project_rows(act, wproj, 7, MC).then_inc(m_ps, 1)

            def keys(i):
                pe.wait_ge(y_ready, i)
                pe.wait_ge(ctx_loaded, 64 * (i + 1))
                pr.project_T(wk, ctxT[:, :, :, 0, :], 5, DC).then_inc(k_ps, 1)
                pe.wait_ge(oT_ready, i)
                pe.wait_ge(x3_ready, i + 1)
                pr.transpose_tiles(x3, 4).then_inc(x3T_ps, 1)

            def queries(i):
                pe.wait_ge(x3T_ready, i + 1)
                pr.project_T(wq, x3T, 4, DC).then_inc(q_ps, 1)
                pe.wait_ge(k_ready, 8 * i + 8)
                for b in range(NB):
                    for c in range(DC):
                        mm = nc.tensor.matmul(bank(PS, 5, [8, S])[:, b, :],
                                              ctxT[:, c, b, :, :].rearrange("p u s -> p (u s)"),
                                              wv[:, c, :], start=(c == 0), stop=(c == 1))
                mm.then_inc(v_ps, 1)

            def scores(t):
                def step(i):
                    if t == 0:
                        pe.wait_ge(qT_ready, 2 * i + 2)
                        pe.wait_ge(pT_ready, 2 * i)
                    else:
                        pe.wait_ge(s_masked, 2 * i + 1)
                    for r in range(RG):
                        rows = slice(32 * r, 32 * r + 32)
                        for c in range(DC):
                            for b2 in range(2):
                                b = 2 * t + b2
                                mm = nc.tensor.matmul(
                                    bank(PS, r, [2, T])[64 * b2:64 * b2 + 64, c, :],
                                    qT[rows, c, b * S:(b + 1) * S],
                                    k_blk[rows, c, b, :, :], start=True, stop=True)
                    mm.then_inc(s_ps, 1)
                return step

            def turn(t):
                def step(i):
                    if t == 0:
                        pe.wait_ge(s_masked, 2 * i + 2)
                    else:
                        pe.wait_ge(pT_ready, 2 * i + 1)
                    pe.wait_ge(p_ready, 2 * i + t + 1)
                    for n in range(H // 2):
                        mm = nc.tensor.transpose(
                            bank(PS, n // 4, [4, P])[:, n % 4, :],
                            sc[t][:, 2 * n:2 * n + 2, :].rearrange("p h k -> p (h k)"), pr.ident)
                    mm.then_inc(pT_ps, 1)
                return step

            def attend(i):
                pe.wait_ge(v_ready, 4 * i + 4)
                for t in range(NP):
                    pe.wait_ge(pT_ready, 2 * i + t + 1)
                    for c in range(DC):
                        for r in range(RG):
                            for b2 in range(2):
                                b = 2 * t + b2
                                for gp in range(2):
                                    mm = nc.tensor.matmul(
                                        bank(PS, 4, [DC, T])[32 * r:32 * r + 32, c,
                                                             b * S:(b + 1) * S],
                                        v_blk[:, b, c * RG + r, gp, :, :].rearrange(
                                            "p g e -> p (g e)"),
                                        pT[t][:, 4 * r + 2 * c + gp, b2 * S:(b2 + 1) * S],
                                        start=(gp == 0), stop=(gp == 1))
                mm.then_inc(o_ps, 1)

            def output(i):
                pe.wait_ge(oT_ready, i + 1)
                pr.project_rows(oT, wo, 5, DC).then_inc(y_ps, 1)

            both(pe, [(None, keys), (None, queries), (mlp_turn, scores(0)), (mlp_up, scores(1)),
                      (mlp_down, turn(0)), (None, turn(1)), (None, attend), (None, output)])


STAGES = [stage_l0, stage_l1, stage_cross1, stage_cross2, stage_l3]


def build(nc, dram, stages=STAGES):
    pr = Program(nc, dram)
    with ExitStack() as ctx:
        pr.psum = ctx.enter_context(nc.psum_tensor("psum", [P, 8, 512], F32))
        consts = ctx.enter_context(nc.sbuf_tensor("consts", [P, 2310], F32))
        pr.cols = ctx.enter_context(nc.sbuf_tensor("cols", [P, pr.ncols], F32))
        pr.rows = ctx.enter_context(nc.sbuf_tensor("rows", [P, D * (len(ROWS) - 1) + S], F32))
        pr.neg_half = ctx.enter_context(nc.sbuf_tensor("neg_half", [P, NP], F32))
        consts_in = ctx.enter_context(nc.semaphore("consts_in"))
        pr.ident = consts[:, 0:P]
        pr.same_head = consts[:, P:2 * P]
        pr.spread = consts[:, 2 * P:10 * P].rearrange("p (j m) -> p j m", j=8)
        pr.gather = consts[:, 10 * P:18 * P].rearrange("p (j m) -> p j m", j=8)
        pr.head2 = consts[:, 18 * P:18 * P + 2]
        pr.head4 = consts[:, 18 * P + 2:18 * P + 6]
        with nc.Block() as block:
            @block.sync
            def _(sp):
                sp.dma_start(consts[:], dram["consts"]).then_inc(consts_in, 16)
                sp.dma_start(pr.cols[:], dram["cols"]).then_inc(consts_in, 16)
                sp.dma_start(pr.rows[:], dram["rows"][0, :].partition_broadcast(P)
                             ).then_inc(consts_in, 16)
                sp.wait_ge(consts_in, 48)

            @block.vector
            def _(dve):
                nc.vector.memset(pr.neg_half[:], -0.5)

        scratch = [nc.dram_tensor(f"scratch{n}", (B * S, D), F32, kind="Internal").ap()
                   for n in range(2)]
        src = dram["x"]
        for n, stage in enumerate(stages):
            dst = dram["out"] if n == len(stages) - 1 else scratch[n % 2]
            stage(pr, src, dst)
            src = dst


_MATRICES = ["L0_xattn_q_w", "L0_xattn_k_w", "L0_xattn_v_w", "L0_xattn_cproj_w", "L0_xattn_fc_w",
             "L0_xattn_proj_w", "L1_xattn_maa_w1", "L1_xattn_td_w1", "L1_xattn_td_w2",
             "L2_xattn_wq1", "L2_xattn_wk1", "L2_xattn_wv1", "L2_xattn_wo1",
             "L2_xattn_wq2", "L2_xattn_wk2", "L2_xattn_wv2", "L2_xattn_wo2",
             "L2_xattn_w_fc1", "L2_xattn_w_fc2", "L2_xattn_bv1", "L2_xattn_bv2",
             "L3_xattn_Wq", "L3_xattn_Wv", "L3_xattn_Wo"]
_TRANSPOSED = ["L1_xattn_Wr", "L1_xattn_Wk", "L1_xattn_Wv", "L1_xattn_Wg", "L1_xattn_Wo",
               "L1_xattn_Wfk", "L1_xattn_Wfr", "L1_xattn_Wfv"]


def kernel(**inputs):
    import numpy as np
    import concourse.bacc as bacc
    from concourse.bass_utils import run_bass_kernel_spmd

    a = {k: np.asarray(v) for k, v in inputs.items()}
    ctx = a["ctx_2048"]
    heads = {"L3_xattn_Wk_rep": np.repeat(a["L3_xattn_Wk"].reshape(D, 8, 1, 8), 4, 2).reshape(D, D)}
    a["L3_xattn_bk_rep"] = np.repeat(a["L3_xattn_bk"].reshape(8, 1, 8), 4, 1).reshape(D)
    arrays = {
        "x": a["x"].reshape(B * S, D),
        "ctxT": ctx.reshape(B * S, D).T,
        "edgeT": ctx[:, 0:2].transpose(2, 1, 0).reshape(DC, P, 2 * B),
        "state0": ctx[:, 2:10].reshape(B, DC, P, 8).transpose(2, 1, 3, 0).reshape(P, DC * 8 * B),
        "key_mask": a["mask_BxS2_bf1"].view(np.uint8),
        "mask": a["mask_Bx1xSxS2_ff0"].reshape(B * S, S),
        "cols": np.concatenate([a[n].reshape(-1, P) for n in COLS], 0).T,
        "rows": np.concatenate([a[n].reshape(-1) for n in ROWS], 0).reshape(1, -1),
        "maa_w2": a["L1_xattn_maa_w2"].reshape(160, D),
        "L3_xattn_Wk_rep": heads["L3_xattn_Wk_rep"],
    }
    for n in _MATRICES:
        arrays[n] = a[n].reshape(1, -1) if a[n].ndim == 1 else a[n]
    for n in _TRANSPOSED:
        arrays[n] = a[n].T
    p = np.arange(P)
    same = (p[:, None] // 8 == p[None, :] // 8).astype(np.float32)
    spread = np.stack([same * (p[:, None] % 8 == j) for j in range(8)], 1).reshape(P, 8 * P)
    gather = np.stack([same * (p[None, :] % 8 == j) for j in range(8)], 1).reshape(P, 8 * P)
    arrays["consts"] = np.concatenate(
        [np.eye(P, dtype=np.float32), same, spread, gather,
         (p[:, None] // 16 % 2 == np.arange(2)[None, :]).astype(np.float32),
         (p[:, None] // 8 % 4 == np.arange(4)[None, :]).astype(np.float32)], 1).astype(np.float32)
    arrays = {f"in_{k}": np.ascontiguousarray(v) for k, v in arrays.items()}

    nc = bacc.Bacc("TRN2", target_bir_lowering=False, num_devices=1)
    dram = {k[3:]: nc.dram_tensor(k, v.shape, mybir.dt.from_np(v.dtype), kind="ExternalInput").ap()
            for k, v in arrays.items()}
    dram["out"] = nc.dram_tensor("out_0", (B * S, D), F32, kind="ExternalOutput").ap()
    build(nc, dram)
    r = run_bass_kernel_spmd(nc, [arrays], core_ids=[0])
    return np.asarray(r.results[0]["out_0"]).reshape(B, S, D)
```

```python
import math
from contextlib import ExitStack

import concourse.bass as bass
from concourse import mybir

F32 = mybir.dt.float32
F32R = mybir.dt.float32r
U8 = mybir.dt.uint8
ALU = mybir.AluOpType
ACT = mybir.ActivationFunctionType
AX = mybir.AxisListType

P = 128
B = 64
S = 64
D = 256
DC = D // P
T = 256
NB = T // S
NP = T // P
TRIPS = B * S // T
INNER = 4 * D
MC = INNER // P

COLS = ["L0_xattn_ln1_w", "L0_xattn_ln1_b", "L0_xattn_q_b", "L0_xattn_k_b", "L0_xattn_ln2_w",
        "L0_xattn_ln2_b", "L0_xattn_fc_b",
        "L1_xattn_ln1_w", "L1_xattn_ln1_b", "L1_xattn_ln2_w", "L1_xattn_ln2_b", "L1_xattn_maa_x",
        "L1_xattn_maa_stack", "L1_xattn_time_decay", "L1_xattn_u", "L1_xattn_gn_w",
        "L1_xattn_gn_b", "L1_xattn_ffn_maa_k", "L1_xattn_ffn_maa_r",
        "L2_xattn_ln1_scale", "L2_xattn_ln1_offset", "L2_xattn_bq1", "L2_xattn_bk1",
        "L2_xattn_bias_k1", "L2_xattn_bias_v1", "L2_xattn_ln2_scale", "L2_xattn_ln2_offset",
        "L2_xattn_bq2", "L2_xattn_bk2", "L2_xattn_bias_k2", "L2_xattn_bias_v2",
        "L2_xattn_ln_mlp_scale", "L2_xattn_ln_mlp_offset", "L2_xattn_b_fc1",
        "L3_xattn_bq", "L3_xattn_bk_rep"]
COL_WIDTH = {"L0_xattn_fc_b": 8, "L1_xattn_maa_stack": 10, "L2_xattn_bq1": 16, "L2_xattn_bk1": 16,
             "L2_xattn_bias_k1": 16, "L2_xattn_bias_v1": 16, "L2_xattn_bq2": 16, "L2_xattn_bk2": 16,
             "L2_xattn_bias_k2": 16, "L2_xattn_bias_v2": 16, "L2_xattn_b_fc1": 8}
ROWS = ["L0_xattn_v_b", "L0_xattn_cproj_b", "L0_xattn_proj_b", "L2_xattn_bo1", "L2_xattn_bo2",
        "L2_xattn_b_fc2", "L3_xattn_bo", "L3_xattn_gamma", "L3_xattn_beta", "L3_xattn_bv"]



class Norm:
    pass


class NormSignals:
    pass


class Program:

    def __init__(self, nc, dram):
        self.nc = nc
        self.dram = dram
        self.at = {}
        self.col0 = {}
        n = 0
        for name in COLS:
            self.col0[name] = n
            n += COL_WIDTH.get(name, 2)
        self.ncols = n

    def col(self, name, c=0):
        n = self.col0[name] + c
        return self.cols[:, n:n + 1]

    def cols_of(self, name):
        n = self.col0[name]
        return self.cols[:, n:n + COL_WIDTH.get(name, 2)]

    def staggered(self, eng, steps):
        most = max(lead for lead, _ in steps)

        def partial(i):
            for lead, step in steps:
                if 1 <= i + lead <= TRIPS:
                    step(i + lead)

        for i in range(1 - most, 1):
            partial(i)
        with eng.Fori(1, TRIPS - most + 1) as i:
            for lead, step in steps:
                step(i + lead)
        for i in range(TRIPS - most + 1, TRIPS + 1):
            partial(i)

    def ln_tiles(self, sb, tag=""):
        ln = Norm()
        ln.stats = sb(f"ln{tag}_stats", [P, NP, 6])
        ln.mv = sb(f"ln{tag}_mv", [P, NP, 2])
        ln.ve = sb(f"ln{tag}_ve", [P, NP])
        ln.rstd = sb(f"ln{tag}_rstd", [P, NP])
        return ln

    def ln_sems(self, sem, tag=""):
        s = NormSignals()
        s.stats, s.mv, s.xn_ready = (sem(f"ln{tag}_{n}", NP) for n in ("stats", "mv", "xn_ready"))
        s.ve, s.rstd = sem(f"ln{tag}_ve", 1), sem(f"ln{tag}_rstd", 1)
        return s

    def ln_rstd(self, pool, ln, s, n):
        pool.wait_ge(s.ve, n + 1)
        self.nc.gpsimd.tensor_tensor(ln.rstd[:], ln.ve[:], self.neg_half[:, 0:NP], ALU.pow
                                     ).then_inc(s.rstd, 1)

    def ln_normalise(self, dve, ln, s, src, dst, n, eps=1e-5):
        v = self.nc.vector
        for t in range(NP):
            v.bn_stats(ln.stats[:, t, :], src[:, t, :]).then_inc(s.stats, 1)
        dve.wait_ge(s.stats, NP * n + NP)
        v.nop(nofuse=True)
        for t in range(NP):
            v.bn_aggr(ln.mv[:, t, :], ln.stats[:, t, :]).then_inc(s.mv, 1)
        dve.wait_ge(s.mv, NP * n + NP)
        v.tensor_scalar(ln.ve[:], ln.mv[:, :, 1], eps, None, ALU.add).then_inc(s.ve, 1)
        dve.wait_ge(s.rstd, n + 1)
        for t in range(NP):
            v.tensor_scalar(dst[:, t, :], src[:, t, :], ln.mv[:, t, 0:1], ln.rstd[:, t:t + 1],
                            ALU.subtract, ALU.mult).then_inc(s.xn_ready, 1)

    def transpose_tiles(self, src, n):
        for c in range(DC):
            for t in range(NP):
                mm = self.nc.tensor.transpose(bank(self.psum, n, [DC, NP, P])[:, c, t, :],
                                              src[:, t, c * P:(c + 1) * P], self.ident)
        return mm

    def project_T(self, w, xT, n, outs):
        for m in range(outs):
            for c in range(DC):
                x = xT[:, c]
                mm = self.nc.tensor.matmul(bank(self.psum, n, [2, T])[:, m, :],
                                           w[:, c, m * P:(m + 1) * P], x,
                                           start=(c == 0), stop=(c == DC - 1))
        return mm

    def project_rows(self, xT, w, n, chunks, tiles=range(NP)):
        for t in tiles:
            for c in range(chunks):
                mm = self.nc.tensor.matmul(bank(self.psum, n, [NP, D])[:, t, :],
                                           xT[:, c, t * P:(t + 1) * P], w[:, c, :],
                                           start=(c == 0), stop=(c == chunks - 1))
        return mm

    def rowv(self, name):
        n = D * ROWS.index(name)
        return self.rows[:, n:n + (S if name == "L3_xattn_bv" else D)]

    def row(self, name, times):
        return self.rowv(name).unsqueeze(1).to_broadcast([P, times, D])


def first_trip(i):
    return isinstance(i, int) and i == 1


def last_trip(i):
    return isinstance(i, int) and i == TRIPS


def weight(ap):
    return ap.rearrange("(c p) n -> p c n", p=P)


def bank(ps, n, shape=None):
    v = ps[:, n, :]
    if shape is not None:
        names = "abcd"[:len(shape)]
        v = v.rearrange(f"p ({' '.join(names)}) -> p {' '.join(names)}", **dict(zip(names, shape)))
    return v


def tokens(ap):
    return ap.rearrange("(g t p) e -> g p t e", t=NP, p=P)


def start_counts(nc, sems):
    with nc.Block() as block:
        @block.gpsimd
        def _(pool):
            for s, _ in sems:
                nc.gpsimd.sem_clear(s)
            for s, per in sems:
                if per:
                    nc.gpsimd.sem_inc(s, per)



def stage_l0(pr, x_src, x_dst):
    nc, dram, PS = pr.nc, pr.dram, pr.psum
    H, HD = 16, 16
    SCALE = 1.0 / math.sqrt(HD)
    MASKED = 3.4028234663852886e38
    RG = 4
    with ExitStack() as ctx:
        def sb(name, shape, dt=F32):
            return ctx.enter_context(nc.sbuf_tensor("l0_" + name, shape, dt))

        sems = []

        def sem(name, per):
            s = ctx.enter_context(nc.semaphore("l0_" + name))
            sems.append((s, per))
            return s

        wq, wk, wv, wo = (sb(n, [P, DC, D]) for n in ("wq", "wk", "wv", "wo"))
        wfc = sb("wfc", [P, DC, INNER])
        wproj = sb("wproj", [P, MC, D])
        qb_scaled = sb("qb_scaled", [P, DC])
        key_mask = sb("key_mask", [P, B // 2, S], U8)
        mask_add = sb("mask_add", [P, B // 2, S])
        x_in = sb("x_in", [P, NP, D])
        x_res = sb("x_res", [P, NP, D])
        ctxT = sb("ctxT", [P, DC, NB, 2, S])
        ln = pr.ln_tiles(sb)
        xn = sb("xn", [P, NP, D])
        hT = sb("hT", [P, DC, T])
        qT = sb("qT", [P, DC, T])
        k_blk = sb("k_blk", [P, DC, NB, 2, S])
        v_blk = sb("v_blk", [P, NB, H // 2, 2, HD])
        sc = [sb(f"sc{t}", [P, H, S]) for t in range(NP)]
        mx = sb("mx", [P, NP, H])
        sm = sb("sm", [P, NP, H])
        rs = sb("rs", [P, NP, H])
        pT = sb("pT", [P, NP, H // 2, P])
        oT = sb("oT", [P, DC, T])
        xb = sb("xb", [P, NP, D])
        ln2 = pr.ln_tiles(sb, "2")
        hn = sb("hn", [P, NP, D])
        hid = sb("hid", [P, NP, D])
        hb = sb("hb", [P, NP, D])
        h2T = sb("h2T", [P, DC, T])
        act = sb("act", [P, MC, T])
        outt = sb("outt", [P, NP, D])

        late_weights_in = sem("late_weights_in", 0)
        weights_in, mask_in, setup = sem("weights_in", 0), sem("mask_in", 0), sem("setup", 0)
        x_loaded, ctx_loaded, res_loaded = (sem("x_loaded", 16), sem("ctx_loaded", 64),
                                            sem("res_loaded", 16))
        stored = sem("stored", 16)
        ln_s = pr.ln_sems(sem)
        xnT_ps, hT_ready = sem("xnT_ps", 1), sem("hT_ready", 2)
        q_ps, qT_ready = sem("q_ps", 1), sem("qT_ready", 2)
        k_ps, k_ready = sem("k_ps", 1), sem("k_ready", 4)
        v_ps, v_ready = sem("v_ps", 2), sem("v_ready", 8)
        s_ps, s_masked, s_max, s_sub, s_exp = (sem(n, NP) for n in
                                               ("s_ps", "s_masked", "s_max", "s_sub", "s_exp"))
        s_sum, s_rec, p_ready = (sem(n, NP) for n in ("s_sum", "s_rec", "p_ready"))
        pT_ps, pT_ready = sem("pT_ps", NP), sem("pT_ready", NP)
        o_ps, oT_ready = sem("o_ps", 1), sem("oT_ready", 1)
        c_ps, xb_ready, hid_ready = sem("c_ps", 1), sem("xb_ready", 1), sem("hid_ready", 1)
        ln2_s = pr.ln_sems(sem, "2")
        hnT_ps, h2T_ready = sem("hnT_ps", 1), sem("h2T_ready", 2)
        fc_ps, act_ready, m_ps = sem("fc_ps", 4), sem("act_ready", MC), sem("m_ps", NP)
        hb_ready, out_ready = sem("hb_ready", 1), sem("out_ready", 1)
        start_counts(nc, sems)
        xv, ov = tokens(x_src), tokens(x_dst)
        cv = dram["ctxT"].rearrange("(c p) (g b s) -> g c p b s", p=P, b=NB, s=S)

        block = ctx.enter_context(nc.Block())

        @block.sync
        def _(sp):
            for b2 in range(2):
                src = dram["key_mask"].rearrange("(n t) k -> t n k", t=2)[b2]
                sp.dma_start(key_mask[64 * b2:64 * b2 + 64, :, :],
                             src.partition_broadcast(64)).then_inc(mask_in, 16)

            def load_x(i):
                sp.wait_ge(ln_s.xn_ready, 2 * i)
                sp.dma_start(x_in[:], xv[i - 1]).then_inc(x_loaded, 16)

            def load_ctx(i):
                sp.wait_ge(v_ps, 2 * i)
                for c in range(DC):
                    for u in range(2):
                        sp.dma_start(ctxT[:, c, :, u, :], cv[i - 1, c]).then_inc(ctx_loaded, 16)

            def load_res(i):
                sp.wait_ge(xb_ready, i)
                sp.dma_start(x_res[:], xv[i - 1]).then_inc(res_loaded, 16)

            def store(i):
                sp.wait_ge(out_ready, i + 1)
                sp.dma_start(ov[i - 1], outt[:]).then_inc(stored, 16)

            pr.staggered(sp, [(3, load_x), (2, load_ctx), (2, load_res), (0, store)])
            sp.wait_ge(stored, 16 * TRIPS + 16)

        @block.gpsimd
        def _(pool):
            pool.wait_ge(pr.consts_in, 48)
            nc.gpsimd.memset(v_blk[:], 0.0).then_inc(setup, 1)

            def front_rstd(i):
                pr.ln_rstd(pool, ln, ln_s, i)

            def residual(i):
                pool.wait_ge(res_loaded, 16 * (i + 1))
                pool.wait_ge(hid_ready, i)
                nc.gpsimd.tensor_tensor(xb[:], x_res[:], pr.row("L0_xattn_cproj_b", NP), ALU.add
                                        ).then_inc(xb_ready, 1)

            def normalise(t):
                def step(i):
                    pool.wait_ge(s_rec, 2 * i + t + 1)
                    nc.gpsimd.tensor_tensor(sc[t][:], sc[t][:],
                                            rs[:, t, :].unsqueeze(2).to_broadcast([P, H, S]),
                                            ALU.mult).then_inc(p_ready, 1)
                return step

            def mlp_rstd(i):
                pr.ln_rstd(pool, ln2, ln2_s, i)

            def mlp_residual(i):
                pool.wait_ge(hid_ready, i + 1)
                pool.wait_ge(out_ready, i)
                nc.gpsimd.tensor_tensor(hb[:], hid[:], pr.row("L0_xattn_proj_b", NP), ALU.add
                                        ).then_inc(hb_ready, 1)

            pr.staggered(pool, [(0, mlp_rstd), (0, mlp_residual), (1, residual), (1, normalise(0)),
                                (1, normalise(1)), (2, front_rstd)])

        @block.scalar
        def _(act_e):
            for dst, name in ((wk, "L0_xattn_k_w"), (wq, "L0_xattn_q_w"), (wv, "L0_xattn_v_w")):
                act_e.dma_start(dst[:], weight(dram[name])).then_inc(weights_in, 16)
            for dst, name in ((wo, "L0_xattn_cproj_w"), (wfc, "L0_xattn_fc_w"),
                              (wproj, "L0_xattn_proj_w")):
                act_e.dma_start(dst[:], weight(dram[name])).then_inc(late_weights_in, 16)
            act_e.wait_ge(pr.consts_in, 48)
            act_e.wait_ge(setup, 3)

            def queries(i):
                act_e.wait_ge(q_ps, i + 1)
                for c in range(DC):
                    nc.scalar.activation(qT[:, c, :], bank(PS, 4, [2, T])[:, c, :], ACT.Identity,
                                         bias=qb_scaled[:, c:c + 1], scale=SCALE
                                         ).then_inc(qT_ready, 1)

            def exps(t):
                def step(i):
                    act_e.wait_ge(s_sub, 2 * i + t + 1)
                    nc.scalar.activation(sc[t][:], sc[t][:], ACT.Exp).then_inc(s_exp, 1)
                return step

            def turned(t):
                def step(i):
                    act_e.wait_ge(pT_ps, 2 * i + t + 1)
                    nc.scalar.copy(pT[:, t, :, :], PS[:, 2 * t:2 * t + 2, :].rearrange(
                        "p a (b q) -> p (a b) q", q=P)).then_inc(pT_ready, 1)
                return step

            def attended(i):
                act_e.wait_ge(o_ps, i + 1)
                nc.scalar.copy(oT[:], bank(PS, 4, [DC, T])).then_inc(oT_ready, 1)

            def gelu(u):
                def step(i):
                    act_e.wait_ge(fc_ps, 4 * i + u + 1)
                    for m in range(2 * u, 2 * u + 2):
                        nc.scalar.activation(act[:, m, :],
                                             bank(PS, 7 - u % 2, [2, T])[:, m % 2, :],
                                             ACT.Gelu_apprx_tanh, bias=pr.col("L0_xattn_fc_b", m)
                                             ).then_inc(act_ready, 1)
                return step

            pr.staggered(act_e, [(1, queries), (0, gelu(0)), (1, exps(0)), (0, gelu(1)),
                                 (0, gelu(2)), (0, gelu(3)), (1, exps(1)), (1, turned(0)),
                                 (1, turned(1)), (1, attended)])

        @block.vector
        def _(dve):
            dve.wait_ge(pr.consts_in, 48)
            dve.wait_ge(mask_in, 32)
            nc.vector.tensor_scalar(mask_add[:], key_mask[:], MASKED, -MASKED, ALU.mult, ALU.add
                                    ).then_inc(setup, 1)
            nc.vector.tensor_scalar(qb_scaled[:], pr.cols_of("L0_xattn_q_b"), SCALE, None, ALU.mult
                                    ).then_inc(setup, 1)
            dve.wait_ge(setup, 3)

            def front_norm(i):
                dve.wait_ge(x_loaded, 16 * (i + 1))
                dve.wait_ge(xnT_ps, i)
                pr.ln_normalise(dve, ln, ln_s, x_in, xn, i)

            def front_weighted(i):
                dve.wait_ge(xnT_ps, i + 1)
                dve.wait_ge(q_ps, i)
                for c in range(DC):
                    nc.vector.tensor_scalar(hT[:, c, :], bank(PS, 6, [DC, T])[:, c, :],
                                            pr.col("L0_xattn_ln1_w", c), pr.col("L0_xattn_ln1_b", c),
                                            ALU.mult, ALU.add).then_inc(hT_ready, 1)

            def keys(i):
                dve.wait_ge(k_ps, i + 1)
                for c in range(DC):
                    for hh in range(2):
                        nc.vector.tensor_scalar(
                            k_blk[:, c, :, hh, :], bank(PS, 5, [DC, NB, S])[:, c, :, :],
                            pr.col("L0_xattn_k_b", c), pr.head2[:, hh:hh + 1], ALU.add, ALU.mult
                        ).then_inc(k_ready, 1)

            def values(t):
                def step(i):
                    dve.wait_ge(v_ps, 2 * i + t + 1)
                    for hh in range(2):
                        half = slice(64 * hh, 64 * hh + 64)
                        for u in range(2):
                            vp = bank(PS, 7 - 2 * t, [2, H // 2, 2, HD])
                            bias = pr.rowv("L0_xattn_v_b")[half, :].rearrange(
                                "p (a h e) -> p a h e", h=2, e=HD)[:, :, hh, :]
                            nc.vector.tensor_tensor(v_blk[half, 2 * t + u, :, hh, :],
                                                    vp[half, u, :, hh, :], bias,
                                                    ALU.add).then_inc(v_ready, 1)
                return step

            def softmax_in(t):
                def step(i):
                    dve.wait_ge(s_ps, 2 * i + t + 1)
                    m = mask_add[:, NP * (i - 1) + t, :]
                    nc.vector.tensor_tensor(
                        sc[t][:].rearrange("p (r h) k -> p r h k", r=RG),
                        PS[:, 0:RG, 0:256].rearrange("p r (h k) -> p r h k", k=S),
                        m.unsqueeze(1).unsqueeze(1).to_broadcast([P, RG, H // RG, S]), ALU.add
                    ).then_inc(s_masked, 1)
                    dve.wait_ge(s_masked, 2 * i + t + 1)
                    nc.vector.tensor_reduce(mx[:, t, :], sc[t][:], AX.X, ALU.max
                                            ).then_inc(s_max, 1)
                    dve.wait_ge(s_max, 2 * i + t + 1)
                    nc.vector.tensor_tensor(sc[t][:], sc[t][:],
                                            mx[:, t, :].unsqueeze(2).to_broadcast([P, H, S]),
                                            ALU.subtract).then_inc(s_sub, 1)
                return step

            def softmax_sum(t):
                def step(i):
                    dve.wait_ge(s_exp, 2 * i + t + 1)
                    nc.vector.tensor_reduce(sm[:, t, :], sc[t][:], AX.X, ALU.add
                                            ).then_inc(s_sum, 1)
                    dve.wait_ge(s_sum, 2 * i + t + 1)
                    nc.vector.reciprocal(rs[:, t, :], sm[:, t, :]).then_inc(s_rec, 1)
                return step

            def hidden(i):
                dve.wait_ge(c_ps, i + 1)
                dve.wait_ge(xb_ready, i + 1)
                dve.wait_ge(hb_ready, i)
                nc.vector.tensor_tensor(hid[:], bank(PS, 5, [NP, D]), xb[:], ALU.add
                                        ).then_inc(hid_ready, 1)

            def mlp_norm(i):
                dve.wait_ge(hid_ready, i + 1)
                dve.wait_ge(hnT_ps, i)
                pr.ln_normalise(dve, ln2, ln2_s, hid, hn, i)

            def mlp_weighted(i):
                dve.wait_ge(hnT_ps, i + 1)
                for c in range(DC):
                    nc.vector.tensor_scalar(h2T[:, c, :], bank(PS, 6, [DC, T])[:, c, :],
                                            pr.col("L0_xattn_ln2_w", c), pr.col("L0_xattn_ln2_b", c),
                                            ALU.mult, ALU.add).then_inc(h2T_ready, 1)

            def mlp_out(i):
                dve.wait_ge(m_ps, 2 * i + 2)
                dve.wait_ge(hb_ready, i + 1)
                dve.wait_ge(stored, 16 * i)
                nc.vector.tensor_tensor(outt[:], bank(PS, 7, [NP, D]), hb[:], ALU.add
                                        ).then_inc(out_ready, 1)

            pr.staggered(dve, [(0, mlp_norm), (1, keys), (1, values(0)), (0, mlp_weighted),
                               (1, softmax_in(0)), (1, values(1)), (1, softmax_in(1)),
                               (1, softmax_sum(0)), (1, softmax_sum(1)), (2, front_norm),
                               (0, mlp_out), (2, front_weighted), (1, hidden)])

        @block.tensor
        def _(pe):
            pe.wait_ge(pr.consts_in, 48)
            pe.wait_ge(setup, 3)

            def keys(i):
                pe.wait_ge(weights_in, 16 * 3)
                pe.wait_ge(hid_ready, i)
                pe.wait_ge(ctx_loaded, 64 * (i + 1))
                pr.project_T(wk, ctxT[:, :, :, 0, :], 5, DC).then_inc(k_ps, 1)

            def front_turn(i):
                pe.wait_ge(ln_s.xn_ready, 2 * i + 2)
                if not first_trip(i):
                    pe.wait_ge(act_ready, 8 * i - 8)
                pe.wait_ge(hT_ready, 2 * i)
                pr.transpose_tiles(xn, 6).then_inc(xnT_ps, 1)

            def queries(i):
                pe.wait_ge(weights_in, 16 * 3)
                pe.wait_ge(oT_ready, i)
                pe.wait_ge(hT_ready, 2 * i + 2)
                pr.project_T(wq, hT, 4, DC).then_inc(q_ps, 1)

            def values(t):
                def step(i):
                    if t == 1:
                        pe.wait_ge(k_ready, 4 * i + 4)
                    elif not first_trip(i):
                        pe.wait_ge(out_ready, i - 1)
                    for u in range(2):
                        b = 2 * t + u
                        for c in range(DC):
                            two = ctxT[:, c, b, :, :].rearrange("p u s -> p (u s)")
                            mm = nc.tensor.matmul(bank(PS, 7 - 2 * t, [2, D])[:, u, :],
                                                  two, wv[:, c, :], start=(c == 0), stop=(c == 1))
                    mm.then_inc(v_ps, 1)
                return step

            def scores(t):
                def step(i):
                    if t == 0:
                        pe.wait_ge(k_ready, 4 * i + 4)
                        pe.wait_ge(qT_ready, 2 * i + 2)
                        pe.wait_ge(pT_ready, 2 * i)
                    else:
                        pe.wait_ge(s_masked, 2 * i + 1)
                    for r in range(RG):
                        rows = slice(32 * r, 32 * r + 32)
                        for c in range(DC):
                            for b2 in range(2):
                                b = 2 * t + b2
                                mm = nc.tensor.matmul(
                                    bank(PS, r, [4, P])[64 * b2:64 * b2 + 64, c, :],
                                    qT[rows, c, b * S:(b + 1) * S],
                                    k_blk[rows, c, b, :, :], start=True, stop=True)
                    mm.then_inc(s_ps, 1)
                return step

            def turn(t):
                def step(i):
                    pe.wait_ge(s_masked, 2 * i + 2)
                    pe.wait_ge(p_ready, 2 * i + t + 1)
                    for n in range(H // 2):
                        mm = nc.tensor.transpose(
                            bank(PS, 2 * t + n // 4, [4, P])[:, n % 4, :],
                            sc[t][:, 2 * n:2 * n + 2, :].rearrange("p h k -> p (h k)"), pr.ident)
                    mm.then_inc(pT_ps, 1)
                return step

            def attend(i):
                pe.wait_ge(v_ready, 8 * i + 8)
                for t in range(NP):
                    pe.wait_ge(pT_ready, 2 * i + t + 1)
                    for c in range(DC):
                        for r in range(RG):
                            for b2 in range(2):
                                b = 2 * t + b2
                                mm = nc.tensor.matmul(
                                    bank(PS, 4, [DC, T])[32 * r:32 * r + 32, c, b * S:(b + 1) * S],
                                    v_blk[:, b, c * RG + r, :, :].rearrange("p h e -> p (h e)"),
                                    pT[:, t, 2 * r + c, b2 * S:(b2 + 1) * S],
                                    start=True, stop=True)
                mm.then_inc(o_ps, 1)

            def output(i):
                pe.wait_ge(late_weights_in, 16 * 3)
                pe.wait_ge(oT_ready, i + 1)
                pr.project_rows(oT, wo, 5, DC).then_inc(c_ps, 1)

            def mlp_turn(i):
                pe.wait_ge(act_ready, 8 * i)
                pe.wait_ge(ln2_s.xn_ready, 2 * i + 2)
                pr.transpose_tiles(hn, 6).then_inc(hnT_ps, 1)

            def mlp_up(u):
                def step(i):
                    if u == 0:
                        pe.wait_ge(v_ready, 8 * i + (8 if last_trip(i) else 12))
                        pe.wait_ge(h2T_ready, 2 * i + 2)
                    if u >= 2:
                        pe.wait_ge(act_ready, 8 * i + 2 * (u - 1))
                    for m in range(2 * u, 2 * u + 2):
                        for c in range(DC):
                            mm = nc.tensor.matmul(bank(PS, 7 - u % 2, [2, T])[:, m % 2, :],
                                                  wfc[:, c, m * P:(m + 1) * P], h2T[:, c, :],
                                                  start=(c == 0), stop=(c == 1))
                    mm.then_inc(fc_ps, 1)
                return step

            def mlp_down(t):
                def step(i):
                    pe.wait_ge(act_ready, 8 * i + 8)
                    pr.project_rows(act, wproj, 7, MC, [t]).then_inc(m_ps, 1)
                return step

            pr.staggered(pe, [(1, queries), (1, keys), (1, values(0)), (0, mlp_turn),
                              (1, scores(0)), (0, mlp_up(0)), (1, values(1)), (1, scores(1)),
                              (0, mlp_up(1)), (0, mlp_up(2)), (0, mlp_up(3)), (0, mlp_down(0)),
                              (0, mlp_down(1)), (1, turn(0)), (1, turn(1)), (1, attend),
                              (2, front_turn), (1, output)])



def stage_l1(pr, x_src, x_dst):
    nc, dram, PS = pr.nc, pr.dram, pr.psum
    HS = 8
    DM, DD, F = 32, 64, 5
    S1 = S + 1
    L = "L1_xattn_"
    with ExitStack() as ctx:
        def sb(name, shape, dt=F32):
            return ctx.enter_context(nc.sbuf_tensor("l1_" + name, shape, dt))

        sems = []

        def sem(name, per):
            s = ctx.enter_context(nc.semaphore("l1_" + name))
            sems.append((s, per))
            return s

        maa_w1 = sb("maa_w1", [P, DC, F * DM])
        maa_w2a = sb("maa_w2a", [P, D])
        maa_w2b = sb("maa_w2b", [DM, D])
        td_w1 = sb("td_w1", [P, DC, DD])
        td_w2 = sb("td_w2", [DD, D])
        wr, wk, wv, wg, wo, wfk, wfr, wfv = (sb(n, [P, DC, D]) for n in (
            "wr", "wk", "wv", "wg", "wo", "wfk", "wfr", "wfv"))
        eps = sb("eps", [P, 1])
        edge = sb("edge", [P, DC, 2, B])
        state0 = sb("state0", [P, DC, HS, B])
        x_in = sb("x_in", [P, NP, D])
        x_res = sb("x_res", [P, NP, D])
        ln = pr.ln_tiles(sb)
        xn = sb("xn", [P, NP, D])
        xa = sb("xa", [P, DC, NB, S1])
        sx = sb("sx", [P, DC, NB, S])
        xx = sb("xx", [P, DC, T])
        th = sb("th", [P, T])
        th4 = sb("th4", [DM, T])
        tf = [sb(f"tf{f}", [P, DC, T]) for f in range(F)]
        xm = [sb(f"xm{f}", [P, DC, T]) for f in range(F)]
        td_t = sb("td_t", [DD, T])
        ew = sb("ew", [P, DC, T])
        w = sb("w", [P, DC, NB, S1])
        kT, rT, vT, gT, sg = (sb(n, [P, DC, T]) for n in ("kT", "rT", "vT", "gT", "sg"))
        ge = sb("ge", [P, DC, T])
        ruk = sb("ruk", [P, DC, T])
        bonus = sb("bonus", [P, DC, T])
        a = sb("a", [P, HS, DC, NB, S1])
        st = sb("st", [P, HS, DC, NB, S1])
        m = sb("m", [P, HS, DC, T])
        og, cen, sq, sd, rstd, yT = (sb(n, [P, DC, T]) for n in (
            "og", "cen", "sq", "sd", "rstd", "yT"))
        x1 = sb("x1", [P, NP, D])
        ln2 = pr.ln_tiles(sb, "2")
        x1n = sb("x1n", [P, NP, D])
        xc = sb("xc", [P, DC, NB, S1])
        sx2 = sb("sx2", [P, DC, NB, S])
        xk2, xr2, rk, kk = (sb(n, [P, DC, T]) for n in ("xk2", "xr2", "rk", "kk"))
        rr = sb("rr", [P, NP, D])
        outt = sb("outt", [P, NP, D])

        weights_in, late_weights_in = sem("weights_in", 0), sem("late_weights_in", 0)
        setup = sem("setup", 0)
        x_loaded, res_loaded, stored = (sem(n, 16) for n in ("x_loaded", "res_loaded", "stored"))
        ln_s = pr.ln_sems(sem)
        xnT_ps, xa_ready, edge_ready, sx_ready, xx_ready = (sem(n, per) for n, per in (
            ("xnT_ps", 1), ("xa_ready", 2), ("edge_ready", 1), ("sx_ready", 1), ("xx_ready", 2)))
        w1_ps, th_ready, w2_ps, tf_ready, xm_ready = (sem(n, per) for n, per in (
            ("w1_ps", 1), ("th_ready", 2), ("w2_ps", F), ("tf_ready", 2 * F), ("xm_ready", F)))
        td1_ps, td1_ready, td2_ps, ew_ready, w_ready = (sem(n, 1) for n in (
            "td1_ps", "td1_ready", "td2_ps", "ew_ready", "w_ready"))
        k_ps, k_ready, r_ps, r_ready, v_ps, v_ready, g_ps, g_copied, g_sig, sg_ready = (
            sem(n, 1) for n in ("k_ps", "k_ready", "r_ps", "r_ready", "v_ps", "v_ready", "g_ps",
                                "g_copied", "g_sig", "sg_ready"))
        ruk_ready, ruk_ps, bonus_ready = sem("ruk_ready", 2), sem("ruk_ps", 1), sem("bonus_ready", 1)
        st0_ready = sem("st0_ready", 1)
        vrep_ps, a_ready, scan_done, m_ready = (sem(n, HS) for n in (
            "vrep_ps", "a_ready", "scan_done", "m_ready"))
        gat_ps, og_ready, mean_ps, cen_ready, sq_ready, var_ps, sd_ready, rstd_ready, cn_ready = (
            sem(n, 1) for n in ("gat_ps", "og_ready", "mean_ps", "cen_ready", "sq_ready",
                                "var_ps", "sd_ready", "rstd_ready", "cn_ready"))
        gn_ready, y_ready, wo_ps, x1_ready = (sem(n, per) for n, per in (
            ("gn_ready", 2), ("y_ready", 1), ("wo_ps", 1), ("x1_ready", 1)))
        ln2_s = pr.ln_sems(sem, "2")
        xcT_ps, xc_ready, edge2_ready, sx2_ready, xk2_ready, xr2_ready = (sem(n, per) for n, per in (
            ("xcT_ps", 1), ("xc_ready", 2), ("edge2_ready", 1), ("sx2_ready", 1),
            ("xk2_ready", 2), ("xr2_ready", 2)))
        fk_ps, rk_ready, kk_ready, fr_ps, fs_ready, fv_ps, mo_ready, out_ready = (
            sem(n, 1) for n in ("fk_ps", "rk_ready", "kk_ready", "fr_ps", "fs_ready", 
                                "fv_ps", "mo_ready", "out_ready"))
        start_counts(nc, sems)
        xv, ov = tokens(x_src), tokens(x_dst)

        block = ctx.enter_context(nc.Block())

        @block.sync
        def _(sp):
            def load_x(i):
                sp.wait_ge(ln_s.xn_ready, 2 * i)
                sp.dma_start(x_in[:], xv[i - 1]).then_inc(x_loaded, 16)

            def load_res(i):
                sp.wait_ge(x1_ready, i)
                sp.dma_start(x_res[:], xv[i - 1]).then_inc(res_loaded, 16)

            def store(i):
                sp.wait_ge(out_ready, i + 1)
                sp.dma_start(ov[i - 1], outt[:]).then_inc(stored, 16)

            pr.staggered(sp, [(4, load_x), (1, load_res), (0, store)])
            sp.wait_ge(stored, 16 * TRIPS + 16)

        @block.gpsimd
        def _(pool):
            pool.wait_ge(pr.consts_in, 48)
            nc.gpsimd.memset(w[:, :, :, 0], 0.0).then_inc(setup, 1)
            pool.wait_ge(weights_in, 16 * 7)
            pool.wait_ge(setup, 2)

            def front_norm(i):
                pr.ln_rstd(pool, ln, ln_s, i)
                pool.wait_ge(sx_ready, i)
                nc.gpsimd.nop(nofuse=True)
                nc.gpsimd.tensor_copy(xa[:, :, :, 0], edge[:, :, 1, bass.ds(NB * (i - 1), NB)]
                                      ).then_inc(edge_ready, 1)

            def mixed(i):
                for f in range(F):
                    pool.wait_ge(tf_ready, 2 * F * i + 2 * f + 2)
                    nc.gpsimd.tensor_tensor(
                        xm[f][:].rearrange("p c (b s) -> p c b s", s=S),
                        tf[f][:].rearrange("p c (b s) -> p c b s", s=S), xa[:, :, :, 1:S1],
                        ALU.add).then_inc(xm_ready, 1)

            def initial(i):
                pool.wait_ge(scan_done, HS * i)
                nc.gpsimd.nop(nofuse=True)
                nc.gpsimd.tensor_copy(
                    a[:, :, :, :, 0],
                    state0[:, :, :, bass.ds(NB * (i - 1), NB)].rearrange("p c j b -> p j c b")
                ).then_inc(st0_ready, 1)

            def read_out(j0):
                def step(i):
                    for j in range(j0, j0 + 4):
                        pool.wait_ge(scan_done, HS * i + j + 1)
                        pool.wait_ge(r_ready, i + 1)
                        nc.gpsimd.tensor_tensor(
                            m[:, j, :, :].rearrange("p c (b s) -> p c b s", s=S),
                            rT[:].rearrange("p c (b s) -> p c b s", s=S), st[:, j, :, :, 0:S],
                            ALU.mult).then_inc(m_ready, 1)
                return step

            def square(i):
                pool.wait_ge(cen_ready, i + 1)
                nc.gpsimd.tensor_tensor(sq[:], cen[:], cen[:], ALU.mult).then_inc(sq_ready, 1)

            def gate(i):
                pool.wait_ge(gn_ready, 2 * i + 2)
                pool.wait_ge(wo_ps, i)
                pool.wait_ge(sg_ready, i + 1)
                nc.gpsimd.tensor_tensor(yT[:], og[:], sg[:], ALU.mult).then_inc(y_ready, 1)

            def back_norm(i):
                pr.ln_rstd(pool, ln2, ln2_s, i)
                pool.wait_ge(xr2_ready, 2 * i)
                pool.wait_ge(sx2_ready, i)
                nc.gpsimd.nop(nofuse=True)
                nc.gpsimd.tensor_copy(xc[:, :, :, 0], edge[:, :, 0, bass.ds(NB * (i - 1), NB)]
                                      ).then_inc(edge2_ready, 1)

            def back_shift(i):
                pool.wait_ge(xc_ready, 2 * i + 2)
                pool.wait_ge(edge2_ready, i + 1)
                nc.gpsimd.tensor_tensor(sx2[:], xc[:, :, :, 0:S], xc[:, :, :, 1:S1], ALU.subtract
                                        ).then_inc(sx2_ready, 1)

            def relu_squared(i):
                pool.wait_ge(rk_ready, i + 1)
                nc.gpsimd.tensor_tensor(kk[:], rk[:], rk[:], ALU.mult).then_inc(kk_ready, 1)

            def final(i):
                pool.wait_ge(mo_ready, i + 1)
                pool.wait_ge(stored, 16 * i)
                nc.gpsimd.tensor_tensor(outt[:], rr[:], x1[:], ALU.add).then_inc(out_ready, 1)

            pr.staggered(pool, [(1, initial), (1, read_out(0)), (1, read_out(4)), (0, back_norm),
                                (1, square), (2, mixed), (3, front_norm), (0, back_shift),
                                (0, relu_squared), (1, gate), (0, final)])

        @block.scalar
        def _(act_e):
            for dst, src in (
                    (edge, dram["edgeT"].rearrange("c p (r b) -> p c r b", r=2)),
                    (maa_w1, weight(dram[f"{L}maa_w1"])), (maa_w2a, dram["maa_w2"][0:P, :]),
                    (maa_w2b, dram["maa_w2"][P:P + DM, :]), (td_w1, weight(dram[f"{L}td_w1"])),
                    (td_w2, dram[f"{L}td_w2"]),
                    (state0, dram["state0"].rearrange("p (c j b) -> p c j b", c=DC, j=HS))):
                act_e.dma_start(dst[:], src).then_inc(weights_in, 16)
            for dst, name in ((wk, "Wk"), (wr, "Wr"), (wv, "Wv"), (wg, "Wg"), (wo, "Wo"),
                              (wfk, "Wfk"), (wfr, "Wfr"), (wfv, "Wfv")):
                act_e.dma_start(dst[:], weight(dram[f"{L}{name}"])).then_inc(late_weights_in, 16)
            act_e.wait_ge(pr.consts_in, 48)
            act_e.wait_ge(setup, 2)

            def shift_tanh(i):
                act_e.wait_ge(w1_ps, i + 1)
                act_e.wait_ge(w2_ps, F * i)
                nc.scalar.activation(th[:], PS[:, 5, 0:T], ACT.Tanh).then_inc(th_ready, 1)
                nc.scalar.activation(th4[:], PS[0:DM, 5, T:2 * T], ACT.Tanh).then_inc(th_ready, 1)

            def projected1(i):
                act_e.wait_ge(td1_ps, i + 1)
                nc.scalar.activation(td_t[:], PS[0:DD, 4, 0:T], ACT.Tanh).then_inc(td1_ready, 1)
                act_e.wait_ge(k_ps, i + 1)
                act_e.wait_ge(a_ready, HS * i)
                nc.scalar.copy(kT[:], bank(PS, 5, [DC, T])).then_inc(k_ready, 1)

            def projected2(i):
                act_e.wait_ge(r_ps, i + 1)
                act_e.wait_ge(m_ready, HS * i)
                nc.scalar.copy(rT[:], bank(PS, 7, [DC, T])).then_inc(r_ready, 1)
                act_e.wait_ge(td2_ps, i + 1)
                for c in range(DC):
                    ins = nc.scalar.activation(ew[:, c, :], bank(PS, 6, [DC, T])[:, c, :], ACT.Exp,
                                               bias=pr.col(f"{L}time_decay", c))
                ins.then_inc(ew_ready, 1)
                act_e.wait_ge(ew_ready, i + 1)
                act_e.wait_ge(scan_done, HS * i)
                nc.scalar.activation(w[:, :, :, 1:S1], ew[:].rearrange("p c (b s) -> p c b s", s=S),
                                     ACT.Exp, scale=-1.0).then_inc(w_ready, 1)
                act_e.wait_ge(v_ps, i + 1)
                act_e.wait_ge(vrep_ps, HS * i)
                nc.scalar.copy(vT[:], bank(PS, 4, [DC, T])).then_inc(v_ready, 1)

            def gate(i):
                act_e.wait_ge(g_ps, i + 1)
                act_e.wait_ge(sg_ready, i)
                nc.scalar.copy(gT[:], bank(PS, 5, [DC, T])).then_inc(g_copied, 1)
                nc.scalar.activation(ge[:], bank(PS, 5, [DC, T]), ACT.Sigmoid).then_inc(g_sig, 1)

            def deviation(i):
                act_e.wait_ge(var_ps, i + 1)
                nc.scalar.activation(sd[:], bank(PS, 1, [DC, T]), ACT.Sqrt, scale=1.0 / HS,
                                     bias=eps[:, 0:1]).then_inc(sd_ready, 1)

            def ffn_in(i):
                act_e.wait_ge(fk_ps, i + 1)
                nc.scalar.activation(rk[:], bank(PS, 0, [DC, T]), ACT.Relu).then_inc(rk_ready, 1)
                act_e.wait_ge(fr_ps, i + 1)
                act_e.wait_ge(out_ready, i)
                nc.scalar.activation(rr[:], bank(PS, 1, [NP, D]), ACT.Sigmoid
                                     ).then_inc(fs_ready, 1)

            pr.staggered(act_e, [(2, shift_tanh), (1, deviation), (2, projected1), (2, projected2),
                                 (0, ffn_in), (2, gate)])

        @block.vector
        def _(dve):
            dve.wait_ge(pr.consts_in, 48)
            nc.vector.memset(eps[:], 1e-5).then_inc(setup, 1)

            def front_norm(i):
                dve.wait_ge(x_loaded, 16 * (i + 1))
                dve.wait_ge(xnT_ps, i)
                pr.ln_normalise(dve, ln, ln_s, x_in, xn, i)

            def shift(i):
                dve.wait_ge(xnT_ps, i + 1)
                dve.wait_ge(xm_ready, F * i)
                for c in range(DC):
                    nc.vector.tensor_scalar(xa[:, c, :, 1:S1], bank(PS, 4, [DC, NB, S])[:, c, :, :],
                                            pr.col(f"{L}ln1_w", c), pr.col(f"{L}ln1_b", c),
                                            ALU.mult, ALU.add).then_inc(xa_ready, 1)
                dve.wait_ge(xa_ready, 2 * i + 2)
                dve.wait_ge(edge_ready, i + 1)
                nc.vector.tensor_tensor(sx[:], xa[:, :, :, 0:S], xa[:, :, :, 1:S1], ALU.subtract
                                        ).then_inc(sx_ready, 1)
                dve.wait_ge(sx_ready, i + 1)
                for c in range(DC):
                    nc.vector.scalar_tensor_tensor(
                        out=xx[:, c, :].rearrange("p (b s) -> p b s", s=S), in0=sx[:, c, :, :],
                        scalar=pr.col(f"{L}maa_x", c), in1=xa[:, c, :, 1:S1],
                        op0=ALU.mult, op1=ALU.add).then_inc(xx_ready, 1)

            def mix(i):
                for f in range(F):
                    dve.wait_ge(w2_ps, F * i + f + 1)
                    for c in range(DC):
                        nc.vector.scalar_tensor_tensor(
                            out=tf[f][:, c, :],
                            in0=bank(PS, (6, 7, 4, 5, 6)[f], [DC, T])[:, c, :],
                            scalar=pr.col(f"{L}maa_stack", 2 * f + c),
                            in1=sx[:, c, :, :].rearrange("p b s -> p (b s)"),
                            op0=ALU.add, op1=ALU.mult).then_inc(tf_ready, 1)

            def gate(i):
                dve.wait_ge(k_ready, i + 1)
                dve.wait_ge(r_ready, i + 1)
                for c in range(DC):
                    nc.vector.scalar_tensor_tensor(
                        out=ruk[:, c, :], in0=rT[:, c, :], scalar=pr.col(f"{L}u", c),
                        in1=kT[:, c, :], op0=ALU.mult, op1=ALU.mult).then_inc(ruk_ready, 1)
                dve.wait_ge(g_sig, i + 1)
                dve.wait_ge(y_ready, i)
                nc.vector.tensor_tensor(sg[:], gT[:], ge[:], ALU.mult).then_inc(sg_ready, 1)
                dve.wait_ge(ruk_ps, i + 1)
                dve.wait_ge(v_ready, i + 1)
                nc.vector.tensor_tensor(bonus[:], bank(PS, 6, [DC, T]), vT[:], ALU.mult
                                        ).then_inc(bonus_ready, 1)

            def scan(j0):
                def step(i):
                    for j in range(j0, j0 + 4):
                        dve.wait_ge(vrep_ps, HS * i + j + 1)
                        nc.vector.tensor_tensor(
                            a[:, j, :, :, 1:S1], kT[:].rearrange("p c (b s) -> p c b s", s=S),
                            bank(PS, j % 2, [DC, NB, S]), ALU.mult).then_inc(a_ready, 1)
                        dve.wait_ge(a_ready, HS * i + j + 1)
                        dve.wait_ge(st0_ready, i + 1)
                        dve.wait_ge(w_ready, i + 1)
                        dve.wait_ge(m_ready, HS * i)
                        dve.nop(nofuse=True)
                        nc.vector.tensor_tensor_scan(
                            st[:, j, :, :, :].rearrange("p c b s -> p (c b s)"),
                            w[:].rearrange("p c b s -> p (c b s)"),
                            a[:, j, :, :, :].rearrange("p c b s -> p (c b s)"),
                            0.0, ALU.mult, ALU.add).then_inc(scan_done, 1)
                return step

            def mean(i):
                dve.wait_ge(gat_ps, i + 1)
                dve.wait_ge(y_ready, i)
                nc.vector.tensor_tensor(og[:], PS[:, 2:4, 0:T], bonus[:], ALU.add
                                        ).then_inc(og_ready, 1)

            def centre(i):
                dve.wait_ge(mean_ps, i + 1)
                nc.vector.scalar_tensor_tensor(
                    out=cen[:], in0=bank(PS, 0, [DC, T]), scalar=-1.0 / HS, in1=og[:],
                    op0=ALU.mult, op1=ALU.add).then_inc(cen_ready, 1)

            def group_norm(i):
                dve.wait_ge(sd_ready, i + 1)
                nc.vector.reciprocal(rstd[:], sd[:]).then_inc(rstd_ready, 1)
                dve.wait_ge(rstd_ready, i + 1)
                nc.vector.tensor_tensor(cen[:], cen[:], rstd[:], ALU.mult).then_inc(cn_ready, 1)
                dve.wait_ge(cn_ready, i + 1)
                for c in range(DC):
                    nc.vector.tensor_scalar(og[:, c, :], cen[:, c, :], pr.col(f"{L}gn_w", c),
                                            pr.col(f"{L}gn_b", c), ALU.mult, ALU.add
                                            ).then_inc(gn_ready, 1)

            def back_norm(i):
                dve.wait_ge(wo_ps, i + 1)
                dve.wait_ge(res_loaded, 16 * (i + 1))
                dve.wait_ge(out_ready, i)
                nc.vector.tensor_tensor(x1[:], bank(PS, 2, [NP, D]), x_res[:], ALU.add
                                        ).then_inc(x1_ready, 1)
                dve.wait_ge(x1_ready, i + 1)
                dve.wait_ge(xcT_ps, i)
                pr.ln_normalise(dve, ln2, ln2_s, x1, x1n, i)

            def back_shift(i):
                dve.wait_ge(xcT_ps, i + 1)
                for c in range(DC):
                    nc.vector.tensor_scalar(xc[:, c, :, 1:S1], bank(PS, 3, [DC, NB, S])[:, c, :, :],
                                            pr.col(f"{L}ln2_w", c), pr.col(f"{L}ln2_b", c),
                                            ALU.mult, ALU.add).then_inc(xc_ready, 1)
                dve.wait_ge(sx2_ready, i + 1)
                for dst, name, done in ((xk2, "ffn_maa_k", xk2_ready), (xr2, "ffn_maa_r", xr2_ready)):
                    for c in range(DC):
                        nc.vector.scalar_tensor_tensor(
                            out=dst[:, c, :].rearrange("p (b s) -> p b s", s=S),
                            in0=sx2[:, c, :, :], scalar=pr.col(f"{L}{name}", c),
                            in1=xc[:, c, :, 1:S1], op0=ALU.mult, op1=ALU.add).then_inc(done, 1)

            def receptance(i):
                dve.wait_ge(fs_ready, i + 1)
                dve.wait_ge(fv_ps, i + 1)
                nc.vector.tensor_tensor(rr[:], bank(PS, 2, [NP, D]), rr[:], ALU.mult
                                        ).then_inc(mo_ready, 1)

            pr.staggered(dve, [(1, scan(0)), (1, scan(4)), (2, shift), (1, mean), (0, back_norm),
                               (1, centre), (2, mix), (3, front_norm), (0, back_shift),
                               (1, group_norm), (2, gate), (0, receptance)])

        @block.tensor
        def _(pe):
            pe.wait_ge(pr.consts_in, 48)
            pe.wait_ge(setup, 2)

            def front_turn(i):
                pe.wait_ge(v_ready, i)
                pe.wait_ge(ln_s.xn_ready, 2 * i + 2)
                pr.transpose_tiles(xn, 4).then_inc(xnT_ps, 1)

            def shift_in(i):
                pe.wait_ge(weights_in, 16 * 7)
                pe.wait_ge(g_copied, i)
                pe.wait_ge(g_sig, i)
                pe.wait_ge(xx_ready, 2 * i + 2)
                for c in range(DC):
                    nc.tensor.matmul(PS[:, 5, 0:T], maa_w1[:, c, 0:P], xx[:, c, :],
                                     start=(c == 0), stop=(c == 1))
                for c in range(DC):
                    mm = nc.tensor.matmul(PS[0:DM, 5, T:2 * T], maa_w1[:, c, P:P + DM], xx[:, c, :],
                                          start=(c == 0), stop=(c == 1))
                mm.then_inc(w1_ps, 1)

            def mix(i):
                pe.wait_ge(th_ready, 2 * i + 2)
                pe.wait_ge(bonus_ready, i)
                pe.wait_ge(r_ready, i)
                for f in range(F):
                    rows = slice(DM * f, DM * f + DM) if f < 4 else slice(0, DM)
                    w2, src = (maa_w2a, th) if f < 4 else (maa_w2b, th4)
                    if f == 4:
                        pe.wait_ge(tf_ready, 10 * i + 2)
                    for c in range(DC):
                        mm = nc.tensor.matmul(bank(PS, (6, 7, 4, 5, 6)[f], [DC, T])[:, c, :],
                                              w2[rows, c * P:(c + 1) * P], src[rows, :],
                                              start=True, stop=True)
                    mm.then_inc(w2_ps, 1)

            def projections1(i):
                pe.wait_ge(tf_ready, 10 * i + 6)
                pe.wait_ge(xm_ready, F * i + 2)
                for c in range(DC):
                    mm = nc.tensor.matmul(PS[0:DD, 4, 0:T], td_w1[:, c, :], xm[1][:, c, :],
                                          start=(c == 0), stop=(c == 1))
                mm.then_inc(td1_ps, 1)
                pe.wait_ge(late_weights_in, 16 * 8)
                pe.wait_ge(tf_ready, 10 * i + 10)
                pr.project_T(wk, xm[0], 5, DC).then_inc(k_ps, 1)

            def projections2(i):
                pe.wait_ge(xm_ready, F * i + 4)
                pr.project_T(wr, xm[3], 7, DC).then_inc(r_ps, 1)
                pe.wait_ge(td1_ready, i + 1)
                for c in range(DC):
                    mm = nc.tensor.matmul(bank(PS, 6, [DC, T])[:, c, :],
                                          td_w2[:, c * P:(c + 1) * P], td_t[:],
                                          start=True, stop=True)
                mm.then_inc(td2_ps, 1)
                pr.project_T(wv, xm[2], 4, DC).then_inc(v_ps, 1)

            def projections3(i):
                pe.wait_ge(xm_ready, F * i + 5)
                pe.wait_ge(k_ready, i + 1)
                pr.project_T(wg, xm[4], 5, DC).then_inc(g_ps, 1)
                pe.wait_ge(ew_ready, i + 1)
                pe.wait_ge(ruk_ready, 2 * i + 2)
                for c in range(DC):
                    mm = nc.tensor.matmul(bank(PS, 6, [DC, T])[:, c, :], pr.same_head,
                                          ruk[:, c, :], start=True, stop=True)
                mm.then_inc(ruk_ps, 1)

            def spread(i, j):
                for c in range(DC):
                    mm = nc.tensor.matmul(bank(PS, j % 2, [DC, T])[:, c, :], pr.spread[:, j, :],
                                          vT[:, c, :], start=True, stop=True)
                mm.then_inc(vrep_ps, 1)

            def gather(i, j):
                pe.wait_ge(m_ready, HS * i + j + 1)
                for c in range(DC):
                    mm = nc.tensor.matmul(PS[:, 2 + c, 0:T], pr.gather[:, j, :], m[:, j, c, :],
                                          start=(j == 0), stop=(j == HS - 1))
                if j == HS - 1:
                    mm.then_inc(gat_ps, 1)

            def states1(i):
                pe.wait_ge(v_ready, i + 1)
                if not first_trip(i):
                    pe.wait_ge(rk_ready, i - 1)
                    pe.wait_ge(fs_ready, i - 1)
                    pe.wait_ge(mo_ready, i - 1)
                    pe.wait_ge(xc_ready, 2 * i - 2)
                for j in range(4):
                    if j >= 2:
                        pe.wait_ge(a_ready, HS * i + j - 1)
                    spread(i, j)
                gather(i, 0)

            def states2(i):
                for j in range(4, 8):
                    pe.wait_ge(a_ready, HS * i + j - 1)
                    spread(i, j)
                    gather(i, j - 3)

            def states3(i):
                for j in range(5, 8):
                    gather(i, j)

            def mean(i):
                pe.wait_ge(og_ready, i + 1)
                for c in range(DC):
                    mm = nc.tensor.matmul(bank(PS, 0, [DC, T])[:, c, :], pr.same_head,
                                          og[:, c, :], start=True, stop=True)
                mm.then_inc(mean_ps, 1)

            def variance(i):
                pe.wait_ge(sq_ready, i + 1)
                for c in range(DC):
                    mm = nc.tensor.matmul(bank(PS, 1, [DC, T])[:, c, :], pr.same_head,
                                          sq[:, c, :], start=True, stop=True)
                mm.then_inc(var_ps, 1)

            def out_projection(i):
                if last_trip(i):
                    pe.wait_ge(rk_ready, i)
                    pe.wait_ge(fs_ready, i)
                    pe.wait_ge(mo_ready, i)
                    pe.wait_ge(xc_ready, 2 * i)
                pe.wait_ge(y_ready, i + 1)
                pr.project_rows(yT, wo, 2, DC).then_inc(wo_ps, 1)

            def back_turn(i):
                pe.wait_ge(ln2_s.xn_ready, 2 * i + 2)
                pr.transpose_tiles(x1n, 3).then_inc(xcT_ps, 1)

            def ffn_in(i):
                pe.wait_ge(xk2_ready, 2 * i + 2)
                pr.project_T(wfk, xk2, 0, DC).then_inc(fk_ps, 1)
                pe.wait_ge(xr2_ready, 2 * i + 2)
                if not last_trip(i):
                    pe.wait_ge(sd_ready, i + 2)
                pr.project_rows(xr2, wfr, 1, DC).then_inc(fr_ps, 1)

            def ffn_out(i):
                pe.wait_ge(kk_ready, i + 1)
                pr.project_rows(kk, wfv, 2, DC).then_inc(fv_ps, 1)

            pr.staggered(pe, [(2, front_turn), (1, states1), (1, states2), (1, states3),
                              (2, shift_in), (1, mean), (0, out_projection), (2, mix),
                              (1, variance), (2, projections1), (0, back_turn), (2, projections2),
                              (0, ffn_in), (2, projections3), (0, ffn_out)])



def stage_cross(pr, x_src, x_dst, x_res_src, tag, half):
    nc, dram, PS = pr.nc, pr.dram, pr.psum
    H, HD = 8, 128
    H0 = H * half
    WIDTH = H * HD
    NU = H // 2
    NG = H // 4
    SCALE = 1.0 / math.sqrt(HD)
    K1 = S + 1
    L = "L2_xattn_"
    with ExitStack() as ctx:
        def sb(name, shape, dt=F32):
            return ctx.enter_context(nc.sbuf_tensor(f"x{tag}{half}_{name}", shape, dt))

        sems = []

        def sem(name, per):
            s = ctx.enter_context(nc.semaphore(f"x{tag}{half}_{name}"))
            sems.append((s, per))
            return s

        raw = [sb(f"raw{n}", [P, DC * WIDTH]) for n in range(2)]
        wk, wq, wv = ([sb(f"{n}_{part}", [P, DC, WIDTH], F32R) for part in ("hi", "lo")]
                      for n in ("wk", "wq", "wv"))
        wo = [sb(f"wo_{part}", [P, H, D], F32R) for part in ("hi", "lo")]
        bv_row = sb("bv_row", [P, WIDTH])
        bq_scaled = sb("bq_scaled", [P, H])
        bias_v_diag = sb("bias_v_diag", [P, H, H])
        bias_vo = sb("bias_vo", [H, D])
        x_in = sb("x_in", [P, NP, D])
        x_res = sb("x_res", [P, NP, D])
        ctxT = sb("ctxT", [P, DC, T])
        ctx_k = [sb(f"ctx_k_{part}", [P, DC, T], F32R) for part in ("hi", "lo")]
        ctx_v = [sb(f"ctx_v_{part}", [P, DC, T], F32R) for part in ("hi", "lo")]
        ln = pr.ln_tiles(sb)
        xn = sb("xn", [P, NP, D])
        hT = sb("hT", [P, DC, T])
        h_split = [sb(f"h_{part}", [P, DC, T], F32R) for part in ("hi", "lo")]
        qT = sb("qT", [P, H, T])
        kT = sb("kT", [P, H, NB, K1])
        v = sb("v", [P, NP, WIDTH])
        sc = [sb(f"sc{t}", [P, H, K1]) for t in range(NP)]
        pn = [sb(f"pn{t}", [P, H, S]) for t in range(NP)]
        px = sb("px", [P, NP, H])
        mx = sb("mx", [P, NP, H])
        sm = sb("sm", [P, NP, H])
        rs = sb("rs", [P, NP, H])
        pT = [sb(f"pT{t}", [P, H, P]) for t in range(NP)]
        p_extra = sb("p_extra", [H, NP, P])
        oT = [sb(f"oT_{part}", [P, H, T], F32R) for part in ("hi", "lo")]
        xb = sb("xb", [P, NP, D])
        outt = sb("outt", [P, NP, D])

        raw_in = [sem(f"raw_{n}_in", 0) for n in ("wk", "wq", "wv", "wo")]
        w_hi, w_lo, bv_in = (sem(n, 0) for n in ("w_hi", "w_lo", "bv_in"))
        setup, bias_ps, bias_vo_ready = (sem(n, 0) for n in ("setup", "bias_ps", "bias_vo_ready"))
        x_loaded, ctx_loaded, res_loaded = (sem(n, 16) for n in
                                            ("x_loaded", "ctx_loaded", "res_loaded"))
        stored = sem("stored", 16)
        ctx_k_hi, ctx_k_lo, ctx_v_hi, ctx_v_lo = (sem(n, 1) for n in (
            "ctx_k_hi", "ctx_k_lo", "ctx_v_hi", "ctx_v_lo"))
        ln_s = pr.ln_sems(sem)
        xnT_ps, hT_ready, h_hi, h_lo = sem("xnT_ps", 1), sem("hT_ready", 2), sem("h_hi", 1), sem(
            "h_lo", 1)
        k_ps, k_ready, q_ps, q_ready = (sem(n, per) for n, per in (
            ("k_ps", NU), ("k_ready", H), ("q_ps", NU), ("q_ready", H)))
        v_ps, v_ready = sem("v_ps", NP * NG), sem("v_ready", NP * NG)
        s_ps, s_max, s_sub, s_exp, s_sum, s_rec, p_ready = (sem(n, NP) for n in (
            "s_ps", "s_max", "s_sub", "s_exp", "s_sum", "s_rec", "p_ready"))
        pT_ps, pT_ready = sem("pT_ps", NP), [sem(f"pT{t}_ready", 4) for t in range(NP)]
        px_ready = sem("px_ready", NP)
        pe_ps, p_extra_ready = sem("pe_ps", 1), sem("p_extra_ready", 1)
        o_ps, o_hi, o_lo = (sem(n, NP * NG) for n in ("o_ps", "o_hi", "o_lo"))
        y_ps, xb_ready, out_ready = sem("y_ps", 1), sem("xb_ready", 1), sem("out_ready", 1)
        start_counts(nc, sems)
        xv, rv, ov = tokens(x_src), tokens(x_res_src), tokens(x_dst)
        cv = dram["ctxT"].rearrange("(c p) (g t) -> g p c t", p=P, t=T)
        cols = slice(WIDTH * half, WIDTH * (half + 1))
        sources = [weight(dram[f"{L}{n}{tag}"])[:, :, cols] for n in ("wk", "wq", "wv")] + [
            weight(dram[f"{L}wo{tag}"])[:, H0:H0 + H, :]]
        split = [wk, wq, wv, wo]

        def all_heads(name):
            return pr.cols_of(f"{L}{name}{tag}")[:, H0:H0 + H]

        def raw_as(n):
            return raw[n % 2][:].rearrange("p (c n) -> p c n", c=(DC if n < 3 else H))

        def block_diagonal(t, b2, hh):
            own, keys = slice(64 * b2, 64 * b2 + 64), slice(64 * hh, 64 * hh + 64)
            return pT[t][own, hh:H:2, own], bank(PS, 2 * t, [NU, P])[keys, :, own]

        def only_first(step):
            def guarded(i):
                if first_trip(i):
                    step()
            return guarded

        block = ctx.enter_context(nc.Block())

        @block.sync
        def _(sp):
            def load_x(i):
                sp.wait_ge(ln_s.xn_ready, 2 * i)
                sp.dma_start(x_in[:], xv[i - 1]).then_inc(x_loaded, 16)

            def load_ctx(i):
                sp.wait_ge(ctx_v_lo, i)
                sp.dma_start(ctxT[:], cv[i - 1]).then_inc(ctx_loaded, 16)

            def load_res(i):
                sp.wait_ge(xb_ready if half == 0 else out_ready, i)
                sp.dma_start(x_res[:], rv[i - 1]).then_inc(res_loaded, 16)

            def load_bias():
                sp.dma_start(bv_row[:], dram[f"{L}bv{tag}"][0, cols].partition_broadcast(P)
                             ).then_inc(bv_in, 16)

            def store(i):
                sp.wait_ge(out_ready, i + 1)
                sp.dma_start(ov[i - 1], outt[:]).then_inc(stored, 16)

            pr.staggered(sp, [(3, load_ctx), (3, load_x), (2, only_first(load_bias)),
                              (1, load_res), (0, store)])
            sp.wait_ge(stored, 16 * TRIPS + 16)

        @block.gpsimd
        def _(pool):
            pool.wait_ge(pr.consts_in, 48)
            nc.gpsimd.memset(pT[0][:], 0.0).then_inc(setup, 1)
            nc.gpsimd.memset(pT[1][:], 0.0).then_inc(setup, 1)

            def split_ctx(parts, hi_done, lo_done, i):
                nc.gpsimd.nop(nofuse=True)
                nc.gpsimd.tensor_copy(parts[0][:], ctxT[:]).then_inc(hi_done, 1)
                pool.wait_ge(hi_done, i + 1)
                nc.gpsimd.tensor_tensor(parts[1][:], ctxT[:], parts[0][:].bitcast(F32),
                                        ALU.subtract).then_inc(lo_done, 1)

            def ctx_for_k(i):
                pool.wait_ge(ctx_loaded, 16 * (i + 1))
                pool.wait_ge(k_ps, NU * i)
                split_ctx(ctx_k, ctx_k_hi, ctx_k_lo, i)

            def ctx_for_v(i):
                pool.wait_ge(v_ps, NP * NG * i)
                split_ctx(ctx_v, ctx_v_hi, ctx_v_lo, i)

            def rstd(i):
                pr.ln_rstd(pool, ln, ln_s, i)

            def residual(i):
                pool.wait_ge(res_loaded, 16 * (i + 1))
                pool.wait_ge(out_ready, i)
                nc.gpsimd.tensor_tensor(xb[:], x_res[:], pr.row(f"{L}bo{tag}", NP), ALU.add
                                        ).then_inc(xb_ready, 1)

            def normalise(t):
                def step(i):
                    pool.wait_ge(s_rec, 2 * i + t + 1)
                    pool.wait_ge(pT_ps, 2 * i + t - 1)
                    nc.gpsimd.tensor_tensor(pn[t][:], sc[t][:, :, 0:S],
                                            rs[:, t, :].unsqueeze(2).to_broadcast([P, H, S]),
                                            ALU.mult).then_inc(p_ready, 1)
                    pool.wait_ge(pe_ps, i)
                    nc.gpsimd.tensor_tensor(px[:, t, :], sc[t][:, :, S], rs[:, t, :], ALU.mult
                                            ).then_inc(px_ready, 1)
                return step

            pr.staggered(pool, [(1, normalise(0)), (1, normalise(1)), (2, rstd), (2, ctx_for_v)]
                         + ([(1, residual)] if half == 0 else []) + [(3, ctx_for_k)])

        @block.scalar
        def _(act_e):
            def load_weight(n):
                act_e.dma_start(raw_as(n), sources[n]).then_inc(raw_in[n], 16)

            def weight_hi(n):
                act_e.wait_ge(raw_in[n], 16)
                nc.scalar.copy(split[n][0][:], raw_as(n)).then_inc(w_hi, 1)

            load_weight(0)
            load_weight(1)
            weight_hi(0)
            weight_hi(1)
            act_e.wait_ge(w_lo, 1)
            load_weight(2)
            act_e.wait_ge(w_lo, 2)
            load_weight(3)
            act_e.wait_ge(pr.consts_in, 48)
            act_e.wait_ge(setup, 6)

            def late_weights():
                weight_hi(2)
                weight_hi(3)

            def keys(i):
                for h in range(H):
                    act_e.wait_ge(k_ps, NU * i + h // 2 + 1)
                    nc.scalar.activation(kT[:, h, :, 0:S],
                                         bank(PS, 4 + h // 2, [2, NB, S])[:, h % 2, :, :],
                                         ACT.Identity, bias=pr.col(f"{L}bk{tag}", H0 + h)).then_inc(k_ready, 1)

            def queries(i):
                for h in range(H):
                    act_e.wait_ge(q_ps, NU * i + h // 2 + 1)
                    nc.scalar.activation(qT[:, h, :], bank(PS, 4 + h // 2, [2, T])[:, h % 2, :],
                                         ACT.Identity, bias=bq_scaled[:, h:h + 1], scale=SCALE
                                         ).then_inc(q_ready, 1)

            def exps(t):
                def step(i):
                    act_e.wait_ge(s_sub, 2 * i + t + 1)
                    nc.scalar.activation(sc[t][:], sc[t][:], ACT.Exp).then_inc(s_exp, 1)
                return step

            def turned(i):
                act_e.wait_ge(pT_ps, 2 * i + 2)
                for b2 in range(2):
                    for hh in range(2):
                        dst, src = block_diagonal(1, b2, hh)
                        nc.scalar.copy(dst, src).then_inc(pT_ready[1], 1)

            def attended_hi(i):
                for n in range(NP * NG):
                    act_e.wait_ge(o_ps, NP * NG * i + n + 1)
                    t, h = n // NG, n % NG * 4
                    nc.scalar.copy(oT[0][:, h:h + 4, t * P:(t + 1) * P],
                                   bank(PS, (5, 6, 7, 0)[n], [4, P])).then_inc(o_hi, 1)

            pr.staggered(act_e, [(1, exps(0)), (1, exps(1)), (2, keys), (1, turned),
                                 (1, attended_hi), (2, queries), (2, only_first(late_weights))])

        @block.vector
        def _(dve):
            dve.wait_ge(pr.consts_in, 48)
            def weight_lo(n):
                dve.wait_ge(w_hi, n + 1)
                nc.vector.tensor_tensor(split[n][1][:], raw_as(n), split[n][0][:].bitcast(F32),
                                        ALU.subtract).then_inc(w_lo, 1)

            nc.vector.tensor_scalar(bq_scaled[:], all_heads("bq"), SCALE, None, ALU.mult
                                    ).then_inc(setup, 1)
            nc.vector.tensor_copy(kT[:, :, :, S], all_heads("bias_k").unsqueeze(2)
                                  .to_broadcast([P, H, NB])).then_inc(setup, 1)
            nc.vector.memset(bias_v_diag[:], 0.0).then_inc(setup, 1)
            dve.wait_ge(setup, 5)
            nc.vector.tensor_copy(bias_v_diag[:].rearrange("p a b -> p (a b)")[:, 0:H * H:H + 1],
                                  all_heads("bias_v")).then_inc(setup, 1)
            weight_lo(0)
            weight_lo(1)

            def late_weights():
                dve.wait_ge(bias_ps, 1)
                nc.vector.tensor_copy(bias_vo[:], PS[0:H, 0, 0:D]).then_inc(bias_vo_ready, 1)
                weight_lo(2)
                weight_lo(3)

            def norm(i):
                dve.wait_ge(x_loaded, 16 * (i + 1))
                dve.wait_ge(xnT_ps, i)
                pr.ln_normalise(dve, ln, ln_s, x_in, xn, i)

            def weighted(i):
                dve.wait_ge(xnT_ps, i + 1)
                for c in range(DC):
                    nc.vector.tensor_scalar(hT[:, c, :], bank(PS, 3, [DC, T])[:, c, :],
                                            pr.col(f"{L}ln{tag}_scale", c),
                                            pr.col(f"{L}ln{tag}_offset", c),
                                            ALU.mult, ALU.add).then_inc(hT_ready, 1)
                dve.wait_ge(hT_ready, 2 * i + 2)
                dve.wait_ge(q_ps, NU * i)
                dve.nop(nofuse=True)
                nc.vector.tensor_copy(h_split[0][:], hT[:]).then_inc(h_hi, 1)
                dve.wait_ge(h_hi, i + 1)
                nc.vector.tensor_tensor(h_split[1][:], hT[:], h_split[0][:].bitcast(F32),
                                        ALU.subtract).then_inc(h_lo, 1)

            def softmax_in(t):
                def step(i):
                    dve.wait_ge(s_ps, 2 * i + t + 1)
                    ps = PS[:, NG * t:NG * t + NG, 0:4 * K1].rearrange(
                        "p r (h k) -> p r h k", k=K1)
                    nc.vector.tensor_reduce(mx[:, t, :].rearrange("p (r h) -> p r h", r=NG), ps,
                                            AX.X, ALU.max).then_inc(s_max, 1)
                    dve.wait_ge(s_max, 2 * i + t + 1)
                    nc.vector.tensor_tensor(
                        sc[t][:].rearrange("p (r h) k -> p r h k", r=NG), ps,
                        mx[:, t, :].rearrange("p (r h) -> p r h", r=NG).unsqueeze(3)
                        .to_broadcast([P, NG, 4, K1]), ALU.subtract).then_inc(s_sub, 1)
                return step

            def softmax_sum(t):
                def step(i):
                    dve.wait_ge(s_exp, 2 * i + t + 1)
                    nc.vector.tensor_reduce(sm[:, t, :], sc[t][:], AX.X, ALU.add
                                            ).then_inc(s_sum, 1)
                    dve.wait_ge(s_sum, 2 * i + t + 1)
                    nc.vector.reciprocal(rs[:, t, :], sm[:, t, :]).then_inc(s_rec, 1)
                return step

            def values(t):
                def step(i):
                    dve.wait_ge(bv_in, 16)
                    for g in range(NG):
                        n = NG * t + g
                        dve.wait_ge(v_ps, NP * NG * i + n + 1)
                        out = slice(512 * g, 512 * g + 512)
                        nc.vector.tensor_tensor(v[:, t, out], PS[:, 4 + n, :], bv_row[:, out],
                                                ALU.add).then_inc(v_ready, 1)
                return step

            def turned(i):
                dve.wait_ge(pT_ps, 2 * i + 1)
                for b2 in range(2):
                    for hh in range(2):
                        dst, src = block_diagonal(0, b2, hh)
                        nc.vector.tensor_copy(dst, src).then_inc(pT_ready[0], 1)

            def attended_lo(i):
                for n in range(NP * NG):
                    dve.wait_ge(o_hi, NP * NG * i + n + 1)
                    t, h = n // NG, n % NG * 4
                    part = (slice(None), slice(h, h + 4), slice(t * P, (t + 1) * P))
                    nc.vector.tensor_tensor(oT[1][part], bank(PS, (5, 6, 7, 0)[n], [4, P]),
                                            oT[0][part].bitcast(F32), ALU.subtract
                                            ).then_inc(o_lo, 1)

            def extra(i):
                dve.wait_ge(pe_ps, i + 1)
                nc.vector.tensor_copy(p_extra[:], bank(PS, 1, [4, P])[0:H, 0:NP, :]
                                      ).then_inc(p_extra_ready, 1)

            def output(i):
                dve.wait_ge(y_ps, i + 1)
                if half == 0:
                    dve.wait_ge(xb_ready, i + 1)
                else:
                    dve.wait_ge(res_loaded, 16 * (i + 1))
                dve.wait_ge(stored, 16 * i)
                base = xb if half == 0 else x_res
                nc.vector.tensor_tensor(outt[:], bank(PS, 1, [NP, D]), base[:], ALU.add
                                        ).then_inc(out_ready, 1)

            pr.staggered(dve, [(1, softmax_in(0)), (1, softmax_in(1)), (1, softmax_sum(0)),
                               (1, values(0)), (1, softmax_sum(1)), (1, values(1)), (2, norm),
                               (0, output), (1, turned), (2, weighted),
                               (2, only_first(late_weights)), (1, extra), (1, attended_lo)])

        @block.tensor
        def _(pe):
            pe.wait_ge(pr.consts_in, 48)
            pe.wait_ge(setup, 6)

            def product3(out, w_parts, x_parts, pick_w, pick_x, chunks, last=True):
                terms = [(c, a, b) for a, b in ((0, 1), (1, 0), (0, 0)) for c in range(chunks)]
                for n, (c, a, b) in enumerate(terms):
                    mm = nc.tensor.matmul(out, pick_w(w_parts[a], c), pick_x(x_parts[b], c),
                                          start=(n == 0), stop=(last and n == len(terms) - 1))
                return mm

            def project(w, x_parts, u):
                for h in range(2 * u, 2 * u + 2):
                    mm = product3(bank(PS, 4 + u, [2, T])[:, h % 2, :], w, x_parts,
                                  lambda a, c: a[:, c, h * HD:(h + 1) * HD],
                                  lambda b, c: b[:, c, :], DC)
                return mm

            def keys(i):
                pe.wait_ge(w_lo, 1)
                pe.wait_ge(ctx_k_lo, i + 1)
                for u in range(NU):
                    pe.wait_ge(v_ready, NP * NG * (i - 1) + u + 1)
                    project(wk, ctx_k, u).then_inc(k_ps, 1)

            def turn_norm(i):
                pe.wait_ge(ln_s.xn_ready, 2 * i + 2)
                pr.transpose_tiles(xn, 3).then_inc(xnT_ps, 1)

            def queries(i):
                pe.wait_ge(w_lo, 2)
                pe.wait_ge(h_lo, i + 1)
                for u in range(NU):
                    if u >= 1:
                        pe.wait_ge(o_lo, NP * NG * (i - 1) + u)
                    pe.wait_ge(k_ready, H * i + 2 * u + 2)
                    project(wq, h_split, u).then_inc(q_ps, 1)

            def extra_value():
                pe.wait_ge(raw_in[3], 16)
                for h in range(H):
                    mm = nc.tensor.matmul(PS[0:H, 0, 0:D], bias_v_diag[:, h, :],
                                          raw_as(3)[:, h, :], start=(h == 0), stop=(h == H - 1))
                mm.then_inc(bias_ps, 1)

            def scores(t):
                def step(i):
                    pe.wait_ge(bias_vo_ready, 1)
                    pe.wait_ge(o_lo, NP * NG * i)
                    pe.wait_ge(p_extra_ready, i)
                    for h in range(H):
                        pe.wait_ge(q_ready, H * i + h + 1)
                        for b2 in range(2):
                            b = 2 * t + b2
                            mm = nc.tensor.matmul(
                                PS[64 * b2:64 * b2 + 64, NG * t + h // 4,
                                   h % 4 * K1:(h % 4 + 1) * K1],
                                qT[:, h, b * S:(b + 1) * S], kT[:, h, b, :],
                                start=True, stop=True)
                    mm.then_inc(s_ps, 1)
                return step

            def values(i):
                pe.wait_ge(w_lo, 3)
                pe.wait_ge(ctx_v_lo, i + 1)
                for n in range(NP * NG):
                    t, g = n // NG, n % NG
                    product3(PS[:, 4 + n, :], ctx_v, wv,
                             lambda a, c: a[:, c, t * P:(t + 1) * P],
                             lambda b, c: b[:, c, 512 * g:512 * g + 512], DC).then_inc(v_ps, 1)

            def turn_extra(i):
                pe.wait_ge(out_ready, i)
                pe.wait_ge(px_ready, 2 * i + 2)
                for t in range(NP):
                    mm = nc.tensor.transpose(bank(PS, 1, [4, P])[0:H, t, :], px[:, t, :],
                                             pr.ident)
                mm.then_inc(pe_ps, 1)

            def turn(t):
                def step(i):
                    pe.wait_ge(p_ready, 2 * i + t + 1)
                    for n in range(NU):
                        mm = nc.tensor.transpose(bank(PS, 2 * t, [NU, P])[:, n, :],
                                                 pn[t][:, 2 * n:2 * n + 2, :].rearrange(
                                                     "p h k -> p (h k)"), pr.ident)
                    mm.then_inc(pT_ps, 1)
                return step

            def attend(i):
                pe.wait_ge(v_ready, NP * NG * i + NP * NG)
                for n in range(NP * NG):
                    t = n // NG
                    pe.wait_ge(pT_ready[t], 4 * i + 4)
                    if not last_trip(i) and n < 3:
                        pe.wait_ge(k_ready, H * (i + 1) + 2 * n + 4)
                    for h in range(n % NG * 4, n % NG * 4 + 4):
                        mm = nc.tensor.matmul(bank(PS, (5, 6, 7, 0)[n], [4, P])[:, h % 4, :],
                                              v[:, t, h * HD:(h + 1) * HD], pT[t][:, h, :],
                                              start=True, stop=True)
                    mm.then_inc(o_ps, 1)

            def output(i):
                pe.wait_ge(w_lo, 4)
                pe.wait_ge(p_extra_ready, i + 1)
                pe.wait_ge(o_lo, NP * NG * i + NP * NG)
                if not last_trip(i):
                    pe.wait_ge(s_sub, NP * (i + 1) + 1)
                for t in range(NP):
                    y = bank(PS, 1, [NP, D])[:, t, :]
                    product3(y, oT, wo, lambda a, h: a[:, h, t * P:(t + 1) * P],
                             lambda b, h: b[:, h, :], H, last=False)
                    mm = nc.tensor.matmul(y, p_extra[:, t, :], bias_vo[:], start=False, stop=True)
                mm.then_inc(y_ps, 1)

            pr.staggered(pe, [(1, scores(0)), (1, scores(1)), (1, values), (0, output), (2, keys),
                              (1, turn(0)), (1, turn(1)), (1, turn_extra), (2, turn_norm),
                              (1, attend), (2, queries), (2, only_first(extra_value))])


def stage_cross1(pr, x_src, x_dst):
    stage_cross(pr, x_src, pr.half_done, x_src, 1, 0)
    stage_cross(pr, x_src, x_dst, pr.half_done, 1, 1)


def stage_cross2(pr, x_src, x_dst):
    stage_cross(pr, x_src, pr.half_done, x_src, 2, 0)
    stage_cross(pr, x_src, x_dst, pr.half_done, 2, 1)



def stage_l3(pr, x_src, x_dst):
    nc, dram, PS = pr.nc, pr.dram, pr.psum
    H, KVH, HD = 32, 8, 8
    G = H // KVH
    SCALE = 1.0 / math.sqrt(HD)
    RG = 4
    L, M = "L3_xattn_", "L2_xattn_"
    with ExitStack() as ctx:
        def sb(name, shape, dt=F32):
            return ctx.enter_context(nc.sbuf_tensor("l3_" + name, shape, dt))

        sems = []

        def sem(name, per):
            s = ctx.enter_context(nc.semaphore("l3_" + name))
            sems.append((s, per))
            return s

        wfc = sb("wfc", [P, DC, INNER])
        wproj = sb("wproj", [P, MC, D])
        wq, wk, wo = (sb(n, [P, DC, D]) for n in ("wq", "wk", "wo"))
        wv = sb("wv", [P, DC, KVH * HD])
        bq_scaled = sb("bq_scaled", [P, DC])
        x_in = sb("x_in", [P, NP, D])
        x_res = sb("x_res", [P, NP, D])
        ctxT = sb("ctxT", [P, DC, NB, 2, S])
        mask = sb("mask", [P, NP, S])
        ln = pr.ln_tiles(sb)
        xn = sb("xn", [P, NP, D])
        hT = sb("hT", [P, DC, T])
        act = sb("act", [P, MC, T])
        xb = sb("xb", [P, NP, D])
        x3 = sb("x3", [P, NP, D])
        x3b = sb("x3b", [P, NP, D])
        x3T = sb("x3T", [P, DC, T])
        qT = sb("qT", [P, DC, T])
        k_blk = sb("k_blk", [P, DC, NB, G, S])
        v_blk = sb("v_blk", [P, NB, KVH, 2, G, HD])
        sc = [sb(f"sc{t}", [P, H, S]) for t in range(NP)]
        mx, sm, rs = (sb(n, [P, NP, H]) for n in ("mx", "sm", "rs"))
        pT = [sb(f"pT{t}", [P, H // 2, P]) for t in range(NP)]
        oT = sb("oT", [P, DC, T])
        y = sb("y", [P, NP, D])
        lnf = pr.ln_tiles(sb, "f")
        yn = sb("yn", [P, NP, D])
        outt = sb("outt", [P, NP, D])

        mlp_weights_in, weights_in, setup = (sem(n, 0) for n in (
            "mlp_weights_in", "weights_in", "setup"))
        x_loaded, res_loaded, ctx_loaded, mask_loaded = (
            sem("x_loaded", 16), sem("res_loaded", 16), sem("ctx_loaded", 64),
            sem("mask_loaded", 16))
        stored = sem("stored", 16)
        ln_s = pr.ln_sems(sem)
        xnT_ps, hT_ready = sem("xnT_ps", 1), sem("hT_ready", 2)
        fc_ps, act_ready, m_ps = sem("fc_ps", 4), sem("act_ready", MC), sem("m_ps", NP)
        xb_ready, x3_ready = sem("xb_ready", 1), sem("x3_ready", 1)
        x3T_ps, x3T_ready, x3b_ready = sem("x3T_ps", 1), sem("x3T_ready", 1), sem("x3b_ready", 1)
        q_ps, qT_ready = sem("q_ps", 1), sem("qT_ready", 2)
        k_ps, k_ready, v_ps, v_ready = (sem("k_ps", 1), sem("k_ready", 8), sem("v_ps", 1),
                                        sem("v_ready", 4))
        s_ps, s_masked, s_max, s_sub, s_exp, s_sum, s_rec, p_ready = (sem(n, NP) for n in (
            "s_ps", "s_masked", "s_max", "s_sub", "s_exp", "s_sum", "s_rec", "p_ready"))
        pT_ps, pT_ready = sem("pT_ps", NP), sem("pT_ready", NP)
        o_ps, oT_ready, y_ps, y_ready = (sem(n, 1) for n in ("o_ps", "oT_ready", "y_ps", "y_ready"))
        lnf_s = pr.ln_sems(sem, "f")
        gamma_done, out_ready = sem("gamma_done", 1), sem("out_ready", 1)
        start_counts(nc, sems)
        xv, ov = tokens(x_src), tokens(x_dst)
        cv = dram["ctxT"].rearrange("(c p) (g b s) -> g c p b s", p=P, b=NB, s=S)
        mv = dram["mask"].rearrange("(g t p) s -> g p t s", t=NP, p=P)

        block = ctx.enter_context(nc.Block())

        @block.sync
        def _(sp):
            def load_x(i):
                sp.wait_ge(ln_s.xn_ready, 2 * i)
                sp.dma_start(x_in[:], xv[i - 1]).then_inc(x_loaded, 16)

            def load_res(i):
                sp.wait_ge(xb_ready, i)
                sp.dma_start(x_res[:], xv[i - 1]).then_inc(res_loaded, 16)

            def load_ctx(i):
                sp.wait_ge(v_ps, i)
                for c in range(DC):
                    for u in range(2):
                        sp.dma_start(ctxT[:, c, :, u, :], cv[i - 1, c]).then_inc(ctx_loaded, 16)

            def load_mask(i):
                sp.wait_ge(s_masked, 2 * i)
                sp.dma_start(mask[:], mv[i - 1]).then_inc(mask_loaded, 16)

            def store(i):
                sp.wait_ge(out_ready, i + 1)
                sp.dma_start(ov[i - 1], outt[:]).then_inc(stored, 16)

            pr.staggered(sp, [(2, load_ctx), (4, load_x), (2, load_mask), (3, load_res),
                              (0, store)])
            sp.wait_ge(stored, 16 * TRIPS + 16)

        @block.gpsimd
        def _(pool):
            pool.wait_ge(pr.consts_in, 48)
            nc.gpsimd.memset(v_blk[:], 0.0).then_inc(setup, 1)

            def mlp_rstd(i):
                pr.ln_rstd(pool, ln, ln_s, i)

            def mlp_residual(i):
                pool.wait_ge(res_loaded, 16 * (i + 1))
                pool.wait_ge(x3_ready, i)
                nc.gpsimd.tensor_tensor(xb[:], x_res[:], pr.row(f"{M}b_fc2", NP), ALU.add
                                        ).then_inc(xb_ready, 1)

            def residual(i):
                pool.wait_ge(x3_ready, i + 1)
                pool.wait_ge(y_ready, i)
                nc.gpsimd.tensor_tensor(x3b[:], x3[:], pr.row(f"{L}bo", NP), ALU.add
                                        ).then_inc(x3b_ready, 1)

            def normalise(t):
                def step(i):
                    pool.wait_ge(s_rec, 2 * i + t + 1)
                    nc.gpsimd.tensor_tensor(sc[t][:], sc[t][:],
                                            rs[:, t, :].unsqueeze(2).to_broadcast([P, H, S]),
                                            ALU.mult).then_inc(p_ready, 1)
                return step

            def final(i):
                pr.ln_rstd(pool, lnf, lnf_s, i)
                pool.wait_ge(lnf_s.xn_ready, 2 * i + 2)
                nc.gpsimd.tensor_tensor(yn[:], yn[:], pr.row(f"{L}gamma", NP), ALU.mult
                                        ).then_inc(gamma_done, 1)
                pool.wait_ge(stored, 16 * i)
                pool.wait_ge(gamma_done, i + 1)
                nc.gpsimd.tensor_tensor(outt[:], yn[:], pr.row(f"{L}beta", NP), ALU.add
                                        ).then_inc(out_ready, 1)

            pr.staggered(pool, [(2, mlp_residual), (1, residual), (1, normalise(0)),
                                (1, normalise(1)), (0, final), (3, mlp_rstd)])

        @block.scalar
        def _(act_e):
            for dst, name in ((wfc, f"{M}w_fc1"), (wproj, f"{M}w_fc2")):
                act_e.dma_start(dst[:], weight(dram[name])).then_inc(mlp_weights_in, 16)
            for dst, name in ((wk, f"{L}Wk_rep"), (wq, f"{L}Wq"), (wv, f"{L}Wv"), (wo, f"{L}Wo")):
                act_e.dma_start(dst[:], weight(dram[name])).then_inc(weights_in, 16)
            act_e.wait_ge(pr.consts_in, 48)
            act_e.wait_ge(setup, 2)

            def x_transposed(i):
                act_e.wait_ge(x3T_ps, i + 1)
                nc.scalar.copy(x3T[:], bank(PS, 4, [DC, T])).then_inc(x3T_ready, 1)

            def queries(i):
                act_e.wait_ge(q_ps, i + 1)
                for c in range(DC):
                    nc.scalar.activation(qT[:, c, :], bank(PS, 4, [2, T])[:, c, :], ACT.Identity,
                                         bias=bq_scaled[:, c:c + 1], scale=SCALE
                                         ).then_inc(qT_ready, 1)

            def exps(t):
                def step(i):
                    act_e.wait_ge(s_sub, 2 * i + t + 1)
                    nc.scalar.activation(sc[t][:], sc[t][:], ACT.Exp).then_inc(s_exp, 1)
                return step

            def turned(t):
                def step(i):
                    act_e.wait_ge(pT_ps, 2 * i + t + 1)
                    nc.scalar.copy(pT[t][:].rearrange("p (a b) q -> p a (b q)", a=4),
                                   PS[:, 0:4, :]).then_inc(pT_ready, 1)
                return step

            def attended(i):
                act_e.wait_ge(o_ps, i + 1)
                nc.scalar.copy(oT[:], bank(PS, 4, [DC, T])).then_inc(oT_ready, 1)

            def gelu(u):
                def step(i):
                    act_e.wait_ge(fc_ps, 4 * i + u + 1)
                    for m in range(2 * u, 2 * u + 2):
                        nc.scalar.activation(act[:, m, :],
                                             bank(PS, 7 - u % 2, [2, T])[:, m % 2, :],
                                             ACT.Gelu, bias=pr.col(f"{M}b_fc1", m)
                                             ).then_inc(act_ready, 1)
                return step

            pr.staggered(act_e, [(2, gelu(0)), (1, exps(0)), (2, gelu(1)), (2, gelu(2)),
                                 (2, gelu(3)), (1, exps(1)), (1, turned(0)), (2, x_transposed),
                                 (1, turned(1)), (2, queries), (1, attended)])

        @block.vector
        def _(dve):
            dve.wait_ge(pr.consts_in, 48)
            nc.vector.tensor_scalar(bq_scaled[:], pr.cols_of(f"{L}bq"), SCALE, None, ALU.mult
                                    ).then_inc(setup, 1)
            dve.wait_ge(setup, 2)

            def mlp_norm(i):
                dve.wait_ge(x_loaded, 16 * (i + 1))
                dve.wait_ge(xnT_ps, i)
                pr.ln_normalise(dve, ln, ln_s, x_in, xn, i)

            def mlp_weighted(i):
                dve.wait_ge(xnT_ps, i + 1)
                dve.wait_ge(fc_ps, 4 * i)
                for c in range(DC):
                    nc.vector.tensor_scalar(hT[:, c, :], bank(PS, 6, [DC, T])[:, c, :],
                                            pr.col(f"{M}ln_mlp_scale", c),
                                            pr.col(f"{M}ln_mlp_offset", c),
                                            ALU.mult, ALU.add).then_inc(hT_ready, 1)

            def mlp_out(i):
                dve.wait_ge(m_ps, 2 * i + 2)
                dve.wait_ge(xb_ready, i + 1)
                dve.wait_ge(x3T_ps, i)
                dve.wait_ge(x3b_ready, i)
                nc.vector.tensor_tensor(x3[:], bank(PS, 7, [NP, D]), xb[:], ALU.add
                                        ).then_inc(x3_ready, 1)

            def keys(i):
                dve.wait_ge(k_ps, i + 1)
                for c in range(DC):
                    for g in range(G):
                        nc.vector.tensor_scalar(
                            k_blk[:, c, :, g, :], bank(PS, 5, [DC, NB, S])[:, c, :, :],
                            pr.col("L3_xattn_bk_rep", c), pr.head4[:, g:g + 1], ALU.add, ALU.mult
                        ).then_inc(k_ready, 1)

            def values(i):
                dve.wait_ge(v_ps, i + 1)
                for gp in range(2):
                    for hh in range(2):
                        half = slice(64 * hh, 64 * hh + 64)
                        bias = pr.rowv("L3_xattn_bv")[half, :].unsqueeze(1).to_broadcast(
                            [64, NB, KVH * HD]).rearrange("p b (h e) -> p b h e", e=HD)
                        nc.vector.tensor_tensor(
                            v_blk[half, :, :, gp, 2 * gp + hh, :],
                            bank(PS, 5, [8, KVH, HD])[half, 0:NB, :, :], bias, ALU.add
                        ).then_inc(v_ready, 1)

            def softmax_in(t):
                def step(i):
                    dve.wait_ge(mask_loaded, 16 * (i + 1))
                    dve.wait_ge(s_ps, 2 * i + t + 1)
                    nc.vector.tensor_tensor(
                        sc[t][:].rearrange("p (r h) k -> p r h k", r=RG),
                        PS[:, 0:RG, :].rearrange("p r (h k) -> p r h k", k=S),
                        mask[:, t, :].unsqueeze(1).unsqueeze(1).to_broadcast([P, RG, H // RG, S]),
                        ALU.add).then_inc(s_masked, 1)
                    dve.wait_ge(s_masked, 2 * i + t + 1)
                    nc.vector.tensor_reduce(mx[:, t, :], sc[t][:], AX.X, ALU.max
                                            ).then_inc(s_max, 1)
                    dve.wait_ge(s_max, 2 * i + t + 1)
                    nc.vector.tensor_tensor(sc[t][:], sc[t][:],
                                            mx[:, t, :].unsqueeze(2).to_broadcast([P, H, S]),
                                            ALU.subtract).then_inc(s_sub, 1)
                return step

            def softmax_sum(t):
                def step(i):
                    dve.wait_ge(s_exp, 2 * i + t + 1)
                    nc.vector.tensor_reduce(sm[:, t, :], sc[t][:], AX.X, ALU.add
                                            ).then_inc(s_sum, 1)
                    dve.wait_ge(s_sum, 2 * i + t + 1)
                    nc.vector.reciprocal(rs[:, t, :], sm[:, t, :]).then_inc(s_rec, 1)
                return step

            def final(i):
                dve.wait_ge(y_ps, i + 1)
                dve.wait_ge(x3b_ready, i + 1)
                dve.wait_ge(lnf_s.xn_ready, 2 * i)
                nc.vector.tensor_tensor(y[:], bank(PS, 5, [NP, D]), x3b[:], ALU.add
                                        ).then_inc(y_ready, 1)

            def final_norm(i):
                dve.wait_ge(y_ready, i + 1)
                dve.wait_ge(out_ready, i)
                pr.ln_normalise(dve, lnf, lnf_s, y, yn, i, eps=1e-6)

            pr.staggered(dve, [(1, softmax_in(0)), (1, softmax_in(1)), (1, softmax_sum(0)),
                               (1, values), (1, softmax_sum(1)), (2, mlp_out), (2, keys),
                               (0, final_norm), (3, mlp_norm), (3, mlp_weighted), (1, final)])

        @block.tensor
        def _(pe):
            pe.wait_ge(pr.consts_in, 48)
            pe.wait_ge(setup, 2)

            def mlp_turn(i):
                pe.wait_ge(act_ready, 8 * i)
                pe.wait_ge(ln_s.xn_ready, 2 * i + 2)
                pr.transpose_tiles(xn, 6).then_inc(xnT_ps, 1)

            def mlp_up(u):
                def step(i):
                    if u == 0:
                        pe.wait_ge(mlp_weights_in, 32)
                        pe.wait_ge(x3_ready, i)
                        pe.wait_ge(hT_ready, 2 * i + 2)
                    if u >= 2:
                        pe.wait_ge(act_ready, 8 * i + 2 * (u - 1))
                    for m in range(2 * u, 2 * u + 2):
                        for c in range(DC):
                            mm = nc.tensor.matmul(bank(PS, 7 - u % 2, [2, T])[:, m % 2, :],
                                                  wfc[:, c, m * P:(m + 1) * P], hT[:, c, :],
                                                  start=(c == 0), stop=(c == 1))
                    mm.then_inc(fc_ps, 1)
                return step

            def mlp_down(t):
                def step(i):
                    pe.wait_ge(act_ready, 8 * i + 8)
                    pr.project_rows(act, wproj, 7, MC, [t]).then_inc(m_ps, 1)
                return step

            def keys(i):
                pe.wait_ge(weights_in, 64)
                pe.wait_ge(v_ready, 4 * i)
                if not first_trip(i):
                    pe.wait_ge(y_ready, i - 1)
                pe.wait_ge(ctx_loaded, 64 * (i + 1))
                pr.project_T(wk, ctxT[:, :, :, 0, :], 5, DC).then_inc(k_ps, 1)

            def turn_x3(i):
                if not first_trip(i):
                    pe.wait_ge(oT_ready, i - 1)
                pe.wait_ge(x3_ready, i + 1)
                pr.transpose_tiles(x3, 4).then_inc(x3T_ps, 1)

            def queries(i):
                pe.wait_ge(x3T_ready, i + 1)
                pr.project_T(wq, x3T, 4, DC).then_inc(q_ps, 1)

            def values(i):
                pe.wait_ge(k_ready, 8 * i + 8)
                pe.wait_ge(y_ready, i)
                for b in range(NB):
                    for c in range(DC):
                        mm = nc.tensor.matmul(bank(PS, 5, [8, S])[:, b, :],
                                              ctxT[:, c, b, :, :].rearrange("p u s -> p (u s)"),
                                              wv[:, c, :], start=(c == 0), stop=(c == 1))
                mm.then_inc(v_ps, 1)

            def scores(t):
                def step(i):
                    if t == 0:
                        pe.wait_ge(k_ready, 8 * i + 8)
                        pe.wait_ge(qT_ready, 2 * i + 2)
                        pe.wait_ge(pT_ready, 2 * i)
                    else:
                        pe.wait_ge(s_masked, 2 * i + 1)
                    for r in range(RG):
                        rows = slice(32 * r, 32 * r + 32)
                        for c in range(DC):
                            for b2 in range(2):
                                b = 2 * t + b2
                                mm = nc.tensor.matmul(
                                    bank(PS, r, [2, T])[64 * b2:64 * b2 + 64, c, :],
                                    qT[rows, c, b * S:(b + 1) * S],
                                    k_blk[rows, c, b, :, :], start=True, stop=True)
                    mm.then_inc(s_ps, 1)
                return step

            def turn(t):
                def step(i):
                    if t == 0:
                        pe.wait_ge(s_masked, 2 * i + 2)
                    else:
                        pe.wait_ge(pT_ready, 2 * i + 1)
                    pe.wait_ge(p_ready, 2 * i + t + 1)
                    for n in range(H // 2):
                        mm = nc.tensor.transpose(
                            bank(PS, n // 4, [4, P])[:, n % 4, :],
                            sc[t][:, 2 * n:2 * n + 2, :].rearrange("p h k -> p (h k)"), pr.ident)
                    mm.then_inc(pT_ps, 1)
                return step

            def attend(i):
                pe.wait_ge(v_ready, 4 * i + 4)
                if not last_trip(i):
                    pe.wait_ge(qT_ready, 2 * i + 4)
                for t in range(NP):
                    pe.wait_ge(pT_ready, 2 * i + t + 1)
                    for c in range(DC):
                        for r in range(RG):
                            for b2 in range(2):
                                b = 2 * t + b2
                                for gp in range(2):
                                    mm = nc.tensor.matmul(
                                        bank(PS, 4, [DC, T])[32 * r:32 * r + 32, c,
                                                             b * S:(b + 1) * S],
                                        v_blk[:, b, c * RG + r, gp, :, :].rearrange(
                                            "p g e -> p (g e)"),
                                        pT[t][:, 4 * r + 2 * c + gp, b2 * S:(b2 + 1) * S],
                                        start=(gp == 0), stop=(gp == 1))
                mm.then_inc(o_ps, 1)

            def output(i):
                pe.wait_ge(oT_ready, i + 1)
                if not last_trip(i):
                    pe.wait_ge(k_ready, 8 * i + 16)
                pr.project_rows(oT, wo, 5, DC).then_inc(y_ps, 1)

            pr.staggered(pe, [(1, scores(0)), (1, values), (2, mlp_up(0)), (1, scores(1)),
                              (2, mlp_up(1)), (2, mlp_up(2)), (2, mlp_up(3)), (2, mlp_down(0)),
                              (2, mlp_down(1)), (2, keys), (1, turn(0)), (2, turn_x3), (1, turn(1)),
                              (2, queries), (1, attend), (3, mlp_turn), (1, output)])


STAGES = [stage_l0, stage_l1, stage_cross1, stage_cross2, stage_l3]


def build(nc, dram, stages=STAGES):
    pr = Program(nc, dram)
    with ExitStack() as ctx:
        pr.psum = ctx.enter_context(nc.psum_tensor("psum", [P, 8, 512], F32))
        consts = ctx.enter_context(nc.sbuf_tensor("consts", [P, 2310], F32))
        pr.cols = ctx.enter_context(nc.sbuf_tensor("cols", [P, pr.ncols], F32))
        pr.rows = ctx.enter_context(nc.sbuf_tensor("rows", [P, D * (len(ROWS) - 1) + S], F32))
        pr.neg_half = ctx.enter_context(nc.sbuf_tensor("neg_half", [P, NP], F32))
        pr.consts_in = ctx.enter_context(nc.semaphore("consts_in"))
        pr.ident = consts[:, 0:P]
        pr.same_head = consts[:, P:2 * P]
        pr.spread = consts[:, 2 * P:10 * P].rearrange("p (j m) -> p j m", j=8)
        pr.gather = consts[:, 10 * P:18 * P].rearrange("p (j m) -> p j m", j=8)
        pr.head2 = consts[:, 18 * P:18 * P + 2]
        pr.head4 = consts[:, 18 * P + 2:18 * P + 6]
        with nc.Block() as block:
            @block.sync
            def _(sp):
                sp.dma_start(consts[:], dram["consts"]).then_inc(pr.consts_in, 16)
                sp.dma_start(pr.cols[:], dram["cols"]).then_inc(pr.consts_in, 16)
                sp.dma_start(pr.rows[:], dram["rows"][0, :].partition_broadcast(P)
                             ).then_inc(pr.consts_in, 16)

            @block.vector
            def _(dve):
                nc.vector.memset(pr.neg_half[:], -0.5)

        scratch = [nc.dram_tensor(f"scratch{n}", (B * S, D), F32, kind="Internal").ap()
                   for n in range(2)]
        pr.half_done = nc.dram_tensor("half_done", (B * S, D), F32, kind="Internal").ap()
        src = dram["x"]
        for n, stage in enumerate(stages):
            dst = dram["out"] if n == len(stages) - 1 else scratch[n % 2]
            stage(pr, src, dst)
            src = dst


_MATRICES = ["L0_xattn_q_w", "L0_xattn_k_w", "L0_xattn_v_w", "L0_xattn_cproj_w", "L0_xattn_fc_w",
             "L0_xattn_proj_w", "L1_xattn_maa_w1", "L1_xattn_td_w1", "L1_xattn_td_w2",
             "L2_xattn_wq1", "L2_xattn_wk1", "L2_xattn_wv1", "L2_xattn_wo1",
             "L2_xattn_wq2", "L2_xattn_wk2", "L2_xattn_wv2", "L2_xattn_wo2",
             "L2_xattn_w_fc1", "L2_xattn_w_fc2", "L2_xattn_bv1", "L2_xattn_bv2",
             "L3_xattn_Wq", "L3_xattn_Wv", "L3_xattn_Wo"]
_TRANSPOSED = ["L1_xattn_Wr", "L1_xattn_Wk", "L1_xattn_Wv", "L1_xattn_Wg", "L1_xattn_Wo",
               "L1_xattn_Wfk", "L1_xattn_Wfr", "L1_xattn_Wfv"]


def kernel(**inputs):
    import numpy as np
    import concourse.bacc as bacc
    from concourse.bass_utils import run_bass_kernel_spmd

    a = {k: np.asarray(v) for k, v in inputs.items()}
    ctx = a["ctx_2048"]
    heads = {"L3_xattn_Wk_rep": np.repeat(a["L3_xattn_Wk"].reshape(D, 8, 1, 8), 4, 2).reshape(D, D)}
    a["L3_xattn_bk_rep"] = np.repeat(a["L3_xattn_bk"].reshape(8, 1, 8), 4, 1).reshape(D)
    arrays = {
        "x": a["x"].reshape(B * S, D),
        "ctxT": ctx.reshape(B * S, D).T,
        "edgeT": ctx[:, 0:2].transpose(2, 1, 0).reshape(DC, P, 2 * B),
        "state0": ctx[:, 2:10].reshape(B, DC, P, 8).transpose(2, 1, 3, 0).reshape(P, DC * 8 * B),
        "key_mask": a["mask_BxS2_bf1"].view(np.uint8),
        "mask": a["mask_Bx1xSxS2_ff0"].reshape(B * S, S),
        "cols": np.concatenate([a[n].reshape(-1, P) for n in COLS], 0).T,
        "rows": np.concatenate([a[n].reshape(-1) for n in ROWS], 0).reshape(1, -1),
        "maa_w2": a["L1_xattn_maa_w2"].reshape(160, D),
        "L3_xattn_Wk_rep": heads["L3_xattn_Wk_rep"],
    }
    for n in _MATRICES:
        arrays[n] = a[n].reshape(1, -1) if a[n].ndim == 1 else a[n]
    for n in _TRANSPOSED:
        arrays[n] = a[n].T
    p = np.arange(P)
    same = (p[:, None] // 8 == p[None, :] // 8).astype(np.float32)
    spread = np.stack([same * (p[:, None] % 8 == j) for j in range(8)], 1).reshape(P, 8 * P)
    gather = np.stack([same * (p[None, :] % 8 == j) for j in range(8)], 1).reshape(P, 8 * P)
    arrays["consts"] = np.concatenate(
        [np.eye(P, dtype=np.float32), same, spread, gather,
         (p[:, None] // 16 % 2 == np.arange(2)[None, :]).astype(np.float32),
         (p[:, None] // 8 % 4 == np.arange(4)[None, :]).astype(np.float32)], 1).astype(np.float32)
    arrays = {f"in_{k}": np.ascontiguousarray(v) for k, v in arrays.items()}

    nc = bacc.Bacc("TRN2", target_bir_lowering=False, num_devices=1)
    dram = {k[3:]: nc.dram_tensor(k, v.shape, mybir.dt.from_np(v.dtype), kind="ExternalInput").ap()
            for k, v in arrays.items()}
    dram["out"] = nc.dram_tensor("out_0", (B * S, D), F32, kind="ExternalOutput").ap()
    build(nc, dram)
    r = run_bass_kernel_spmd(nc, [arrays], core_ids=[0])
    return np.asarray(r.results[0]["out_0"]).reshape(B, S, D)
```
